# Optimizing a Trainium2 kernel written in Bass

```python
import numpy as np
import jax
import jax.numpy as jnp

def _softmax(x, axis=-1):
    return jax.nn.softmax(x, axis=axis)

def _gelu(x):
    return jax.nn.gelu(x, approximate=True)

def _silu(x):
    return jax.nn.silu(x)

def _sigmoid(x):
    return jax.nn.sigmoid(x)

def _layernorm(x, axis=-1, eps=1e-05):
    m = jnp.mean(x, axis=axis, keepdims=True)
    v = jnp.var(x, axis=axis, keepdims=True)
    return (x - m) / jnp.sqrt(v + eps)

def _scatter_add(tgt, idx, src, axis=0):
    return tgt.at[idx].add(src)

def _segment_sum(src, seg, n):
    return jax.ops.segment_sum(src, seg, n)
kernel_name = 'mk_seq_postln_d4_jaxref_r8_67329d'

def setup_inputs(seed: int=0):
    np.random.seed(seed)
    _w = jnp.asarray

    def _L0_attn_setup():
        import jax, jax.numpy as jnp
        import numpy as np
        N_EMBD = 128
        N_HEAD = 16
        HEAD_DIM = N_EMBD // N_HEAD
        KV_RANK = 32
        Q_RANK = 64
        ROPE_DIM = 32
        B, T = (2, 256)
        EPS = 1e-06

        def _rope_tables(T, dim):
            inv_freq = 1.0 / 10000.0 ** (np.arange(0, dim, 2, dtype=np.float32) / dim)
            t = np.arange(T, dtype=np.float32)
            freqs = np.outer(t, inv_freq)
            emb = np.concatenate([freqs, freqs], -1)
            return (jnp.asarray(np.cos(emb)), jnp.asarray(np.sin(emb)))

        def _apply_rope(x, cos, sin):
            d2 = x.shape[-1] // 2
            x1, x2 = (x[..., :d2], x[..., d2:])
            rot = jnp.concatenate([-x2, x1], axis=-1)
            return x * cos[None, None, :, :] + rot * sin[None, None, :, :]
        key = jax.random.key(seed)
        ks = jax.random.split(key, 10)

        def w(k, fan_in, fan_out):
            return jax.random.normal(k, (fan_in, fan_out), dtype=jnp.float32) * fan_in ** (-0.5)
        return {'x': jax.random.normal(ks[0], (B, T, N_EMBD), dtype=jnp.float32), 'W_kv': w(ks[1], N_EMBD, KV_RANK), 'g_kv': jnp.ones((KV_RANK,), dtype=jnp.float32), 'W_kdec': w(ks[2], KV_RANK, N_HEAD * HEAD_DIM), 'W_vdec': w(ks[3], KV_RANK, N_HEAD * HEAD_DIM), 'W_q': w(ks[4], N_EMBD, Q_RANK), 'W_qdec': w(ks[5], Q_RANK, N_HEAD * HEAD_DIM), 'W_krope': w(ks[6], N_EMBD, N_HEAD * ROPE_DIM), 'W_qrope': w(ks[7], Q_RANK, N_HEAD * ROPE_DIM), 'W_o': w(ks[8], N_HEAD * HEAD_DIM, N_EMBD)}
    _L0_attn_in = _L0_attn_setup()

    def _L0_ffn_setup():
        import jax, jax.numpy as jnp
        import numpy as np
        BEST_K = 2

        def _expert(xf, w1, w3, w2):
            return jax.nn.silu(xf @ w1) * (xf @ w3) @ w2
        key = jax.random.key(seed)
        ks = jax.random.split(key, 9)
        E, S_sh, D, H = (8, 2, 128, 64)
        B, S = (2, 256)
        w = lambda k, shape: jax.random.normal(k, shape, dtype=jnp.float32) * 0.02
        return {'x': jax.random.normal(ks[0], (B, S, D), dtype=jnp.float32), 'router_w': w(ks[1], (D, E)), 'router_b': jnp.zeros((E,), dtype=jnp.float32), 'routed_w1': w(ks[2], (E, D, H)), 'routed_w3': w(ks[3], (E, D, H)), 'routed_w2': w(ks[4], (E, H, D)), 'shared_w1': w(ks[5], (S_sh, D, H)), 'shared_w3': w(ks[6], (S_sh, D, H)), 'shared_w2': w(ks[7], (S_sh, H, D))}
    _L0_ffn_in = _L0_ffn_setup()

    def _L1_attn_setup():
        import jax, jax.numpy as jnp
        import numpy as np
        from math import log, sqrt
        B, S, D, H = (2, 256, 128, 16)
        HD = D // H
        NUM_BUCKETS = 32
        MAX_DISTANCE = 128
        ROPE_BASE = 10000.0

        def _rope_cos_sin(seq_len, dim, base):
            inv_freq = 1.0 / base ** (jnp.arange(0, dim, 2, dtype=jnp.float32) / dim)
            t = jnp.arange(seq_len, dtype=jnp.float32)
            freqs = jnp.outer(t, inv_freq)
            emb = jnp.concatenate([freqs, freqs], axis=-1)
            return (jnp.cos(emb), jnp.sin(emb))

        def _rotate_half(t):
            d = t.shape[-1] // 2
            return jnp.concatenate([-t[..., d:], t[..., :d]], axis=-1)

        def _rel_pos_bucket(relative_position, num_buckets, max_distance):
            rp = -jnp.minimum(relative_position, 0)
            max_exact = num_buckets // 2
            is_small = rp < max_exact
            rp_f = jnp.maximum(rp.astype(jnp.float32), 1.0)
            large = max_exact + (jnp.log(rp_f / max_exact) / log(max_distance / max_exact) * (num_buckets - max_exact)).astype(jnp.int32)
            large = jnp.minimum(large, num_buckets - 1)
            return jnp.where(is_small, rp, large)
        key = jax.random.key(seed)
        kx, kq, kk, kv, ko, kr = jax.random.split(key, 6)
        scale = 0.02
        return {'x': jax.random.normal(kx, (B, S, D), dtype=jnp.float32), 'Wq': jax.random.normal(kq, (D, D), dtype=jnp.float32) * scale, 'Wk': jax.random.normal(kk, (D, D), dtype=jnp.float32) * scale, 'Wv': jax.random.normal(kv, (D, D), dtype=jnp.float32) * scale, 'Wo': jax.random.normal(ko, (D, D), dtype=jnp.float32) * scale, 'rel_emb': jax.random.normal(kr, (NUM_BUCKETS, H), dtype=jnp.float32) * scale}
    _L1_attn_in = _L1_attn_setup()

    def _L1_ffn_setup():
        import jax, jax.numpy as jnp
        import numpy as np
        TOP_K = 2
        key = jax.random.key(seed)
        ks = jax.random.split(key, 5)
        B, S, D, E = (4, 256, 128, 8)
        H = 4 * D
        scale = 0.02
        return {'x': jax.random.normal(ks[0], (B, S, D), dtype=jnp.float32), 'gate_w': jax.random.normal(ks[1], (E, D), dtype=jnp.float32) * scale, 'gate_b': jnp.zeros((E,), dtype=jnp.float32), 'w1': jax.random.normal(ks[2], (E, H, D), dtype=jnp.float32) * scale, 'b1': jnp.zeros((E, H), dtype=jnp.float32), 'w2': jax.random.normal(ks[3], (E, D, H), dtype=jnp.float32) * scale, 'b2': jnp.zeros((E, D), dtype=jnp.float32)}
    _L1_ffn_in = _L1_ffn_setup()

    def _L2_attn_setup():
        import jax, jax.numpy as jnp
        import numpy as np
        NUM_HEADS = 16
        key = jax.random.key(seed)
        ks = jax.random.split(key, 5)
        B, N, C = (2, 256, 128)
        x = jax.random.normal(ks[0], (B, N, C), dtype=jnp.float32)
        s_in = 1.0 / np.sqrt(C)
        Wq = jax.random.normal(ks[1], (C, 2 * C), dtype=jnp.float32) * s_in
        Wk = jax.random.normal(ks[2], (C, 2 * C), dtype=jnp.float32) * s_in
        Wv = jax.random.normal(ks[3], (C, 2 * C), dtype=jnp.float32) * s_in
        Wo = jax.random.normal(ks[4], (2 * C, C), dtype=jnp.float32) * (1.0 / np.sqrt(2 * C))
        return {'x': x, 'Wq': Wq, 'Wk': Wk, 'Wv': Wv, 'Wo': Wo}
    _L2_attn_in = _L2_attn_setup()

    def _L2_ffn_setup():
        import jax, jax.numpy as jnp
        import numpy as np
        B, N, D = (4, 1024, 128)
        HEADS, DH = (8, 64)
        HID = HEADS * DH
        WIN = 128
        NQ, NKV = (128, 256)
        EPS, N_ITERS, FETCH_K = (1.0, 50, 9.0 / 8.0)
        SCALE = DH ** (-0.5)

        def rmsnorm(x, gamma):
            norm = jnp.maximum(jnp.linalg.norm(x, axis=-1, keepdims=True), 1e-12)
            return x / norm * x.shape[-1] ** 0.5 * gamma

        def coor_descent(s, k):
            logk = jnp.log(jnp.asarray(k, s.dtype))

            def body(_, ab):
                a, b = ab
                a = EPS * (logk - jax.nn.logsumexp((s + b) / EPS, axis=-1, keepdims=True))
                b = -jax.nn.relu(s + a)
                return (a, b)
            a, b = jax.lax.fori_loop(0, N_ITERS, body, (jnp.zeros_like(s[..., :1]), -s))
            return jnp.exp((s + a + b) / EPS)

        def route(x, routing_token, num_tokens):
            s = jnp.einsum('bnd,d->bn', x, routing_token)
            k = min(num_tokens * FETCH_K, x.shape[1])
            scores = coor_descent(s, k)
            sel_scores, sel_idx = jax.lax.top_k(scores, num_tokens)
            sel_scores = sel_scores + jax.lax.stop_gradient(1.0 - sel_scores)
            return (sel_scores, sel_idx)

        def light_local_attn(x, gamma, wq, wkv, wo):
            b, n, d = x.shape
            xn = rmsnorm(x, gamma)
            q = xn @ wq
            k, v = jnp.split(xn @ wkv, 2, axis=-1)

            def win(t):
                return t.reshape(b, n // WIN, WIN, HEADS, DH).transpose(0, 1, 3, 2, 4)
            q, k, v = (win(q) * SCALE, win(k), win(v))
            attn = jax.nn.softmax(jnp.einsum('bwhid,bwhjd->bwhij', q, k), axis=-1)
            out = jnp.einsum('bwhij,bwhjd->bwhid', attn, v)
            out = out.transpose(0, 1, 3, 2, 4).reshape(b, n, HID)
            return out @ wo

        def heavy_attn(xq, context, scores_kv, gamma, wq, wkv_t, wo):
            b, nq, d = xq.shape
            nkv = context.shape[1]
            xqn = rmsnorm(xq, gamma)
            ctx = rmsnorm(context, gamma)[:, None]
            q = (xqn @ wq).reshape(b, nq, HEADS, DH).transpose(0, 2, 1, 3) * SCALE
            kvw = wkv_t.reshape(1, HEADS, 2 * DH, d)
            kv = jnp.einsum('rhdi,brni->brhnd', kvw, ctx)
            k, v = jnp.split(kv, 2, axis=-1)
            v = v * scores_kv[:, None, None, :, None]
            k = k.reshape(b, HEADS, nkv, DH)
            v = v.reshape(b, HEADS, nkv, DH)
            attn = jax.nn.softmax(jnp.einsum('bhid,bhjd->bhij', q, k), axis=-1)
            out = jnp.einsum('bhij,bhjd->bhid', attn, v)
            out = out.transpose(0, 2, 1, 3).reshape(b, nq, HID)
            return out @ wo
        key = jax.random.key(seed)
        ks = jax.random.split(key, 10)
        lin = lambda k, shape, fan: jax.random.normal(k, shape, jnp.float32) * fan ** (-0.5)
        return dict(x=jax.random.normal(ks[0], (B, N, D), jnp.float32), gamma_light=jnp.ones((D,), jnp.float32), wq_light=lin(ks[1], (D, HID), D), wkv_light=lin(ks[2], (D, 2 * HID), D), wo_light=lin(ks[3], (HID, D), HID), q_routing_token=jax.random.normal(ks[4], (D,), jnp.float32), kv_routing_token=jax.random.normal(ks[5], (D,), jnp.float32), gamma_heavy=jnp.ones((D,), jnp.float32), wq_heavy=lin(ks[6], (D, HID), D), wkv_heavy=lin(ks[7], (2 * HID, D), D), wo_heavy=lin(ks[8], (HID, D), HID))
    _L2_ffn_in = _L2_ffn_setup()

    def _L3_attn_setup():
        import jax, jax.numpy as jnp
        import numpy as np
        import math
        EMBED_DIM = 128
        NHEAD = 16
        HEAD_DIM = 64
        BATCH = 2
        SEQ = 256
        key = jax.random.key(seed)
        k_in, k_wqkv, k_wo, k_g = jax.random.split(key, 4)
        std = math.sqrt(2.0 / EMBED_DIM)
        inputs = jax.random.normal(k_in, (BATCH, SEQ, EMBED_DIM), dtype=jnp.float32)
        Wqkv_w = jax.random.normal(k_wqkv, (3 * NHEAD * HEAD_DIM, EMBED_DIM), dtype=jnp.float32) * std
        Wqkv_b = jnp.zeros((3 * NHEAD * HEAD_DIM,), dtype=jnp.float32)
        Wo_w = jax.random.normal(k_wo, (EMBED_DIM, NHEAD * HEAD_DIM), dtype=jnp.float32) * std
        Wo_b = jnp.zeros((EMBED_DIM,), dtype=jnp.float32)
        ghost = jax.random.uniform(k_g, (NHEAD,), dtype=jnp.float32) * 0.1
        return {'inputs': inputs, 'Wqkv_w': Wqkv_w, 'Wqkv_b': Wqkv_b, 'Wo_w': Wo_w, 'Wo_b': Wo_b, 'ghost': ghost}
    _L3_attn_in = _L3_attn_setup()

    def _L3_ffn_setup():
        import jax, jax.numpy as jnp
        import numpy as np
        EPS = 1e-05

        def _ln(x, g, b):
            mu = jnp.mean(x, axis=-1, keepdims=True)
            var = jnp.mean(jnp.square(x - mu), axis=-1, keepdims=True)
            return (x - mu) * jax.lax.rsqrt(var + EPS) * g + b

        def _forward(x, index_b, index_t, sw1, sb1, sw2, sb2, sw3, sb3, s_ln_g, s_ln_b, sg_w, sg_b, eg_w, eg_b, exp_bias, ew1, eb1, ew2, eb2, ew3, eb3, sel_ln_g, sel_ln_b):
            x1 = jnp.einsum('btd,hd->bth', x, sw1) + sb1
            x2 = jnp.einsum('btd,hd->bth', x, sw2) + sb2
            sh = _ln(jax.nn.silu(x1) * x2, s_ln_g, s_ln_b)
            shared_out = jnp.einsum('bth,dh->btd', sh, sw3) + sb3
            x_moe = x[index_b, index_t]
            shared_scores = jax.nn.sigmoid(x_moe @ sg_w.T + sg_b)
            expert_scores = jax.nn.sigmoid(x_moe @ eg_w.T + eg_b)
            top1_idx = jnp.argmax(expert_scores + exp_bias, axis=-1)
            top1_score = jnp.take_along_axis(expert_scores, top1_idx[:, None], axis=-1)
            weights = jax.nn.softmax(jnp.concatenate([shared_scores, top1_score], axis=-1), axis=-1)
            shared_w, expert_w = (weights[:, 0], weights[:, 1])
            shared_moe_out = shared_out[index_b, index_t] * shared_w[:, None]
            h1 = jnp.einsum('md,ehd->meh', x_moe, ew1) + eb1
            h2 = jnp.einsum('md,ehd->meh', x_moe, ew2) + eb2
            z = _ln(jax.nn.silu(h1) * h2, sel_ln_g, sel_ln_b)
            out_all = jnp.einsum('meh,edh->med', z, ew3) + eb3
            expert_out = jnp.take_along_axis(out_all, top1_idx[:, None, None], axis=1)[:, 0]
            expert_moe_out = expert_out * expert_w[:, None]
            final_out = shared_out.at[index_b, index_t].set(shared_moe_out + expert_moe_out)
            return final_out
        B, T, D, E, H, M = (2, 256, 128, 8, 64, 256)
        key = jax.random.key(seed)
        ks = jax.random.split(key, 24)
        s = 0.02
        inp = {}
        inp['x'] = jax.random.normal(ks[0], (B, T, D), jnp.float32)
        flat = jnp.arange(M, dtype=jnp.int32) * 2
        inp['index_b'] = flat // T
        inp['index_t'] = flat % T
        inp['sw1'] = jax.random.normal(ks[1], (H, D), jnp.float32) * s
        inp['sb1'] = jnp.zeros((H,), jnp.float32)
        inp['sw2'] = jax.random.normal(ks[2], (H, D), jnp.float32) * s
        inp['sb2'] = jnp.zeros((H,), jnp.float32)
        inp['sw3'] = jax.random.normal(ks[3], (D, H), jnp.float32) * s
        inp['sb3'] = jnp.zeros((D,), jnp.float32)
        inp['s_ln_g'] = jnp.ones((H,), jnp.float32)
        inp['s_ln_b'] = jnp.zeros((H,), jnp.float32)
        inp['sg_w'] = jax.random.normal(ks[4], (1, D), jnp.float32) * s
        inp['sg_b'] = jnp.zeros((1,), jnp.float32)
        inp['eg_w'] = jax.random.normal(ks[5], (E, D), jnp.float32) * s
        inp['eg_b'] = jnp.zeros((E,), jnp.float32)
        inp['exp_bias'] = jnp.zeros((E,), jnp.float32)
        inp['ew1'] = jax.random.normal(ks[6], (E, H, D), jnp.float32) * s
        inp['eb1'] = jnp.zeros((E, H), jnp.float32)
        inp['ew2'] = jax.random.normal(ks[7], (E, H, D), jnp.float32) * s
        inp['eb2'] = jnp.zeros((E, H), jnp.float32)
        inp['ew3'] = jax.random.normal(ks[8], (E, D, H), jnp.float32) * s
        inp['eb3'] = jnp.zeros((E, D), jnp.float32)
        inp['sel_ln_g'] = jnp.ones((H,), jnp.float32)
        inp['sel_ln_b'] = jnp.zeros((H,), jnp.float32)
        return inp
    _L3_ffn_in = _L3_ffn_setup()
    _d = {'L0_attn_x': _L0_attn_in['x'], 'L0_attn_W_kv': _L0_attn_in['W_kv'], 'L0_attn_g_kv': _L0_attn_in['g_kv'], 'L0_attn_W_kdec': _L0_attn_in['W_kdec'], 'L0_attn_W_vdec': _L0_attn_in['W_vdec'], 'L0_attn_W_q': _L0_attn_in['W_q'], 'L0_attn_W_qdec': _L0_attn_in['W_qdec'], 'L0_attn_W_krope': _L0_attn_in['W_krope'], 'L0_attn_W_qrope': _L0_attn_in['W_qrope'], 'L0_attn_W_o': _L0_attn_in['W_o'], 'L0_ffn_router_w': _L0_ffn_in['router_w'], 'L0_ffn_router_b': _L0_ffn_in['router_b'], 'L0_ffn_routed_w1': _L0_ffn_in['routed_w1'], 'L0_ffn_routed_w3': _L0_ffn_in['routed_w3'], 'L0_ffn_routed_w2': _L0_ffn_in['routed_w2'], 'L0_ffn_shared_w1': _L0_ffn_in['shared_w1'], 'L0_ffn_shared_w3': _L0_ffn_in['shared_w3'], 'L0_ffn_shared_w2': _L0_ffn_in['shared_w2'], 'L1_attn_Wq': _L1_attn_in['Wq'], 'L1_attn_Wk': _L1_attn_in['Wk'], 'L1_attn_Wv': _L1_attn_in['Wv'], 'L1_attn_Wo': _L1_attn_in['Wo'], 'L1_attn_rel_emb': _L1_attn_in['rel_emb'], 'L1_ffn_gate_w': _L1_ffn_in['gate_w'], 'L1_ffn_gate_b': _L1_ffn_in['gate_b'], 'L1_ffn_w1': _L1_ffn_in['w1'], 'L1_ffn_b1': _L1_ffn_in['b1'], 'L1_ffn_w2': _L1_ffn_in['w2'], 'L1_ffn_b2': _L1_ffn_in['b2'], 'L2_attn_Wq': _L2_attn_in['Wq'], 'L2_attn_Wk': _L2_attn_in['Wk'], 'L2_attn_Wv': _L2_attn_in['Wv'], 'L2_attn_Wo': _L2_attn_in['Wo'], 'L2_ffn_gamma_light': _L2_ffn_in['gamma_light'], 'L2_ffn_wq_light': _L2_ffn_in['wq_light'], 'L2_ffn_wkv_light': _L2_ffn_in['wkv_light'], 'L2_ffn_wo_light': _L2_ffn_in['wo_light'], 'L2_ffn_q_routing_token': _L2_ffn_in['q_routing_token'], 'L2_ffn_kv_routing_token': _L2_ffn_in['kv_routing_token'], 'L2_ffn_gamma_heavy': _L2_ffn_in['gamma_heavy'], 'L2_ffn_wq_heavy': _L2_ffn_in['wq_heavy'], 'L2_ffn_wkv_heavy': _L2_ffn_in['wkv_heavy'], 'L2_ffn_wo_heavy': _L2_ffn_in['wo_heavy'], 'L3_attn_Wqkv_w': _L3_attn_in['Wqkv_w'], 'L3_attn_Wqkv_b': _L3_attn_in['Wqkv_b'], 'L3_attn_Wo_w': _L3_attn_in['Wo_w'], 'L3_attn_Wo_b': _L3_attn_in['Wo_b'], 'L3_attn_ghost': _L3_attn_in['ghost'], 'L3_ffn_index_b': _L3_ffn_in['index_b'], 'L3_ffn_index_t': _L3_ffn_in['index_t'], 'L3_ffn_sw1': _L3_ffn_in['sw1'], 'L3_ffn_sb1': _L3_ffn_in['sb1'], 'L3_ffn_sw2': _L3_ffn_in['sw2'], 'L3_ffn_sb2': _L3_ffn_in['sb2'], 'L3_ffn_sw3': _L3_ffn_in['sw3'], 'L3_ffn_sb3': _L3_ffn_in['sb3'], 'L3_ffn_s_ln_g': _L3_ffn_in['s_ln_g'], 'L3_ffn_s_ln_b': _L3_ffn_in['s_ln_b'], 'L3_ffn_sg_w': _L3_ffn_in['sg_w'], 'L3_ffn_sg_b': _L3_ffn_in['sg_b'], 'L3_ffn_eg_w': _L3_ffn_in['eg_w'], 'L3_ffn_eg_b': _L3_ffn_in['eg_b'], 'L3_ffn_exp_bias': _L3_ffn_in['exp_bias'], 'L3_ffn_ew1': _L3_ffn_in['ew1'], 'L3_ffn_eb1': _L3_ffn_in['eb1'], 'L3_ffn_ew2': _L3_ffn_in['ew2'], 'L3_ffn_eb2': _L3_ffn_in['eb2'], 'L3_ffn_ew3': _L3_ffn_in['ew3'], 'L3_ffn_eb3': _L3_ffn_in['eb3'], 'L3_ffn_sel_ln_g': _L3_ffn_in['sel_ln_g'], 'L3_ffn_sel_ln_b': _L3_ffn_in['sel_ln_b']}
    _x0 = _d['L0_attn_x']
    _d['L0_attn_x'] = jax.random.normal(jax.random.fold_in(jax.random.key(seed), 1), (16, 256, 128), dtype=_x0.dtype)
    del _x0
    return _d

def reference(L0_attn_x, L0_attn_W_kv, L0_attn_g_kv, L0_attn_W_kdec, L0_attn_W_vdec, L0_attn_W_q, L0_attn_W_qdec, L0_attn_W_krope, L0_attn_W_qrope, L0_attn_W_o, L0_ffn_router_w, L0_ffn_router_b, L0_ffn_routed_w1, L0_ffn_routed_w3, L0_ffn_routed_w2, L0_ffn_shared_w1, L0_ffn_shared_w3, L0_ffn_shared_w2, L1_attn_Wq, L1_attn_Wk, L1_attn_Wv, L1_attn_Wo, L1_attn_rel_emb, L1_ffn_gate_w, L1_ffn_gate_b, L1_ffn_w1, L1_ffn_b1, L1_ffn_w2, L1_ffn_b2, L2_attn_Wq, L2_attn_Wk, L2_attn_Wv, L2_attn_Wo, L2_ffn_gamma_light, L2_ffn_wq_light, L2_ffn_wkv_light, L2_ffn_wo_light, L2_ffn_q_routing_token, L2_ffn_kv_routing_token, L2_ffn_gamma_heavy, L2_ffn_wq_heavy, L2_ffn_wkv_heavy, L2_ffn_wo_heavy, L3_attn_Wqkv_w, L3_attn_Wqkv_b, L3_attn_Wo_w, L3_attn_Wo_b, L3_attn_ghost, L3_ffn_index_b, L3_ffn_index_t, L3_ffn_sw1, L3_ffn_sb1, L3_ffn_sw2, L3_ffn_sb2, L3_ffn_sw3, L3_ffn_sb3, L3_ffn_s_ln_g, L3_ffn_s_ln_b, L3_ffn_sg_w, L3_ffn_sg_b, L3_ffn_eg_w, L3_ffn_eg_b, L3_ffn_exp_bias, L3_ffn_ew1, L3_ffn_eb1, L3_ffn_ew2, L3_ffn_eb2, L3_ffn_ew3, L3_ffn_eb3, L3_ffn_sel_ln_g, L3_ffn_sel_ln_b):

    def _L0_attn_ref(x, W_kv, g_kv, W_kdec, W_vdec, W_q, W_qdec, W_krope, W_qrope, W_o):
        import jax, jax.numpy as jnp
        import numpy as np
        N_EMBD = 128
        N_HEAD = 16
        HEAD_DIM = N_EMBD // N_HEAD
        KV_RANK = 32
        Q_RANK = 64
        ROPE_DIM = 32
        B, T = (2, 256)
        EPS = 1e-06

        def _rope_tables(T, dim):
            inv_freq = 1.0 / 10000.0 ** (np.arange(0, dim, 2, dtype=np.float32) / dim)
            t = np.arange(T, dtype=np.float32)
            freqs = np.outer(t, inv_freq)
            emb = np.concatenate([freqs, freqs], -1)
            return (jnp.asarray(np.cos(emb)), jnp.asarray(np.sin(emb)))

        def _apply_rope(x, cos, sin):
            d2 = x.shape[-1] // 2
            x1, x2 = (x[..., :d2], x[..., d2:])
            rot = jnp.concatenate([-x2, x1], axis=-1)
            return x * cos[None, None, :, :] + rot * sin[None, None, :, :]
        Bx, Tx, C = x.shape
        kv_c = x @ W_kv
        kv_c = kv_c * jax.lax.rsqrt(jnp.mean(kv_c * kv_c, axis=-1, keepdims=True) + EPS) * g_kv
        q_c = x @ W_q

        def heads(y, d):
            return y.reshape(Bx, Tx, N_HEAD, d).transpose(0, 2, 1, 3)
        k_content = heads(kv_c @ W_kdec, HEAD_DIM)
        v = heads(kv_c @ W_vdec, HEAD_DIM)
        q_content = heads(q_c @ W_qdec, HEAD_DIM)
        k_rope = heads(x @ W_krope, ROPE_DIM)
        q_rope = heads(q_c @ W_qrope, ROPE_DIM)
        cos, sin = _rope_tables(Tx, ROPE_DIM)
        q_rope = _apply_rope(q_rope, cos, sin)
        k_rope = _apply_rope(k_rope, cos, sin)
        q = jnp.concatenate([q_content, q_rope], axis=-1)
        k = jnp.concatenate([k_content, k_rope], axis=-1)
        scale = 1.0 / jnp.sqrt(jnp.float32(q.shape[-1]))
        scores = jnp.einsum('bhqd,bhkd->bhqk', q, k) * scale
        causal = jnp.tril(jnp.ones((Tx, Tx), dtype=bool))
        scores = jnp.where(causal[None, None], scores, jnp.float32(-jnp.inf))
        attn = jax.nn.softmax(scores, axis=-1)
        out = jnp.einsum('bhqk,bhkd->bhqd', attn, v)
        out = out.transpose(0, 2, 1, 3).reshape(Bx, Tx, N_HEAD * HEAD_DIM)
        return out @ W_o

    def _L0_ffn_ref(x, router_w, router_b, routed_w1, routed_w3, routed_w2, shared_w1, shared_w3, shared_w2):
        import jax, jax.numpy as jnp
        import numpy as np
        BEST_K = 2

        def _expert(xf, w1, w3, w2):
            return jax.nn.silu(xf @ w1) * (xf @ w3) @ w2
        B, S, D = x.shape
        T = B * S
        xf = x.reshape(T, D)
        logits = xf @ router_w + router_b
        topk_vals, topk_idx = jax.lax.top_k(logits, BEST_K)
        sparse = jnp.full_like(logits, -jnp.inf)
        sparse = sparse.at[jnp.arange(T)[:, None], topk_idx].set(topk_vals)
        gates = jax.nn.softmax(sparse, axis=-1)
        routed = jax.vmap(_expert, in_axes=(None, 0, 0, 0))(xf, routed_w1, routed_w3, routed_w2)
        routed_out = jnp.einsum('etd,te->td', routed, gates)
        shared_out = jax.vmap(_expert, in_axes=(None, 0, 0, 0))(xf, shared_w1, shared_w3, shared_w2).sum(axis=0)
        return (routed_out + shared_out).reshape(B, S, D)

    def _L1_attn_ref(x, Wq, Wk, Wv, Wo, rel_emb):
        import jax, jax.numpy as jnp
        import numpy as np
        from math import log, sqrt
        B, S, D, H = (2, 256, 128, 16)
        HD = D // H
        NUM_BUCKETS = 32
        MAX_DISTANCE = 128
        ROPE_BASE = 10000.0

        def _rope_cos_sin(seq_len, dim, base):
            inv_freq = 1.0 / base ** (jnp.arange(0, dim, 2, dtype=jnp.float32) / dim)
            t = jnp.arange(seq_len, dtype=jnp.float32)
            freqs = jnp.outer(t, inv_freq)
            emb = jnp.concatenate([freqs, freqs], axis=-1)
            return (jnp.cos(emb), jnp.sin(emb))

        def _rotate_half(t):
            d = t.shape[-1] // 2
            return jnp.concatenate([-t[..., d:], t[..., :d]], axis=-1)

        def _rel_pos_bucket(relative_position, num_buckets, max_distance):
            rp = -jnp.minimum(relative_position, 0)
            max_exact = num_buckets // 2
            is_small = rp < max_exact
            rp_f = jnp.maximum(rp.astype(jnp.float32), 1.0)
            large = max_exact + (jnp.log(rp_f / max_exact) / log(max_distance / max_exact) * (num_buckets - max_exact)).astype(jnp.int32)
            large = jnp.minimum(large, num_buckets - 1)
            return jnp.where(is_small, rp, large)
        b, s, d = x.shape

        def heads_split(t):
            return t.reshape(b, s, H, HD).transpose(0, 2, 1, 3)
        q = heads_split(x @ Wq)
        k = heads_split(x @ Wk)
        v = heads_split(x @ Wv)
        cos, sin = _rope_cos_sin(s, HD, ROPE_BASE)
        q = q * cos + _rotate_half(q) * sin
        k = k * cos + _rotate_half(k) * sin
        pos = jnp.arange(s, dtype=jnp.int32)
        rel = pos[None, :] - pos[:, None]
        buckets = _rel_pos_bucket(rel, NUM_BUCKETS, MAX_DISTANCE)
        bias = rel_emb[buckets].transpose(2, 0, 1)[None]
        scores = jnp.einsum('bhqd,bhkd->bhqk', q, k) / sqrt(HD) + bias
        causal = jnp.tril(jnp.ones((s, s), dtype=bool))
        scores = jnp.where(causal, scores, jnp.float32(-1000000000.0))
        attn = jax.nn.softmax(scores, axis=-1)
        ctx = jnp.einsum('bhqk,bhkd->bhqd', attn, v)
        ctx = ctx.transpose(0, 2, 1, 3).reshape(b, s, d)
        return ctx @ Wo

    def _L1_ffn_ref(x, gate_w, gate_b, w1, b1, w2, b2):
        import jax, jax.numpy as jnp
        import numpy as np
        TOP_K = 2
        B, S, D = x.shape
        E = gate_w.shape[0]
        logits = jnp.einsum('bsd,ed->bse', x, gate_w) + gate_b
        scores = jax.nn.softmax(logits, axis=-1)
        topk_scores, topk_idx = jax.lax.top_k(scores, TOP_K)
        onehot = jax.nn.one_hot(topk_idx, E, dtype=scores.dtype)
        dispatch = jnp.einsum('bsk,bske->bse', topk_scores, onehot)
        x_flat = x.reshape(B * S, D)
        w_flat = dispatch.reshape(B * S, E)
        out = jnp.zeros_like(x_flat)
        for i in range(E):
            wi = w_flat[:, i:i + 1]
            h = jax.nn.relu(jnp.einsum('nd,hd->nh', x_flat * wi, w1[i]) + b1[i])
            y = jnp.einsum('nh,dh->nd', h, w2[i]) + b2[i]
            out = jnp.where(wi > 0, y, out)
        return out.reshape(B, S, D)

    def _L2_attn_ref(x, Wq, Wk, Wv, Wo):
        import jax, jax.numpy as jnp
        import numpy as np
        NUM_HEADS = 16
        B, N, C = x.shape
        H = NUM_HEADS
        hd = C // H

        def proj(W):
            return (x @ W).reshape(B, N, H, 2 * hd).transpose(0, 2, 1, 3)
        q = proj(Wq)
        k = proj(Wk)
        v = proj(Wv)
        q_r, q_i = (q[..., :hd], q[..., hd:])
        k_r, k_i = (k[..., :hd], k[..., hd:])
        v_r, v_i = (v[..., :hd], v[..., hd:])
        scores = (jnp.einsum('bhnd,bhmd->bhnm', q_r, k_r) + jnp.einsum('bhnd,bhmd->bhnm', q_i, k_i)) / jnp.sqrt(jnp.float32(hd))
        causal = jnp.tril(jnp.ones((N, N), dtype=bool))
        scores = jnp.where(causal[None, None], scores, -jnp.inf)
        probs = jax.nn.softmax(scores, axis=-1)
        out_r = jnp.einsum('bhnm,bhmd->bhnd', probs, v_r)
        out_i = jnp.einsum('bhnm,bhmd->bhnd', probs, v_i)
        out = jnp.concatenate([out_r, out_i], axis=-1)
        out = out.transpose(0, 2, 1, 3).reshape(B, N, 2 * C)
        return out @ Wo

    def _L2_ffn_ref(x, gamma_light, wq_light, wkv_light, wo_light, q_routing_token, kv_routing_token, gamma_heavy, wq_heavy, wkv_heavy, wo_heavy):
        import jax, jax.numpy as jnp
        import numpy as np
        B, N, D = (4, 1024, 128)
        HEADS, DH = (8, 64)
        HID = HEADS * DH
        WIN = 128
        NQ, NKV = (128, 256)
        EPS, N_ITERS, FETCH_K = (1.0, 50, 9.0 / 8.0)
        SCALE = DH ** (-0.5)

        def rmsnorm(x, gamma):
            norm = jnp.maximum(jnp.linalg.norm(x, axis=-1, keepdims=True), 1e-12)
            return x / norm * x.shape[-1] ** 0.5 * gamma

        def coor_descent(s, k):
            logk = jnp.log(jnp.asarray(k, s.dtype))

            def body(_, ab):
                a, b = ab
                a = EPS * (logk - jax.nn.logsumexp((s + b) / EPS, axis=-1, keepdims=True))
                b = -jax.nn.relu(s + a)
                return (a, b)
            a, b = jax.lax.fori_loop(0, N_ITERS, body, (jnp.zeros_like(s[..., :1]), -s))
            return jnp.exp((s + a + b) / EPS)

        def route(x, routing_token, num_tokens):
            s = jnp.einsum('bnd,d->bn', x, routing_token)
            k = min(num_tokens * FETCH_K, x.shape[1])
            scores = coor_descent(s, k)
            sel_scores, sel_idx = jax.lax.top_k(scores, num_tokens)
            sel_scores = sel_scores + jax.lax.stop_gradient(1.0 - sel_scores)
            return (sel_scores, sel_idx)

        def light_local_attn(x, gamma, wq, wkv, wo):
            b, n, d = x.shape
            xn = rmsnorm(x, gamma)
            q = xn @ wq
            k, v = jnp.split(xn @ wkv, 2, axis=-1)

            def win(t):
                return t.reshape(b, n // WIN, WIN, HEADS, DH).transpose(0, 1, 3, 2, 4)
            q, k, v = (win(q) * SCALE, win(k), win(v))
            attn = jax.nn.softmax(jnp.einsum('bwhid,bwhjd->bwhij', q, k), axis=-1)
            out = jnp.einsum('bwhij,bwhjd->bwhid', attn, v)
            out = out.transpose(0, 1, 3, 2, 4).reshape(b, n, HID)
            return out @ wo

        def heavy_attn(xq, context, scores_kv, gamma, wq, wkv_t, wo):
            b, nq, d = xq.shape
            nkv = context.shape[1]
            xqn = rmsnorm(xq, gamma)
            ctx = rmsnorm(context, gamma)[:, None]
            q = (xqn @ wq).reshape(b, nq, HEADS, DH).transpose(0, 2, 1, 3) * SCALE
            kvw = wkv_t.reshape(1, HEADS, 2 * DH, d)
            kv = jnp.einsum('rhdi,brni->brhnd', kvw, ctx)
            k, v = jnp.split(kv, 2, axis=-1)
            v = v * scores_kv[:, None, None, :, None]
            k = k.reshape(b, HEADS, nkv, DH)
            v = v.reshape(b, HEADS, nkv, DH)
            attn = jax.nn.softmax(jnp.einsum('bhid,bhjd->bhij', q, k), axis=-1)
            out = jnp.einsum('bhij,bhjd->bhid', attn, v)
            out = out.transpose(0, 2, 1, 3).reshape(b, nq, HID)
            return out @ wo
        b = x.shape[0]
        light_out = light_local_attn(x, gamma_light, wq_light, wkv_light, wo_light)
        scores_q, idx_q = route(x, q_routing_token, NQ)
        scores_kv, idx_kv = route(x, kv_routing_token, NKV)
        routed_q = jnp.take_along_axis(x, idx_q[..., None], axis=1)
        routed_kv = jnp.take_along_axis(x, idx_kv[..., None], axis=1)
        routed_out = heavy_attn(routed_q, routed_kv, scores_kv, gamma_heavy, wq_heavy, wkv_heavy, wo_heavy)
        routed_out = routed_out * scores_q[..., None]
        heavy_out = jnp.zeros_like(x).at[jnp.arange(b)[:, None], idx_q].set(routed_out)
        return light_out + heavy_out

    def _L3_attn_ref(inputs, Wqkv_w, Wqkv_b, Wo_w, Wo_b, ghost):
        import jax, jax.numpy as jnp
        import numpy as np
        import math
        EMBED_DIM = 128
        NHEAD = 16
        HEAD_DIM = 64
        BATCH = 2
        SEQ = 256
        b, s, e = inputs.shape
        QKV = inputs @ Wqkv_w.T + Wqkv_b
        QKVh = QKV.reshape(b, s, 3, NHEAD, HEAD_DIM).transpose(0, 3, 2, 1, 4)
        Q, K, V = (QKVh[:, :, 0], QKVh[:, :, 1], QKVh[:, :, 2])
        scores = jnp.einsum('bhqd,bhkd->bhqk', Q, K) / math.sqrt(HEAD_DIM)
        row = jnp.arange(s)
        mask = jnp.where(row[None, :] > row[:, None], -jnp.inf, 0.0).astype(scores.dtype)
        scores = scores + mask[None, None]
        m = jnp.max(scores, axis=-1, keepdims=True)
        z = jnp.exp(scores - m)
        S = z / (jnp.sum(z, axis=-1, keepdims=True) + ghost.reshape(1, -1, 1, 1))
        A = jnp.einsum('bhqk,bhkd->bhqd', S, V)
        A = A.transpose(0, 2, 1, 3).reshape(b, s, NHEAD * HEAD_DIM)
        return A @ Wo_w.T + Wo_b

    def _L3_ffn_ref(x, index_b, index_t, sw1, sb1, sw2, sb2, sw3, sb3, s_ln_g, s_ln_b, sg_w, sg_b, eg_w, eg_b, exp_bias, ew1, eb1, ew2, eb2, ew3, eb3, sel_ln_g, sel_ln_b):
        import jax, jax.numpy as jnp
        import numpy as np
        EPS = 1e-05

        def _ln(x, g, b):
            mu = jnp.mean(x, axis=-1, keepdims=True)
            var = jnp.mean(jnp.square(x - mu), axis=-1, keepdims=True)
            return (x - mu) * jax.lax.rsqrt(var + EPS) * g + b

        def _forward(x, index_b, index_t, sw1, sb1, sw2, sb2, sw3, sb3, s_ln_g, s_ln_b, sg_w, sg_b, eg_w, eg_b, exp_bias, ew1, eb1, ew2, eb2, ew3, eb3, sel_ln_g, sel_ln_b):
            x1 = jnp.einsum('btd,hd->bth', x, sw1) + sb1
            x2 = jnp.einsum('btd,hd->bth', x, sw2) + sb2
            sh = _ln(jax.nn.silu(x1) * x2, s_ln_g, s_ln_b)
            shared_out = jnp.einsum('bth,dh->btd', sh, sw3) + sb3
            x_moe = x[index_b, index_t]
            shared_scores = jax.nn.sigmoid(x_moe @ sg_w.T + sg_b)
            expert_scores = jax.nn.sigmoid(x_moe @ eg_w.T + eg_b)
            top1_idx = jnp.argmax(expert_scores + exp_bias, axis=-1)
            top1_score = jnp.take_along_axis(expert_scores, top1_idx[:, None], axis=-1)
            weights = jax.nn.softmax(jnp.concatenate([shared_scores, top1_score], axis=-1), axis=-1)
            shared_w, expert_w = (weights[:, 0], weights[:, 1])
            shared_moe_out = shared_out[index_b, index_t] * shared_w[:, None]
            h1 = jnp.einsum('md,ehd->meh', x_moe, ew1) + eb1
            h2 = jnp.einsum('md,ehd->meh', x_moe, ew2) + eb2
            z = _ln(jax.nn.silu(h1) * h2, sel_ln_g, sel_ln_b)
            out_all = jnp.einsum('meh,edh->med', z, ew3) + eb3
            expert_out = jnp.take_along_axis(out_all, top1_idx[:, None, None], axis=1)[:, 0]
            expert_moe_out = expert_out * expert_w[:, None]
            final_out = shared_out.at[index_b, index_t].set(shared_moe_out + expert_moe_out)
            return final_out
        return _forward(x, index_b, index_t, sw1, sb1, sw2, sb2, sw3, sb3, s_ln_g, s_ln_b, sg_w, sg_b, eg_w, eg_b, exp_bias, ew1, eb1, ew2, eb2, ew3, eb3, sel_ln_g, sel_ln_b)
    x = L0_attn_x
    x = _layernorm(x + _L0_attn_ref(x, L0_attn_W_kv, L0_attn_g_kv, L0_attn_W_kdec, L0_attn_W_vdec, L0_attn_W_q, L0_attn_W_qdec, L0_attn_W_krope, L0_attn_W_qrope, L0_attn_W_o), axis=-1)
    x = _layernorm(x + _L0_ffn_ref(x, L0_ffn_router_w, L0_ffn_router_b, L0_ffn_routed_w1, L0_ffn_routed_w3, L0_ffn_routed_w2, L0_ffn_shared_w1, L0_ffn_shared_w3, L0_ffn_shared_w2), axis=-1)
    x = _layernorm(x + _L1_attn_ref(x, L1_attn_Wq, L1_attn_Wk, L1_attn_Wv, L1_attn_Wo, L1_attn_rel_emb), axis=-1)
    x = _layernorm(x + _L1_ffn_ref(x, L1_ffn_gate_w, L1_ffn_gate_b, L1_ffn_w1, L1_ffn_b1, L1_ffn_w2, L1_ffn_b2), axis=-1)
    x = _layernorm(x + _L2_attn_ref(x, L2_attn_Wq, L2_attn_Wk, L2_attn_Wv, L2_attn_Wo), axis=-1)
    x = _layernorm(x + _L2_ffn_ref(x, L2_ffn_gamma_light, L2_ffn_wq_light, L2_ffn_wkv_light, L2_ffn_wo_light, L2_ffn_q_routing_token, L2_ffn_kv_routing_token, L2_ffn_gamma_heavy, L2_ffn_wq_heavy, L2_ffn_wkv_heavy, L2_ffn_wo_heavy), axis=-1)
    x = _layernorm(x + _L3_attn_ref(x, L3_attn_Wqkv_w, L3_attn_Wqkv_b, L3_attn_Wo_w, L3_attn_Wo_b, L3_attn_ghost), axis=-1)
    x = _layernorm(x + _L3_ffn_ref(x, L3_ffn_index_b, L3_ffn_index_t, L3_ffn_sw1, L3_ffn_sb1, L3_ffn_sw2, L3_ffn_sb2, L3_ffn_sw3, L3_ffn_sb3, L3_ffn_s_ln_g, L3_ffn_s_ln_b, L3_ffn_sg_w, L3_ffn_sg_b, L3_ffn_eg_w, L3_ffn_eg_b, L3_ffn_exp_bias, L3_ffn_ew1, L3_ffn_eb1, L3_ffn_ew2, L3_ffn_eb2, L3_ffn_ew3, L3_ffn_eb3, L3_ffn_sel_ln_g, L3_ffn_sel_ln_b), axis=-1)
    return x

_drawn_inputs = setup_inputs


def setup_inputs(seed=0):
    import zlib

    import numpy as np

    out = dict(_drawn_inputs(seed))
    spreads = {'L0_attn_g_kv': (1.0, 0.2),
     'L0_ffn_router_b': (0.0, 0.536),
     'L1_ffn_gate_b': (0.0, 0.1),
     'L1_ffn_b1': (0.0, 0.1),
     'L1_ffn_b2': (0.0, 0.1),
     'L2_ffn_gamma_light': (1.0, 0.2),
     'L2_ffn_gamma_heavy': (1.0, 0.2),
     'L3_attn_Wqkv_b': (0.0, 0.1),
     'L3_attn_Wo_b': (0.0, 0.1),
     'L3_ffn_sb1': (0.0, 0.1),
     'L3_ffn_sb2': (0.0, 0.1),
     'L3_ffn_sb3': (0.0, 0.1),
     'L3_ffn_s_ln_g': (1.0, 0.2),
     'L3_ffn_s_ln_b': (0.0, 0.455),
     'L3_ffn_eg_b': (0.0, 0.493),
     'L3_ffn_exp_bias': (0.0, 0.1),
     'L3_ffn_eb1': (0.0, 0.8),
     'L3_ffn_eb2': (0.0, 0.8),
     'L3_ffn_eb3': (0.0, 0.611),
     'L3_ffn_sel_ln_g': (1.0, 0.6),
     'L3_ffn_sel_ln_b': (0.0, 0.8)}
    factors = {'L0_ffn_router_w': 3.498,
     'L0_ffn_routed_w1': 3.614,
     'L0_ffn_routed_w3': 3.247,
     'L0_ffn_routed_w2': 3.471,
     'L1_attn_Wq': 5.407,
     'L1_attn_Wk': 6.331,
     'L1_attn_rel_emb': 37.143,
     'L2_ffn_kv_routing_token': 64.0,
     'L3_attn_ghost': 4.969,
     'L3_ffn_sg_w': 37.034,
     'L3_ffn_eg_w': 2.942,
     'L3_ffn_ew1': 3.207,
     'L3_ffn_ew2': 3.263,
     'L3_ffn_ew3': 2.948}
    for name, (base, spread) in spreads.items():
        noise = np.random.default_rng([zlib.crc32(name.encode()), seed]).standard_normal(out[name].shape)
        drawn = base * np.exp(spread * noise) if base else spread * noise
        out[name] = jnp.asarray(drawn.astype(out[name].dtype))
    for name, factor in factors.items():
        out[name] = (out[name] * factor).astype(out[name].dtype)
    return out
```

```python
import math
from contextlib import ExitStack

import numpy as np

import concourse.bass as bass
from concourse import mybir

ALU = mybir.AluOpType
ACT = mybir.ActivationFunctionType
AX = mybir.AxisListType
F32 = mybir.dt.float32
U32 = mybir.dt.uint32

P = 128
BATCH, SEQ, DM = 16, 256, 128
TILES = BATCH * SEQ // P
TOK = BATCH * SEQ
BIG = 1.0e30
LN_EPS = 1e-5
CREDIT = 1
BANK = 512
W_COLS = (5760, 8864)


def rope_tables(dim, heads_rows, content, scale):
    inv = (1.0 / 10000.0 ** (np.arange(0, dim, 2, dtype=np.float32) / np.float32(dim))).astype(np.float32)
    f = np.outer(np.arange(SEQ, dtype=np.float32), inv)
    emb = np.concatenate([f, f], -1).astype(np.float32)
    c, s = np.cos(emb).T, np.sin(emb).T.copy()
    s[: dim // 2] *= -1.0
    one = np.concatenate([np.ones((content, SEQ), np.float32), c], 0)
    two = np.concatenate([np.zeros((content, SEQ), np.float32), s], 0)
    pad = np.zeros((P, 2, SEQ), np.float32)
    n = heads_rows * (content + dim)
    pad[:n, 0] = np.tile(one, (heads_rows, 1)) * np.float32(scale)
    pad[:n, 1] = np.tile(two, (heads_rows, 1)) * np.float32(scale)
    return pad.reshape(P, 2 * SEQ)


def head_rows(D):
    hpc = P // D
    m = np.zeros((P, hpc), np.float32)
    for h in range(hpc):
        m[h * D:(h + 1) * D, h] = 1.0
    return m


def shape_constants():
    q = np.arange(P)[:, None]
    c = np.arange(2 * P)[None, :]
    dist = 255 - np.arange(383)
    n = np.maximum(dist, 0)
    large = 16 + (np.log(np.maximum(n, 1).astype(np.float32) / np.float32(16)) / np.float32(math.log(8.0))
                  * np.float32(16)).astype(np.int32)
    bucket = np.where(n < 16, n, np.minimum(large, 31))
    onehot = np.zeros((P, 383), np.float32)
    onehot[bucket, np.arange(383)] = 1.0
    onehot[:, dist < 0] = 0.0
    neg = np.zeros((P, 383), np.float32)
    neg[:, dist < 0] = BIG
    logk = np.zeros((P, 1), np.float32)
    logk[0:BATCH] = np.log(np.float32(144.0))
    logk[BATCH:2 * BATCH] = np.log(np.float32(256.0))
    before = np.concatenate([(c < q), (c < q + P)], 1).astype(np.float32)
    parts = [
        ("ident", np.eye(P, dtype=np.float32)),
        ("flip", np.ascontiguousarray(np.eye(P, dtype=np.float32)[::-1])),
        ("causal", np.where(c - P > q, np.float32(BIG), np.float32(0.0)).astype(np.float32)),
        ("rope40q", rope_tables(32, 3, 8, -1.0 / math.sqrt(40.0))),
        ("rope40k", rope_tables(32, 3, 8, 1.0)),
        ("rope8q", rope_tables(8, 16, 0, -1.0 / math.sqrt(8.0))),
        ("rope8k", rope_tables(8, 16, 0, 1.0)),
        ("heads40", head_rows(40)), ("heads8", head_rows(8)), ("heads16", head_rows(16)), ("heads64", head_rows(64)),
        ("bucket", onehot), ("future", neg), ("logk", logk), ("before", before),
        ("gaterows", np.pad(np.repeat(np.eye(8, dtype=np.float32), 64, 1), ((0, P - 8), (0, 0)))),
        ("iota8", np.tile(np.arange(8, dtype=np.float32), (P, 1))),
    ]
    at, out, resident, staged = 0, {}, [], {}
    for name, a in parts:
        if name in STAGED:
            staged[name] = a
            continue
        out[name] = (at, a.shape[1])
        at += a.shape[1]
        resident.append(a)
    return out, np.ascontiguousarray(np.concatenate(resident, 1)), staged


STAGED = {"rope40q": 0, "rope40k": 0, "gaterows": 1, "rope8q": 2, "rope8k": 2, "bucket": 2, "future": 2, "before": 5}


class Core:

    def __init__(self, nc, ctx, dram):
        self.nc, self.dram = nc, dram
        self.at, table, _ = shape_constants()
        self.X = ctx.enter_context(nc.sbuf_tensor("X", [P, TILES, DM], F32))
        self.XT = ctx.enter_context(nc.sbuf_tensor("XT", [P, (BATCH + 1) * SEQ], F32))
        self.cst = ctx.enter_context(nc.sbuf_tensor("cst", [P, table.shape[1]], F32))
        self.mv = ctx.enter_context(nc.sbuf_tensor("mv", [P, TILES, 2], F32))
        self.rstd = ctx.enter_context(nc.sbuf_tensor("rstd", [P, TILES], F32))
        self.W = [ctx.enter_context(nc.sbuf_tensor(f"W{i}", [P, W_COLS[i]], F32)) for i in range(2)]
        self.bank = [ctx.enter_context(nc.psum_tensor(f"bank{i}", [P, BANK], F32)) for i in range(8)]
        self.weights_in = [ctx.enter_context(nc.semaphore(f"weights_in{k}")) for k in range(8)]
        self.carried = ctx.enter_context(nc.semaphore("carried"))
        self.consts_in = ctx.enter_context(nc.semaphore("consts_in"))

    def const(self, name, rows=P):
        if name in STAGED:
            return weight(self, STAGED[name], name)[0:rows, :]
        a, n = self.at[name]
        return self.cst[0:rows, a:a + n]


def place_weights(items, region_cols):
    at, out = 0, {}
    for name, rows, cols in items:
        out[name] = (rows, at, cols)
        at += cols
    assert at <= region_cols, (at, region_cols)
    return out


WEIGHTS = {
    0: [("l0_wkv", 128, 32), ("l0_wq", 128, 64), ("l0_gkv", 32, 1), ("l0_wqall", 64, 640), ("l0_wqrot", 64, 640),
        ("l0_wkdec", 32, 640), ("l0_wkrope", 128, 640), ("l0_wkrot", 128, 640), ("l0_wvdec", 32, 128),
        ("l0_wo", 128, 512), ("rope40q", 128, 512), ("rope40k", 128, 512)],
    1: [("l0_rw", 128, 8), ("l0_rb", 128, 8), ("l0_w1", 128, 640), ("l0_w3", 128, 640), ("l0_w2", 128, 640), ("gaterows", 128, 512)],
    2: [("l1_wq", 128, 128), ("l1_wqrot", 128, 128), ("l1_wk", 128, 128), ("l1_wkrot", 128, 128),
        ("l1_wv", 128, 128), ("l1_rel", 32, 16), ("l1_wo", 128, 512), ("rope8q", 128, 512), ("rope8k", 128, 512), ("bucket", 128, 383),
        ("future", 128, 383)],
    3: [("l1_gw", 128, 8), ("l1_gb", 128, 8), ("l1_w1", 128, 4096), ("l1_b1", 8, 512), ("l1_w2", 128, 4096),
        ("l1_b2", 8, 128)],
    4: [("l2_wq", 128, 256), ("l2_wk", 128, 256), ("l2_wv", 128, 256), ("l2_wo", 128, 512)],
    5: [("l2_gl", 128, 1), ("l2_wql", 128, 512), ("l2_wkl", 128, 512), ("l2_wvl", 128, 512), ("l2_wol", 128, 512),
        ("l2_tok", 128, 64), ("before", 128, 512),
        ("l2_gh", 128, 1), ("l2_wqh", 128, 512), ("l2_wkh", 128, 512), ("l2_wvh", 128, 512), ("l2_woh", 128, 512)],
    6: [("l3_wq", 128, 1024), ("l3_wk", 128, 1024), ("l3_wv", 128, 1024), ("l3_bq", 128, 8), ("l3_bk", 128, 8),
        ("l3_bv", 128, 1024), ("l3_wo", 128, 1024), ("l3_bo", 128, 128), ("l3_ghost", 128, 16)],
    7: [("l3_s1", 128, 128), ("l3_sb", 128, 128), ("l3_s3", 64, 128), ("l3_sb3", 128, 128), ("l3_sln", 128, 128),
        ("l3_gw", 128, 9), ("l3_gb", 128, 9), ("l3_eb", 128, 8), ("l3_e1", 128, 512), ("l3_e2", 128, 512),
        ("l3_eb1", 128, 512), ("l3_eb2", 128, 512), ("l3_e3", 128, 512), ("l3_eb3", 8, 128), ("l3_eln", 128, 128),
        ("l3_token", 128, 32), ("l3_base", 128, 8), ("l3_iota", 128, 512)],
}
LAYOUT = {k: place_weights(v, W_COLS[k % 2]) for k, v in WEIGHTS.items()}


def weight(core, k, name):
    rows, at, cols = LAYOUT[k][name]
    return core.W[k % 2][0:rows, at:at + cols]


def load_weights(core, eng, k):
    for name, rows, cols in WEIGHTS[k]:
        src = core.dram[name]
        if src.shape[0] == 1 and rows > 1:
            src = src.to_broadcast([rows, cols])
        eng.dma_start(weight(core, k, name), src).then_inc(core.weights_in[k], 16)


def new_sem(core, ctx, name, credited):
    s = core.nc.alloc_semaphore(name)
    credited.append(s)
    return s


def retire(core, credited):
    core.nc.clear_and_free_semaphores(credited)
    core.nc.all_engine_barrier()


def give_credit(sp, credited):
    for s in credited:
        sp.sem_inc(s, 1)


def counter(start):
    total = [start]

    def one_more():
        total[0] += 1
        return total[0]

    return one_more


def carry_waits(core, eng):
    eng.sem_inc(core.carried, 1)


def loaded_count(k):
    return 16 * len(WEIGHTS[k])


def normalize_stage(core, ctx, n, first=False, last=False, unit=False, next_weights=()):
    nc, X, XT = core.nc, core.X, core.XT
    G = 4
    GROUPS = TILES // G
    SQUARES = 8
    LOADS = 4 if first else 0
    BY_ACT = 5
    credited = []
    sem = lambda s: new_sem(core, ctx, f"n{n}_{s}", credited)
    with ExitStack() as mem:
        mem.callback(retire, core, credited)
        std = mem.enter_context(nc.sbuf_tensor(f"n{n}_std", [P, TILES], F32))
        sq = mem.enter_context(nc.sbuf_tensor(f"n{n}_sq", [P, SQUARES, DM], F32)) if unit else None
        normed = mem.enter_context(nc.sbuf_tensor(f"n{n}_unit", [P, TILES, DM], F32)) if unit else X
        x_loaded = [sem(f"x_loaded{k}") for k in range(LOADS)]
        var_ready, std_ready, rstd_ready = sem("var_ready"), sem("std_ready"), sem("rstd_ready")
        group_normed, group_turned, out_stored, squared = (
            sem("group_normed"), sem("group_turned"), sem("out_stored"), sem("squared"))
        ident = core.const("ident")
        block = mem.enter_context(nc.Block())

        @block.sync
        def _(sp):
            give_credit(sp, credited)
            if first:
                sp.dma_start(core.cst[:, :], core.dram["consts"]).then_inc(core.consts_in, 16)
                x = core.dram["x"].rearrange("(t p) d -> p t d", p=P)
                for k in range(LOADS):
                    part = slice(k * TILES // LOADS, (k + 1) * TILES // LOADS)
                    sp.dma_start(X[:, part, :], x[:, part, :]).then_inc(x_loaded[k], 16)
            for k in next_weights:
                load_weights(core, sp, k)
            if last:
                out = core.dram["out"].rearrange("(t p) d -> p t d", p=P)
                for g in range(GROUPS):
                    sp.wait_ge(group_normed, g + 1 + CREDIT)
                    sp.dma_start(out[:, g * G:(g + 1) * G, :], X[:, g * G:(g + 1) * G, :]).then_inc(out_stored, 16)
                sp.wait_ge(out_stored, 16 * GROUPS + CREDIT)

        @block.vector
        def _(dve):
            dve.wait_ge(credited[-1], CREDIT)
            if first:
                dve.memset(XT[:, TOK:], 0.0)
            elif unit:
                squared_so_far = counter(CREDIT)
                for c in range(0, TILES, SQUARES):
                    dve.tensor_tensor(sq[:, :, :], X[:, c:c + SQUARES, :], X[:, c:c + SQUARES, :], ALU.mult
                                      ).then_inc(squared, 1)
                    dve.wait_ge(squared, squared_so_far())
                    dve.tensor_reduce(core.rstd[:, c:c + SQUARES], sq[:, :, :], AX.X, ALU.add).then_inc(squared, 1)
                    dve.wait_ge(squared, squared_so_far())
                dve.tensor_scalar(core.rstd[:, :], core.rstd[:, :], 1.0 / DM, None, ALU.mult).then_inc(var_ready, 1)
                dve.wait_ge(std_ready, 1 + CREDIT)
                dve.tensor_scalar(std[:, :], std[:, :], 1e-12 / math.sqrt(DM), None, ALU.max).then_inc(var_ready, 1)
                dve.wait_ge(var_ready, 2 + CREDIT)
                dve.reciprocal(core.rstd[:, :], std[:, :]).then_inc(rstd_ready, 1)
                dve.wait_ge(rstd_ready, 1 + CREDIT)
            else:
                dve.tensor_scalar(core.rstd[:, :], core.mv[:, :, 1], LN_EPS, None, ALU.add).then_inc(var_ready, 1)
                dve.wait_ge(std_ready, 1 + CREDIT)
                dve.reciprocal(core.rstd[:, :], std[:, :]).then_inc(rstd_ready, 1)
                dve.wait_ge(rstd_ready, 1 + CREDIT)
            for t in range(TILES):
                if first:
                    break
                if unit:
                    ins = dve.tensor_scalar(normed[:, t, :], X[:, t, :], core.rstd[:, t:t + 1], None, ALU.mult)
                else:
                    ins = dve.tensor_scalar(X[:, t, :], X[:, t, :], core.mv[:, t, 0:1], core.rstd[:, t:t + 1],
                                            ALU.subtract, ALU.mult)
                if t % G == G - 1:
                    ins.then_inc(group_normed, 1)
            if not last:
                for g in range(BY_ACT, GROUPS):
                    dve.wait_ge(group_turned, g + 1 + CREDIT)
                    dve.tensor_copy(XT[:, g * BANK:(g + 1) * BANK], core.bank[g][:, :])

        @block.tensor
        def _(pe):
            pe.wait_ge(core.consts_in, 16)
            if last:
                return
            for g in range(GROUPS):
                if first:
                    pe.wait_ge(x_loaded[g * LOADS // GROUPS], 16 + CREDIT)
                else:
                    pe.wait_ge(group_normed, g + 1 + CREDIT)
                for t in range(G):
                    mm = pe.transpose(core.bank[g][:, t * P:(t + 1) * P], normed[:, g * G + t, :], ident)
                mm.then_inc(group_turned, 1)

        @block.scalar
        def _(act):
            if not first:
                act.wait_ge(var_ready, 1 + CREDIT)
                act.activation(std[:, :], core.rstd[:, :], ACT.Sqrt).then_inc(std_ready, 1)
            if not last:
                for g in range(BY_ACT):
                    act.wait_ge(group_turned, g + 1 + CREDIT)
                    act.activation(XT[:, g * BANK:(g + 1) * BANK], core.bank[g][:, :], ACT.Copy)


class Heads:

    def __init__(self, H, D, dv, keys, causal=False):
        self.H, self.D, self.dv, self.causal = H, D, dv, causal
        self.hpc = P // D
        self.chunks = -(-H // self.hpc)
        self.dvp = 32 if dv <= 32 else 64
        self.hps = P // self.dvp
        self.slots = H // self.hps
        self.keys = keys
        self.units = [(qt, h, BANK // keys[qt][1]) for qt in range(2)
                      for h in range(0, H, BANK // keys[qt][1])]
        self.two_banks = self.slots > 4

    def rows(self, c):
        return min(self.hpc, self.H - c * self.hpc) * self.D


def attention_stage(core, ctx, n, hd, steps, epilogue, setup=None, moments=True,
                    next_weights=(), head_bias=False, ghost=None, weights_of=None):
    nc, X, XT = core.nc, core.X, core.XT
    wk = n if weights_of is None else weights_of
    H, dv, dvp, hps, slots, keys, units = hd.H, hd.dv, hd.dvp, hd.hps, hd.slots, hd.keys, hd.units
    U = len(units)
    LT, LV = (3, 5) if U >= 8 else (2, 3)
    LE = LV - 1 if hd.two_banks else LV
    TAIL = LE + (6 if moments else 3)
    per_qt = [sum(1 for u in units if u[0] == qt) for qt in range(2)]
    last_of = [per_qt[0] - 1, U - 1]
    credited = []
    sem = lambda s: new_sem(core, ctx, f"a{n}_{s}", credited)
    mem = ExitStack()
    sb = lambda s, shape, dt=F32: mem.enter_context(nc.sbuf_tensor(f"a{n}_{s}", shape, dt))
    with mem:
        mem.callback(retire, core, credited)
        S0, S1, T0, T1, O0, O1, PRE, EPI = core.bank
        sbank, tbank, obank = [S0, S1], [T0, T1], [O0, O1]
        B = {}
        B["xs"] = sb("xs", [P, SEQ])
        B["q"] = [sb(f"q{i}", [P, hd.chunks, SEQ]) for i in range(2)]
        B["k"] = sb("k", [P, hd.chunks, SEQ])
        B["kx"] = [sb(f"kx{i}", [P, H, SEQ]) for i in range(2)]
        B["v"] = [sb(f"v{i}", [P, 2, H, dvp]) for i in range(2)]
        masked = hd.causal
        R = 4
        sm = [sb(f"sm{i}", [P, BANK]) for i in range(R)] if masked else None
        pr = [sb(f"pr{i}", [P, BANK]) for i in range(R)]
        pt = [sb(f"pt{i}", [P, BANK]) for i in range(R)]
        top = sb("top", [P, 2, H])
        den = sb("den", [P, 2, H])
        rden = sb("rden", [P, 2, H])
        rx = sb("rx", [P, H, dvp])
        rt = sb("rt", [P, slots, P])
        on = sb("on", [P, slots, P])
        B["bias"] = sb("bias", [P, H, SEQ]) if head_bias else None
        S = {}
        for s in ("x_copied", "step_mm", "step_out", "k_spread", "k_out", "scores", "masked", "probs", "turned", "turned_out0",
                  "turned_out1", "values", "recip", "repeated", "rep_turned", "rep_out", "normed", "projected",
                  "residual", "stats", "aggregated", "v_zero", "ghosted",
                  "rope_added", "epilogue", "moments_kept"):
            S[s] = sem(s)
        steps.alloc(sb, sem, B, S)
        B["stat"] = sb("stat", [P, 6])
        B["mv"] = sb("mv", [P, 2])
        epilogue.alloc(sb, B)
        if head_bias:
            bias_setup_stage(core, ctx, B["bias"][:, :, :])
        ident = core.const("ident")
        causal = core.const("causal")
        hmask = core.const(f"heads{hd.D}")
        NS = steps.count
        NK = steps.kinds.count("k")
        NR = NK + steps.kinds.count("q")
        EW = 2 if hd.two_banks else 1
        block = mem.enter_context(nc.Block())

        at_slot = [[] for _ in range(U)]
        for j in range(NS):
            at_slot[min(U - 1, 1 + j * (U - 1) // NS)].append(j)

        def unit_runs(u):
            qt, h0, nh = units[u]
            h = h0
            while h < h0 + nh:
                c = h // hd.hpc
                m = min(h0 + nh, (c + 1) * hd.hpc) - h
                yield h, m, c
                h += m

        def end_of(e):
            return (e // 2) * U + last_of[e % 2]

        def slots_of_pair(eng, slot):
            for s in range(2 * U):
                slot(0, s)
            with eng.Fori(1, BATCH // 2) as i:
                for s in range(2 * U):
                    slot(i, s)
            for s in range(TAIL):
                slot(BATCH // 2, s)

        def lagging(i, s, lag):
            u = s - lag
            if (u >= 0 and in_pair(i, s)) or (u < 0 and not (isinstance(i, int) and i == 0)):
                return [u]
            return []

        def in_pair(i, s):
            return not (isinstance(i, int) and i == BATCH // 2)

        def ending(i, s, lag):
            return [e for e in range(-4, 4) if end_of(e) == s - lag and lagging(i, s, lag)]

        @block.sync
        def _(sp):
            give_credit(sp, credited)
            for k in next_weights:
                load_weights(core, sp, k)

        @block.tensor
        def _(pe):
            pe.wait_ge(core.weights_in[wk], loaded_count(wk))

            def scores(i, s):
                b, u = divmod(s % (2 * U), U)
                qt, h0, nh = units[u]
                k0, kw = keys[qt]
                read = S["masked"] if masked else S["probs"]
                pe.wait_ge(read, total(i, 2 * U, s - 1) + CREDIT)
                if u == 0:
                    pe.wait_ge(S["k_spread"], (2 * i + b + 1) * NK + CREDIT)
                    pe.wait_ge(S["step_out"], (2 * i + b + 1) * NS + CREDIT)
                    if steps.roped:
                        pe.wait_ge(S["rope_added"], (2 * i + b + 1) * NR + CREDIT)
                for h, m, c in unit_runs(u):
                    rows = hd.rows(c)
                    mm = pe.matmul(sbank[s % 2][:, (h - h0) * kw:(h - h0 + m) * kw],
                                   B["q"][b][0:rows, c, qt * P:(qt + 1) * P],
                                   B["kx"][b][0:rows, h:h + m, k0:k0 + kw], start=True, stop=True)
                mm.then_inc(S["scores"], 1)

            def turn(i, s):
                b, u = divmod(s % (2 * U), U)
                pe.wait_ge(S["probs"], i * 2 * U + s + 1 + CREDIT)
                out = S["turned_out%d" % (s % 2)]
                pe.wait_ge(out, i * U + s // 2 + CREDIT)
                for j in range(4):
                    mm = pe.transpose(tbank[s % 2][:, j * P:(j + 1) * P], pr[s % R][:, j * P:(j + 1) * P], ident)
                mm.then_inc(S["turned"], 1)

            def values(i, s):
                b, u = divmod(s % (2 * U), U)
                qt, h0, nh = units[u]
                k0, kw = keys[qt]
                pe.wait_ge(S["turned_out%d" % (s % 2)], i * U + s // 2 + 1 + CREDIT)
                if h0 == 0:
                    e = s // U * 2 + qt
                    pe.wait_ge(S["normed"], total(i, 4, e - (0 if hd.two_banks else 1)) + CREDIT)
                nb = kw // P
                for h in range(h0, h0 + nh):
                    slot, j = divmod(h, hps)
                    ob = obank[slot // 4] if hd.two_banks else obank[qt]
                    o = ob[j * dvp:(j + 1) * dvp, (slot % 4) * P:(slot % 4 + 1) * P]
                    for kb in range(nb):
                        col = ((h - h0) * nb + kb) * P
                        mm = pe.matmul(o, B["v"][b][:, k0 // P + kb, h, :], pt[s % R][:, col:col + P],
                                       start=(kb == 0), stop=(kb == nb - 1))
                mm.then_inc(S["values"], 1)

            def epi_turn(i, e):
                for r in range(EW):
                    ne = (4 * i + e) * EW + r
                    if r == 0:
                        pe.wait_ge(S["repeated"], 4 * i + e + 1 + CREDIT)
                        pe.wait_ge(S["residual"], 4 * i + e + CREDIT)
                    pe.wait_ge(S["rep_out"], ne + CREDIT)
                    for j in range(4):
                        mm = pe.transpose(EPI[:, j * P:(j + 1) * P],
                                          rx[:, (r * 4 + j) * hps:(r * 4 + j + 1) * hps, :].rearrange("p a b -> p (a b)"),
                                          ident)
                    mm.then_inc(S["rep_turned"], 1)

            def epi_project(i, e):
                pe.wait_ge(S["normed"], 4 * i + e + 1 + CREDIT)
                wo = epilogue.wo
                for j in range(slots):
                    mm = pe.matmul(EPI[:, 0:DM], on[:, j, :], wo[:, j * DM:(j + 1) * DM],
                                   start=(j == 0), stop=(j == slots - 1))
                mm.then_inc(S["projected"], 1)

            def step(i, b, j):
                seq = 2 * i + b
                pe.wait_ge(S["step_out"], seq * NS + j + CREDIT)
                if j == 0:
                    pe.wait_ge(S["x_copied"], seq + 1 + CREDIT)
                steps.pe(pe, core, B, S, PRE, j, b % 2, seq).then_inc(S["step_mm"], 1)

            for j in range(NS):
                step(0, 0, j)

            def slot(i, s):
                if in_pair(i, s):
                    scores(i, s)
                    b, u = divmod(s, U)
                    for j in at_slot[u]:
                        step(i, b + 1, j)
                for v in lagging(i, s, LT):
                    turn(i, v)
                for v in lagging(i, s, LV):
                    values(i, v)
                for e in ending(i, s, LE + 2):
                    epi_project(i, e)
                for e in ending(i, s, LE):
                    epi_turn(i, e)

            slots_of_pair(pe, slot)

        @block.vector
        def _(dve):
            dve.wait_ge(core.weights_in[wk], loaded_count(wk))
            for b in range(2):
                dve.memset(B["v"][b][:, :, :, :], 0.0).then_inc(S["v_zero"], 1)

            def mask(i, s):
                b, u = divmod(s % (2 * U), U)
                qt, h0, nh = units[u]
                k0, kw = keys[qt]
                dve.wait_ge(S["scores"], i * 2 * U + s + 1 + CREDIT)
                if masked:
                    dve.wait_ge(S["probs"], total(i, 2 * U, s - R + 1) + CREDIT)
                    carry_waits(core, dve)
                    m0 = SEQ - kw
                    for h in range(nh):
                        mk = B["bias"][:, h0 + h, m0:SEQ] if head_bias else causal[:, m0:SEQ]
                        ins = dve.tensor_tensor_reduce(
                            sm[s % R][:, h * kw:(h + 1) * kw], sbank[s % 2][:, h * kw:(h + 1) * kw], mk,
                            1.0, 3.0e38, ALU.add, ALU.min, top[:, qt, h0 + h:h0 + h + 1])
                    ins.then_inc(S["masked"], 1)
                else:
                    dve.tensor_reduce(top[:, qt, h0:h0 + nh],
                                      sbank[s % 2][:, :].rearrange("p (h k) -> p h k", k=kw), AX.X, ALU.min
                                      ).then_inc(S["masked"], 1)

            def turn_out(i, s):
                dve.wait_ge(S["turned"], i * 2 * U + s + 1 + CREDIT)
                dve.wait_ge(S["values"], total(i, 2 * U, s - R + 1) + CREDIT)
                dve.tensor_copy(pt[s % R][:, :], tbank[s % 2][:, :]).then_inc(S["turned_out0"], 1)

            def recip(i, e):
                qt = e % 2
                dve.wait_ge(S["probs"], i * 2 * U + end_of(e) + 1 + CREDIT)
                dve.wait_ge(S["repeated"], total(i, 4, e - 1) + CREDIT)
                if ghost:
                    dve.tensor_tensor(rden[:, qt, :], den[:, qt, :], weight(core, wk, ghost), ALU.add).then_inc(S["ghosted"], 1)
                    dve.wait_ge(S["ghosted"], 4 * i + e + 1 + CREDIT)
                    dve.reciprocal(rden[:, qt, :], rden[:, qt, :]).then_inc(S["recip"], 1)
                else:
                    dve.reciprocal(rden[:, qt, :], den[:, qt, :]).then_inc(S["recip"], 1)

            def norm(i, e):
                qt = e % 2
                dve.wait_ge(S["values"], i * 2 * U + end_of(e) + 1 + CREDIT)
                dve.wait_ge(S["rep_out"], (4 * i + e + 1) * EW + CREDIT)
                dve.wait_ge(S["projected"], 4 * i + e + CREDIT)
                if hd.two_banks:
                    for r in range(2):
                        ins = dve.tensor_tensor(on[:, 4 * r:4 * r + 4, :].rearrange("p a b -> p (a b)"),
                                                obank[r][:, :], rt[:, 4 * r:4 * r + 4, :].rearrange("p a b -> p (a b)"),
                                                ALU.mult)
                else:
                    ins = dve.tensor_tensor(on[:, :, :].rearrange("p a b -> p (a b)"), obank[qt][:, :],
                                            rt[:, :, :].rearrange("p a b -> p (a b)"), ALU.mult)
                ins.then_inc(S["normed"], 1)

            def residual(i, e):
                t = 4 * i + e
                dve.wait_ge(S["projected"], 4 * i + e + 1 + CREDIT)
                xt = X[:, bass.ds(t, 1), :].rearrange("p t d -> p (t d)")
                epilogue.dve(dve, core, B, S, i, e, xt, EPI[:, 0:DM])

            def tile_stats(i, e):
                t = 4 * i + e
                dve.wait_ge(S["residual"], t + 1 + CREDIT)
                dve.wait_ge(S["moments_kept"], t + CREDIT)
                carry_waits(core, dve)
                dve.bn_stats(B["stat"][:, :], joined(X[:, bass.ds(t, 1), :])).then_inc(S["stats"], 1)

            def tile_aggregate(i, e):
                dve.wait_ge(S["stats"], 4 * i + e + 1 + CREDIT)
                carry_waits(core, dve)
                dve.bn_aggr(B["mv"][:, :], B["stat"][:, :]).then_inc(S["aggregated"], 1)

            def keep_moments(i, e):
                t = 4 * i + e
                dve.wait_ge(S["aggregated"], t + 1 + CREDIT)
                dve.tensor_copy(joined(core.mv[:, bass.ds(t, 1), :]), B["mv"][:, :]).then_inc(S["moments_kept"], 1)

            def step(i, b, j):
                seq = 2 * i + b
                if steps.engine[j] == "dve":
                    dve.wait_ge(S["step_mm"], seq * NS + j + 1 + CREDIT)
                    if steps.kinds[j] == "v":
                        dve.wait_ge(S["v_zero"], 2 + CREDIT)
                        dve.wait_ge(S["values"], total(i, 2 * U, (b - 1) * U) + CREDIT)
                    if steps.kinds[j] == "k" and not steps.roped:
                        dve.wait_ge(S["k_spread"], seq * NK + CREDIT)
                    if steps.roped and steps.kinds[j] in "qk":
                        dve.wait_ge(S["rope_added"], seq * NR + max(steps.rank(j) - 1, 0) + CREDIT)
                    steps.dve(dve, core, B, S, PRE, j, b % 2, seq).then_inc(S["step_out"], 1)

            steps.before(dve, core, B, S)
            for j in range(NS):
                step(0, 0, j)

            def slot(i, s):
                if in_pair(i, s):
                    mask(i, s)
                    b, u = divmod(s, U)
                    for j in at_slot[u]:
                        step(i, b + 1, j)
                for v in lagging(i, s, LT):
                    if v % 2 == 0:
                        turn_out(i, v)
                for e in ending(i, s, 1):
                    recip(i, e)
                if moments:
                    for e in ending(i, s, LE + 5):
                        keep_moments(i, e)
                    for e in ending(i, s, LE + 4):
                        tile_aggregate(i, e)
                    for e in ending(i, s, LE + 3):
                        tile_stats(i, e)
                for e in ending(i, s, LE + 2):
                    residual(i, e)
                for e in ending(i, s, LE + 1):
                    norm(i, e)

            slots_of_pair(dve, slot)

        @block.scalar
        def _(act):
            act.wait_ge(core.weights_in[wk], loaded_count(wk))

            def probs(i, s):
                b, u = divmod(s % (2 * U), U)
                qt, h0, nh = units[u]
                k0, kw = keys[qt]
                act.wait_ge(S["masked"], i * 2 * U + s + 1 + CREDIT)
                act.wait_ge(S["turned"], total(i, 2 * U, s - R + 1) + CREDIT)
                if u in (0, per_qt[0]):
                    e = s // U * 2 + qt
                    act.wait_ge(S["recip"], total(i, 4, e - 1) + CREDIT)
                src = sm[s % R] if masked else sbank[s % 2]
                for h in range(nh):
                    ins = act.activation(pr[s % R][:, h * kw:(h + 1) * kw], src[:, h * kw:(h + 1) * kw], ACT.Exp,
                                         bias=top[:, qt, h0 + h:h0 + h + 1], scale=-1.0,
                                         accum_out=den[:, qt, h0 + h:h0 + h + 1])
                ins.then_inc(S["probs"], 1)

            def turn_out(i, s):
                act.wait_ge(S["turned"], i * 2 * U + s + 1 + CREDIT)
                act.wait_ge(S["values"], total(i, 2 * U, s - R + 1) + CREDIT)
                act.activation(pt[s % R][:, :], tbank[s % 2][:, :], ACT.Copy).then_inc(S["turned_out1"], 1)

            def rep_out(i, e):
                for r in range(EW):
                    act.wait_ge(S["rep_turned"], (4 * i + e) * EW + r + 1 + CREDIT)
                    if r == 0:
                        act.wait_ge(S["normed"], 4 * i + e + CREDIT)
                    act.activation(rt[:, 4 * r:4 * r + 4, :].rearrange("p a b -> p (a b)"), EPI[:, :],
                                   ACT.Copy).then_inc(S["rep_out"], 1)

            def step(i, b, j):
                seq = 2 * i + b
                if steps.engine[j] == "act":
                    act.wait_ge(S["step_mm"], seq * NS + j + 1 + CREDIT)
                    if steps.kinds[j] == "k":
                        act.wait_ge(S["k_spread"], seq * NK + CREDIT)
                    steps.act(act, core, B, S, PRE, j, b % 2, seq).then_inc(S["step_out"], 1)

            for j in range(NS):
                step(0, 0, j)

            def slot(i, s):
                if in_pair(i, s):
                    probs(i, s)
                    b, u = divmod(s, U)
                    for j in at_slot[u]:
                        step(i, b + 1, j)
                for v in lagging(i, s, LT):
                    if v % 2 == 1:
                        turn_out(i, v)
                for e in ending(i, s, LE):
                    rep_out(i, e)

            slots_of_pair(act, slot)

        @block.gpsimd
        def _(pool):
            def copy_x(i, b):
                seq = 2 * i + b
                pool.wait_ge(S["step_mm"], seq * NS + CREDIT)
                carry_waits(core, pool)
                steps.copy_x(pool, core, B, S, seq)
                pool.tensor_copy(B["xs"][:, :], XT[:, bass.ds(seq * SEQ, SEQ)]).then_inc(S["x_copied"], 1)

            def step(i, b, j):
                seq = 2 * i + b
                kind = steps.kinds[j]
                if kind not in "qk":
                    return
                c0, c1 = steps.chunks_of[j]
                if steps.roped:
                    r = steps.rank(j)
                    rows = hd.rows(c0)
                    pool.wait_ge(S["step_out"], seq * NS + j + 1 + CREDIT)
                    dst = (B["q"][b % 2] if kind == "q" else B["k"])[0:rows, c0, :]
                    if kind == "k":
                        pool.wait_ge(S["k_spread"], seq * NK + CREDIT)
                    tt = B["tt"][j % 2]
                    pool.tensor_tensor(dst, tt[0:rows, 0, :], tt[0:rows, 1, :], ALU.add).then_inc(S["rope_added"], 1)
                if kind == "k":
                    if steps.roped:
                        pool.wait_ge(S["rope_added"], seq * NR + r + 1 + CREDIT)
                    else:
                        pool.wait_ge(S["step_out"], seq * NS + j + 1 + CREDIT)
                    for c in range(c0, c1):
                        a, z, rows = c * hd.hpc, min(H, (c + 1) * hd.hpc), hd.rows(c)
                        ins = pool.tensor_tensor(
                            B["kx"][b % 2][0:rows, a:z, :],
                            B["k"][0:rows, c:c + 1, :].to_broadcast([rows, z - a, SEQ]),
                            hmask[0:rows, 0:z - a].unsqueeze(2).to_broadcast([rows, z - a, SEQ]), ALU.mult)
                    ins.then_inc(S["k_spread"], 1)

            def repeat(i, e):
                pool.wait_ge(S["recip"], 4 * i + e + 1 + CREDIT)
                pool.wait_ge(S["rep_turned"], (4 * i + e) * EW + CREDIT)
                carry_waits(core, pool)
                pool.tensor_copy(rx[:, :, :], rden[:, e % 2, :].unsqueeze(2).to_broadcast([P, H, dvp])
                                 ).then_inc(S["repeated"], 1)

            copy_x(0, 0)
            for j in range(NS):
                step(0, 0, j)

            def slot(i, s):
                for e in ending(i, s, 1):
                    repeat(i, e)
                if in_pair(i, s):
                    b, u = divmod(s, U)
                    if u == 0:
                        copy_x(i, b + 1)
                    for j in at_slot[u]:
                        step(i, b + 1, j)

            slots_of_pair(pool, slot)


def total(i, each, k):
    return max(i * each + k, 0) if isinstance(i, int) else i * each + k


def joined(ap):
    return ap.rearrange("p t d -> p (t d)")


class Steps:

    roped = False

    def alloc(self, sb, sem, B, S):
        if self.roped:
            B["tt"] = [sb(f"tt{i}", [P, 2, SEQ]) for i in range(2)]

    def before(self, dve, core, B, S):
        pass

    def copy_x(self, pool, core, B, S, seq):
        pass

    @property
    def count(self):
        return len(self.kinds)

    def rank(self, j):
        return sum(1 for k in self.kinds[:j] if k in "qk")


def value_out(dve, B, PRE, b, dv, H):
    return dve.tensor_copy(B["v"][b][:, :, :, 0:dv], PRE[:, 0:2 * H * dv].rearrange("p (t h d) -> p t h d", t=2, h=H))


class RotarySteps(Steps):

    roped = True

    def __init__(self, stage):
        self.kinds = ["q", "k", "v"]
        self.engine = ["dve"] * 3
        self.chunks_of = [(0, 1), (0, 1), None]
        self.stage = stage

    def pe(self, pe, core, B, S, PRE, j, b, seq):
        w = lambda s: weight(core, self.stage, s)
        if self.kinds[j] in "qk":
            k = self.kinds[j]
            pe.matmul(PRE[:, 0:SEQ], w(f"l1_w{k}"), B["xs"][:, :], start=True, stop=True)
            return pe.matmul(PRE[:, SEQ:2 * SEQ], w(f"l1_w{k}rot"), B["xs"][:, :], start=True, stop=True)
        for t in range(2):
            mm = pe.matmul(PRE[:, t * P:(t + 1) * P], B["xs"][:, t * P:(t + 1) * P], w("l1_wv"), start=True, stop=True)
        return mm

    def dve(self, dve, core, B, S, PRE, j, b, seq):
        if self.kinds[j] in "qk":
            table = core.const("rope8" + self.kinds[j])
            return dve.tensor_tensor(B["tt"][j % 2][:, :, :].rearrange("p a b -> p (a b)"), PRE[:, :], table, ALU.mult)
        return value_out(dve, B, PRE, b, 8, 16)


class Epilogue:

    def __init__(self, wo):
        self.wo = wo

    def alloc(self, sb, B):
        pass

    def dve(self, dve, core, B, S, i, e, xt, y):
        dve.tensor_tensor(xt, y, xt, ALU.add).then_inc(S["residual"], 1)


def bias_setup_stage(core, ctx, bias):
    nc = core.nc
    credited = []
    sem = lambda s: new_sem(core, ctx, f"bias_{s}", credited)
    rows_mm, rows_out, rows_stored, bias_in = sem("rows_mm"), sem("rows_out"), sem("rows_stored"), sem("loaded")
    flip_mm, flip_out = sem("flip_mm"), sem("flip_out")
    scratch = nc.dram_tensor("bias_rows", (16, 383), F32, kind="Internal").ap()
    with ExitStack() as mem:
        mem.callback(retire, core, credited)
        rows = mem.enter_context(nc.sbuf_tensor("bias_rows_sb", [16, 383], F32))
        block = mem.enter_context(nc.Block())

        @block.tensor
        def _(pe):
            pe.wait_ge(core.weights_in[2], loaded_count(2))
            pe.matmul(core.bank[2][0:16, 0:383], weight(core, 2, "l1_rel"), core.const("bucket", 32),
                      start=True, stop=True).then_inc(rows_mm, 1)
            pe.wait_ge(bias_in, 16 + CREDIT)
            for g in range(8):
                if g >= 2:
                    pe.wait_ge(flip_out, g - 1 + CREDIT)
                pe.matmul(core.bank[g % 2][:, :], core.const("flip"), bias[:, 2 * g:2 * g + 2, :],
                          start=True, stop=True).then_inc(flip_mm, 1)

        @block.vector
        def _(dve):
            dve.wait_ge(rows_mm, 1 + CREDIT)
            dve.scalar_tensor_tensor(rows[:, :], core.bank[2][0:16, 0:383], -1.0, core.const("future", 16),
                                     ALU.mult, ALU.add).then_inc(rows_out, 1)

        @block.sync
        def _(sp):
            give_credit(sp, credited)
            sp.wait_ge(rows_out, 1 + CREDIT)
            sp.dma_start(scratch, rows[:, :]).then_inc(rows_stored, 16)
            sp.wait_ge(rows_stored, 16 + CREDIT)
            window = bass.AP(scratch.tensor, 0, [[1, P], [383, 16], [1, SEQ]])
            sp.dma_start(bias, window).then_inc(bias_in, 16)

        @block.scalar
        def _(act):
            for g in range(8):
                act.wait_ge(flip_mm, g + 1 + CREDIT)
                act.activation(bias[:, 2 * g:2 * g + 2, :].rearrange("p h c -> p (h c)"), core.bank[g % 2][:, :],
                               ACT.Copy).then_inc(flip_out, 1)


def l1_attention(core, ctx, next_weights=()):
    hd = Heads(16, 8, 8, [(0, P), (0, SEQ)], causal=True)
    attention_stage(core, ctx, 2, hd, RotarySteps(2), Epilogue(weight(core, 2, "l1_wo")),
                    next_weights=next_weights, head_bias=True)


class PlainSteps(Steps):

    def __init__(self, stage, names, width, vwidth, dv, scale, biases=None, value_scale=None):
        self.stage, self.names, self.scale, self.biases = stage, names, scale, biases
        n = width // P // 2
        nv = 1 if 2 * vwidth <= BANK else 2 * vwidth // BANK
        self.nv, self.dv, self.vwidth, self.value_scale = nv, dv, vwidth, value_scale
        self.kinds = ["q"] * n + ["k"] * n + ["v"] * nv
        self.engine = ["act"] * n + ["act"] * n + ["dve"] * nv
        self.chunks_of = [(2 * j, 2 * j + 2) for j in range(n)] * 2 + [None] * nv

    def alloc(self, sb, sem, B, S):
        if self.biases:
            B["nbq"] = sb("nbq", [P, 8])
            S["bias_scaled"] = sem("bias_scaled")

    def before(self, dve, core, B, S):
        if self.biases:
            dve.tensor_scalar(B["nbq"][:, :], weight(core, self.stage, self.biases[0]), self.scale, None,
                              ALU.mult).then_inc(S["bias_scaled"], 1)

    def pe(self, pe, core, B, S, PRE, j, b, seq):
        kind = self.kinds[j]
        w = weight(core, self.stage, self.names["qkv".index(kind)])
        if kind in "qk":
            c0, c1 = self.chunks_of[j]
            for c in (c0, c0 + 1):
                mm = pe.matmul(PRE[:, (c - c0) * SEQ:(c - c0 + 1) * SEQ], w[:, c * P:(c + 1) * P], B["xs"][:, :],
                               start=True, stop=True)
            return mm
        r = j - self.kinds.index("v")
        if self.nv == 1:
            for t in range(2):
                mm = pe.matmul(PRE[:, t * self.vwidth:(t + 1) * self.vwidth], B["xs"][:, t * P:(t + 1) * P],
                               w, start=True, stop=True)
            return mm
        per = self.nv // 2
        t, part = divmod(r, per)
        return pe.matmul(PRE[:, :], B["xs"][:, t * P:(t + 1) * P], w[:, part * BANK:(part + 1) * BANK],
                         start=True, stop=True)

    def act(self, act, core, B, S, PRE, j, b, seq):
        c0, c1 = self.chunks_of[j]
        q = self.kinds[j] == "q"
        dst = B["q"][b] if q else B["k"]
        if not self.biases:
            return act.activation(dst[:, c0:c1, :].rearrange("p c t -> p (c t)"), PRE[:, :], ACT.Copy,
                                  scale=self.scale if q else 1.0)
        act.wait_ge(S["bias_scaled"], 1 + CREDIT)
        for c in range(c0, c1):
            bias = B["nbq"][:, c:c + 1] if q else weight(core, self.stage, self.biases[1])[:, c:c + 1]
            ins = act.activation(dst[:, c, :], PRE[:, (c - c0) * SEQ:(c - c0 + 1) * SEQ], ACT.Identity,
                                 bias=bias, scale=self.scale if q else 1.0)
        return ins

    def dve(self, dve, core, B, S, PRE, j, b, seq):
        H = self.vwidth // self.dv
        if self.nv == 1:
            return value_out(dve, B, PRE, b, self.dv, H)
        r = j - self.kinds.index("v")
        per = self.nv // 2
        t, part = divmod(r, per)
        h0, h1 = part * BANK // self.dv, (part + 1) * BANK // self.dv
        dst = B["v"][b][:, t, h0:h1, :].rearrange("p h d -> p (h d)")
        if self.biases:
            bv = weight(core, self.stage, self.biases[2])[:, part * BANK:(part + 1) * BANK]
            return dve.tensor_tensor(dst, PRE[:, :], bv, ALU.add)
        if self.value_scale is not None:
            return dve.tensor_scalar(dst, PRE[:, :], self.value_scale[:, bass.ds(seq, 1), t], None, ALU.mult)
        return dve.tensor_copy(dst, PRE[:, :])


def l2_attention(core, ctx, next_weights=()):
    hd = Heads(16, 16, 16, [(0, P), (0, SEQ)], causal=True)
    steps = PlainSteps(4, ("l2_wq", "l2_wk", "l2_wv"), 256, 256, 16, -1.0 / math.sqrt(8.0))
    attention_stage(core, ctx, 4, hd, steps, Epilogue(weight(core, 4, "l2_wo")), next_weights=next_weights)


class BiasedEpilogue(Epilogue):

    def __init__(self, wo, bo):
        self.wo, self.bo = wo, bo

    def alloc(self, sb, B):
        B["yb"] = sb("yb", [P, DM])

    def dve(self, dve, core, B, S, i, e, xt, y):
        dve.tensor_tensor(B["yb"][:, :], y, self.bo, ALU.add).then_inc(S["epilogue"], 1)
        dve.wait_ge(S["epilogue"], 4 * i + e + 1 + CREDIT)
        dve.tensor_tensor(xt, B["yb"][:, :], xt, ALU.add).then_inc(S["residual"], 1)


def l3_attention(core, ctx, next_weights=()):
    hd = Heads(16, 64, 64, [(0, P), (0, SEQ)], causal=True)
    steps = PlainSteps(6, ("l3_wq", "l3_wk", "l3_wv"), 1024, 1024, 64, -1.0 / 8.0, biases=("l3_bq", "l3_bk", "l3_bv"))
    attention_stage(core, ctx, 6, hd, steps, BiasedEpilogue(weight(core, 6, "l3_wo"), weight(core, 6, "l3_bo")),
                    next_weights=next_weights, ghost="l3_ghost")


class LatentSteps(Steps):

    roped = True

    def __init__(self, rkv, KV):
        self.kinds = ["pre"] + ["q"] * 6 + ["k"] * 6 + ["v"]
        self.engine = ["act"] + ["dve"] * 13
        self.chunks_of = [None] + [(c, c + 1) for c in range(6)] * 2 + [None]
        self.rkv, self.KV = rkv, KV

    def alloc(self, sb, sem, B, S):
        Steps.alloc(self, sb, sem, B, S)
        B["kvs"] = sb("kvs", [P, 2, 32])
        B["kvT"] = sb("kvT", [32, SEQ])
        B["qcT"] = sb("qcT", [64, SEQ])
        S["kv_scaled"] = sem("kv_scaled")

    def copy_x(self, pool, core, B, S, seq):
        pool.tensor_tensor(B["kvs"][:, :, :], self.KV[:, bass.ds(seq * 2, 2), :],
                           self.rkv[:, bass.ds(seq * 2, 2)].unsqueeze(2).to_broadcast([P, 2, 32]),
                           ALU.mult).then_inc(S["kv_scaled"], 1)

    def pe(self, pe, core, B, S, PRE, j, b, seq):
        w = lambda s: weight(core, 0, s)
        kind = self.kinds[j]
        if kind == "pre":
            pe.wait_ge(S["kv_scaled"], seq + 1 + CREDIT)
            for t in range(2):
                pe.transpose(PRE[0:32, t * P:(t + 1) * P], B["kvs"][:, t, :], core.const("ident"))
            return pe.matmul(PRE[0:64, SEQ:2 * SEQ], w("l0_wq"), B["xs"][:, :], start=True, stop=True)
        if kind == "v":
            for t in range(2):
                mm = pe.matmul(PRE[:, t * P:(t + 1) * P], B["kvT"][:, t * P:(t + 1) * P], w("l0_wvdec"),
                               start=True, stop=True)
            return mm
        c = self.chunks_of[j][0]
        a, z = c * 120, min(640, (c + 1) * 120)
        m = z - a
        if kind == "q":
            if m <= 64:
                carry_waits(core, pe)
            pe.matmul(PRE[0:m, 0:SEQ], w("l0_wqall")[:, a:z], B["qcT"][:, :], start=True, stop=True)
            return pe.matmul(PRE[0:m, SEQ:2 * SEQ], w("l0_wqrot")[:, a:z], B["qcT"][:, :], start=True, stop=True)
        pe.matmul(PRE[0:m, 0:SEQ], w("l0_wkdec")[:, a:z], B["kvT"][:, :], start=True, stop=False)
        pe.matmul(PRE[0:m, 0:SEQ], w("l0_wkrope")[:, a:z], B["xs"][:, :], start=False, stop=True)
        return pe.matmul(PRE[0:m, SEQ:2 * SEQ], w("l0_wkrot")[:, a:z], B["xs"][:, :], start=True, stop=True)

    def act(self, act, core, B, S, PRE, j, b, seq):
        act.activation(B["kvT"][:, :], PRE[0:32, 0:SEQ], ACT.Copy, scale=weight(core, 0, "l0_gkv"))
        return act.activation(B["qcT"][:, :], PRE[0:64, SEQ:2 * SEQ], ACT.Copy)

    def dve(self, dve, core, B, S, PRE, j, b, seq):
        if self.kinds[j] == "v":
            return value_out(dve, B, PRE, b, 8, 16)
        c = self.chunks_of[j][0]
        m = min(640, (c + 1) * 120) - c * 120
        table = core.const("rope40" + self.kinds[j], m)
        return dve.tensor_tensor(B["tt"][j % 2][0:m, :, :].rearrange("p a b -> p (a b)"), PRE[0:m, :], table, ALU.mult)


def latent_stage(core, ctx, KV, rkv):
    nc = core.nc
    credited = []
    sem = lambda s: new_sem(core, ctx, f"kv_{s}", credited)
    x_copied, kv_mm, kv_out, squared, mean_ready, std_ready, rkv_ready, pad_zero = (
        sem("x_copied"), sem("mm"), sem("out"), sem("squared"), sem("mean"), sem("std"), sem("rkv"), sem("pad_zero"))
    with ExitStack() as mem:
        mem.callback(retire, core, credited)
        xs = [mem.enter_context(nc.sbuf_tensor(f"kv_xs{i}", [P, SEQ], F32)) for i in range(2)]
        sq = mem.enter_context(nc.sbuf_tensor("kv_sq", [P, 2, 32], F32))
        std = mem.enter_context(nc.sbuf_tensor("kv_std", [P, TILES], F32))
        block = mem.enter_context(nc.Block())

        @block.sync
        def _(sp):
            give_credit(sp, credited)

        @block.gpsimd
        def _(pool):
            pool.memset(KV[:, TILES:TILES + 2, :], 0.0).then_inc(pad_zero, 1)
            pool.memset(rkv[:, TILES:TILES + 2], 0.0).then_inc(pad_zero, 1)
            with pool.Fori(0, BATCH // 2) as i:
                for b in range(2):
                    pool.wait_ge(kv_mm, 2 * i + CREDIT)
                    carry_waits(core, pool)
                    pool.tensor_copy(xs[b][:, :], core.XT[:, bass.ds((2 * i + b) * SEQ, SEQ)]).then_inc(x_copied, 1)

        @block.tensor
        def _(pe):
            pe.wait_ge(core.weights_in[0], loaded_count(0))
            with pe.Fori(0, BATCH // 2) as i:
                for b in range(2):
                    pe.wait_ge(x_copied, 2 * i + b + 1 + CREDIT)
                    pe.wait_ge(kv_out, 2 * i + CREDIT)
                    for t in range(2):
                        mm = pe.matmul(core.bank[b][:, t * 32:(t + 1) * 32], xs[b][:, t * P:(t + 1) * P],
                                       weight(core, 0, "l0_wkv"), start=True, stop=True)
                    mm.then_inc(kv_mm, 1)

        @block.vector
        def _(dve):
            with dve.Fori(0, BATCH // 2) as i:
                for b in range(2):
                    s = 2 * i + b
                    dve.wait_ge(kv_mm, s + 1 + CREDIT)
                    dst = KV[:, bass.ds(2 * s, 2), :]
                    dve.tensor_copy(dst, core.bank[b][:, 0:64].rearrange("p (t r) -> p t r", t=2)).then_inc(kv_out, 1)
                    dve.wait_ge(kv_out, s + 1 + CREDIT)
                    dve.wait_ge(squared, s + CREDIT)
                    dve.tensor_tensor(sq[:, :, :], dst, dst, ALU.mult).then_inc(mean_ready, 1)
                    dve.wait_ge(mean_ready, s + 1 + CREDIT)
                    dve.tensor_reduce(rkv[:, bass.ds(2 * s, 2)], sq[:, :, :], AX.X, ALU.add).then_inc(squared, 1)
            dve.wait_ge(squared, BATCH + CREDIT)
            dve.tensor_scalar(rkv[:, 0:TILES], rkv[:, 0:TILES], 1.0 / 32, 1e-6, ALU.mult, ALU.add).then_inc(mean_ready, 1)
            dve.wait_ge(std_ready, 1 + CREDIT)
            dve.reciprocal(rkv[:, 0:TILES], std[:, :]).then_inc(rkv_ready, 1)

        @block.scalar
        def _(act):
            act.wait_ge(mean_ready, BATCH + 1 + CREDIT)
            act.activation(std[:, :], rkv[:, 0:TILES], ACT.Sqrt).then_inc(std_ready, 1)


def l0_attention(core, ctx, next_weights=()):
    with ExitStack() as mem:
        KV = mem.enter_context(core.nc.sbuf_tensor("KV", [P, TILES + 2, 32], F32))
        rkv = mem.enter_context(core.nc.sbuf_tensor("rkv", [P, TILES + 2], F32))
        latent_stage(core, ctx, KV, rkv)
        hd = Heads(16, 40, 8, [(0, P), (0, SEQ)], causal=True)
        attention_stage(core, ctx, 0, hd, LatentSteps(rkv, KV), Epilogue(weight(core, 0, "l0_wo")),
                        next_weights=next_weights)


def over(ap, shape, axis):
    return ap.unsqueeze(axis).to_broadcast(shape)


def gate_stage(core, ctx, n, w, m, dve_part, act_part, outs, setup=None):
    nc = core.nc
    credited = []
    sem = lambda s: new_sem(core, ctx, f"g{n}_{s}", credited)
    logits_mm, logits_out, logits_turned, dve_done, act_done, ready, turned, turned_out, extra = [
        sem(s) for s in ("logits_mm", "logits_out", "logits_turned", "dve_done", "act_done", "ready", "turned",
                         "turned_out", "extra")]
    GR = TOK // BANK
    with ExitStack() as mem:
        mem.callback(retire, core, credited)
        LT = mem.enter_context(nc.sbuf_tensor(f"g{n}_LT", [m, TOK], F32))
        sb = lambda s, shape, dt=F32: mem.enter_context(nc.sbuf_tensor(f"g{n}_{s}", shape, dt))
        B = {"logits": core.bank[0][:, 0:TILES * m].rearrange("p (t e) -> p t e", e=m), "sb": sb}
        if setup:
            setup(B)
        ident = core.const("ident")
        block = mem.enter_context(nc.Block())

        @block.sync
        def _(sp):
            give_credit(sp, credited)

        @block.tensor
        def _(pe):
            pe.wait_ge(core.weights_in[n], loaded_count(n))
            pe.wait_ge(credited[-1], CREDIT)
            for g in range(GR):
                pe.matmul(core.bank[g][0:m, :], w, core.XT[:, g * BANK:(g + 1) * BANK],
                          start=True, stop=True).then_inc(logits_mm, 1)
            pe.wait_ge(logits_out, GR + CREDIT)
            for t in range(TILES):
                mm = pe.transpose(core.bank[0][:, t * m:(t + 1) * m], LT[:, t * P:(t + 1) * P], ident[0:m, 0:m])
            mm.then_inc(logits_turned, 1)
            if "pe" in B:
                B["pe"](pe, extra)
            for j, (nat, dst) in enumerate(outs):
                r = nat.shape[2]
                pe.wait_ge(ready, j + 1 + CREDIT)
                for g in range(GR):
                    if j:
                        pe.wait_ge(turned_out, (j - 1) * GR + g + 1 + CREDIT)
                    for t in range(4):
                        mm = pe.transpose(core.bank[g][0:r, t * P:(t + 1) * P], nat[:, g * 4 + t, :], ident)
                    mm.then_inc(turned, 1)

        @block.vector
        def _(dve):
            dve.wait_ge(core.weights_in[n], loaded_count(n))
            dve.wait_ge(logits_turned, 1 + CREDIT)
            dve_done_so_far = counter(CREDIT)
            dve_part(dve, core, B, dve_done, dve_done_so_far, act_done, ready, extra)

        @block.scalar
        def _(act):
            for g in range(GR):
                act.wait_ge(logits_mm, g + 1 + CREDIT)
                act.activation(LT[:, g * BANK:(g + 1) * BANK], core.bank[g][0:m, :], ACT.Copy).then_inc(logits_out, 1)
            act_part(act, core, B, dve_done, act_done)
            for j, (nat, dst) in enumerate(outs):
                r = nat.shape[2]
                for g in range(GR):
                    act.wait_ge(turned, j * GR + g + 1 + CREDIT)
                    act.activation(dst[:, g * BANK:(g + 1) * BANK], core.bank[g][0:r, :], ACT.Copy
                                   ).then_inc(turned_out, 1)


def top_entries(dve, B, dve_done, dve_done_so_far, scores, TE):
    for t in range(TILES):
        ins = dve.max(B["vals"][:, t, :], scores[:, t, :])
    ins.then_inc(dve_done, 1)
    dve.wait_ge(dve_done, dve_done_so_far())
    for t in range(TILES):
        ins = dve.max_index(B["idx"][:, t, :], B["vals"][:, t, :], scores[:, t, :])
    ins.then_inc(dve_done, 1)
    dve.wait_ge(dve_done, dve_done_so_far())
    dve.tensor_copy(B["idxf"][:, :, :], B["idx"][:, :, :]).then_inc(dve_done, 1)
    dve.wait_ge(dve_done, dve_done_so_far())


def tile_moments(dve, core, B, xt, t, count, sems):
    stats, aggregated, kept = sems
    dve.wait_ge(kept, count + CREDIT)
    carry_waits(core, dve)
    dve.bn_stats(B["stat"][:, :], xt).then_inc(stats, 1)
    dve.wait_ge(stats, count + 1 + CREDIT)
    carry_waits(core, dve)
    dve.bn_aggr(B["mv"][:, :], B["stat"][:, :]).then_inc(aggregated, 1)
    dve.wait_ge(aggregated, count + 1 + CREDIT)
    dve.tensor_copy(joined(core.mv[:, bass.ds(t, 1), :]), B["mv"][:, :]).then_inc(kept, 1)


SH = [P, TILES, 8]


def l0_gates(core, ctx, gates, gatesT):
    def setup(B):
        for s in ("lg", "vals", "idxf", "one", "two"):
            B[s] = B["sb"](s, SH)
        B["idx"] = B["sb"]("idx", SH, U32)
        for s in ("d", "e", "den", "p1", "p2"):
            B[s] = B["sb"](s, [P, TILES])

    def dve_part(dve, core, B, dve_done, dve_done_so_far, act_done, ready, extra):
        iota = core.const("iota8")
        rb = weight(core, 1, "l0_rb")
        dve.tensor_tensor(B["lg"][:, :, :], B["logits"], over(rb, SH, 1), ALU.add).then_inc(dve_done, 1)
        dve.wait_ge(dve_done, dve_done_so_far())
        top_entries(dve, B, dve_done, dve_done_so_far, B["lg"], 8)
        dve.tensor_tensor(B["d"][:, :], B["vals"][:, :, 1], B["vals"][:, :, 0], ALU.subtract).then_inc(dve_done, 1)
        dve.wait_ge(dve_done, dve_done_so_far())
        dve.tensor_tensor(B["one"][:, :, :], over(iota, SH, 1), over(B["idxf"][:, :, 0], SH, 2), ALU.is_equal).then_inc(dve_done, 1)
        dve.wait_ge(dve_done, dve_done_so_far())
        dve.tensor_tensor(B["two"][:, :, :], over(iota, SH, 1), over(B["idxf"][:, :, 1], SH, 2), ALU.is_equal).then_inc(dve_done, 1)
        dve.wait_ge(dve_done, dve_done_so_far())
        dve.wait_ge(act_done, 1 + CREDIT)
        dve.tensor_scalar(B["den"][:, :], B["e"][:, :], 1.0, None, ALU.add).then_inc(dve_done, 1)
        dve.wait_ge(dve_done, dve_done_so_far())
        dve.reciprocal(B["p1"][:, :], B["den"][:, :]).then_inc(dve_done, 1)
        dve.wait_ge(dve_done, dve_done_so_far())
        dve.tensor_tensor(B["p2"][:, :], B["e"][:, :], B["p1"][:, :], ALU.mult).then_inc(dve_done, 1)
        dve.wait_ge(dve_done, dve_done_so_far())
        dve.tensor_tensor(B["one"][:, :, :], B["one"][:, :, :], over(B["p1"][:, :], SH, 2), ALU.mult).then_inc(dve_done, 1)
        dve.wait_ge(dve_done, dve_done_so_far())
        dve.tensor_tensor(B["two"][:, :, :], B["two"][:, :, :], over(B["p2"][:, :], SH, 2), ALU.mult).then_inc(dve_done, 1)
        dve.wait_ge(dve_done, dve_done_so_far())
        dve.tensor_tensor(gates[:, :, :], B["one"][:, :, :], B["two"][:, :, :], ALU.add).then_inc(ready, 1)

    def act_part(act, core, B, dve_done, act_done):
        act.wait_ge(dve_done, 5 + CREDIT)
        act.activation(B["e"][:, :], B["d"][:, :], ACT.Exp).then_inc(act_done, 1)

    gate_stage(core, ctx, 1, weight(core, 1, "l0_rw"), 8, dve_part, act_part, [(gates, gatesT)], setup)


def l0_ffn(core, ctx, next_weights=()):
    nc, X, XT = core.nc, core.X, core.XT
    credited = []
    sem = lambda s: new_sem(core, ctx, f"f0_{s}", credited)
    with ExitStack() as mem:
        mem.callback(retire, core, credited)
        sb = lambda s, shape, dt=F32: mem.enter_context(nc.sbuf_tensor(f"f0_{s}", shape, dt))
        gates, gatesT = sb("gates", SH), sb("gatesT", [8, TOK])
        l0_gates(core, ctx, gates, gatesT)
        act_sb = [sb(f"act{i}", [P, BANK]) for i in range(2)]
        prod = [sb(f"prod{i}", [P, BANK]) for i in range(2)]
        hid = [sb(f"hid{i}", [P, 5, BANK]) for i in range(2)]
        B = {"stat": sb("stat", [P, 6]), "mv": sb("mv", [P, 2])}
        up, silu_out, product, hidden, down, residual, stats, aggregated, kept = [
            sem(s) for s in ("up", "silu_out", "product", "hidden", "down", "residual", "stats", "aggregated", "kept")]
        w = lambda s: weight(core, 1, s)
        ident = core.const("ident")
        gate_rows = core.const("gaterows", 8)
        PAIRS = 5
        bank = core.bank
        block = mem.enter_context(nc.Block())

        @block.sync
        def _(sp):
            give_credit(sp, credited)
            for k in next_weights:
                load_weights(core, sp, k)

        @block.tensor
        def _(pe):
            def ups(i, g):
                for p in range(PAIRS):
                    u = g * PAIRS + p
                    pe.wait_ge(hidden, i * 10 + max(u - 1, 0) + CREDIT)
                    carry_waits(core, pe)
                    b = bank[3 * (u % 2):3 * (u % 2) + 3]
                    x = XT[:, bass.ds((2 * i + g) * BANK, BANK)]
                    pe.matmul(b[0][:, :], w("l0_w1")[:, p * P:(p + 1) * P], x, start=True, stop=True)
                    mm = pe.matmul(b[1][:, :], w("l0_w3")[:, p * P:(p + 1) * P], x, start=True, stop=True)
                    if p < 4:
                        mm = pe.matmul(b[2][:, :], gate_rows[:, p * P:(p + 1) * P],
                                       gatesT[:, bass.ds((2 * i + g) * BANK, BANK)], start=True, stop=True)
                    mm.then_inc(up, 1)

            def downs(i, g):
                pe.wait_ge(hidden, i * 10 + (g + 1) * PAIRS + CREDIT)
                pe.wait_ge(residual, 2 * i + CREDIT)
                for t in range(4):
                    for p in range(PAIRS):
                        mm = pe.matmul(bank[6 + g][:, t * P:(t + 1) * P], hid[g][:, p, t * P:(t + 1) * P],
                                       w("l0_w2")[:, p * P:(p + 1) * P], start=(p == 0), stop=(p == PAIRS - 1))
                mm.then_inc(down, 1)

            with pe.Fori(0, 4) as i:
                ups(i, 0)
                ups(i, 1)
                downs(i, 0)
                downs(i, 1)

        @block.scalar
        def _(act):
            with act.Fori(0, 4) as i:
                for u in range(2 * PAIRS):
                    act.wait_ge(up, i * 10 + u + 1 + CREDIT)
                    act.wait_ge(hidden, i * 10 + max(u - 1, 0) + CREDIT)
                    act.activation(act_sb[u % 2][:, :], bank[3 * (u % 2)][:, :], ACT.Silu).then_inc(silu_out, 1)

        @block.vector
        def _(dve):
            with dve.Fori(0, 4) as i:
                for g in range(2):
                    for p in range(PAIRS):
                        u = g * PAIRS + p
                        b = bank[3 * (u % 2):3 * (u % 2) + 3]
                        dve.wait_ge(silu_out, i * 10 + u + 1 + CREDIT)
                        dst = prod[u % 2][:, :] if p < 4 else hid[g][:, p, :]
                        if p == 0 or p == 4:
                            dve.wait_ge(down, 2 * i + CREDIT)
                        dve.tensor_tensor(dst, act_sb[u % 2][:, :], b[1][:, :], ALU.mult
                                          ).then_inc(product if p < 4 else hidden, 1)
                        if p < 4:
                            dve.wait_ge(product, i * 8 + g * 4 + p + 1 + CREDIT)
                            dve.tensor_tensor(hid[g][:, p, :], dst, b[2][:, :], ALU.mult).then_inc(hidden, 1)
                for g in range(2):
                    dve.wait_ge(down, 2 * i + g + 1 + CREDIT)
                    xg = X[:, bass.ds((2 * i + g) * 4, 4), :]
                    dve.tensor_tensor(xg, bank[6 + g][:, :].rearrange("p (t d) -> p t d", t=4), xg, ALU.add
                                      ).then_inc(residual, 1)
                    dve.wait_ge(residual, 2 * i + g + 1 + CREDIT)
                    for t in range(4):
                        tt = (2 * i + g) * 4 + t
                        tile_moments(dve, core, B, joined(X[:, bass.ds(tt, 1), :]), tt, (2 * i + g) * 4 + t,
                                     (stats, aggregated, kept))


def l1_gates(core, ctx, win, winT, gate, gateT):
    def setup(B):
        for s in ("lg", "ex", "sc", "vals", "idxf", "pos"):
            B[s] = B["sb"](s, SH)
        B["idx"] = B["sb"]("idx", SH, U32)
        for s in ("m", "sum", "r", "w"):
            B[s] = B["sb"](s, [P, TILES])

    def dve_part(dve, core, B, dve_done, dve_done_so_far, act_done, ready, extra):
        iota = core.const("iota8")
        dve.tensor_tensor(B["lg"][:, :, :], B["logits"], over(weight(core, 3, "l1_gb"), SH, 1), ALU.add).then_inc(dve_done, 1)
        dve.wait_ge(dve_done, dve_done_so_far())
        dve.tensor_reduce(B["m"][:, :], B["lg"][:, :, :], AX.X, ALU.max).then_inc(dve_done, 1)
        dve.wait_ge(dve_done, dve_done_so_far())
        dve.tensor_tensor(B["lg"][:, :, :], B["lg"][:, :, :], over(B["m"][:, :], SH, 2), ALU.subtract).then_inc(dve_done, 1)
        dve.wait_ge(dve_done, dve_done_so_far())
        dve.wait_ge(act_done, 1 + CREDIT)
        dve.tensor_reduce(B["sum"][:, :], B["ex"][:, :, :], AX.X, ALU.add).then_inc(dve_done, 1)
        dve.wait_ge(dve_done, dve_done_so_far())
        dve.reciprocal(B["r"][:, :], B["sum"][:, :]).then_inc(dve_done, 1)
        dve.wait_ge(dve_done, dve_done_so_far())
        dve.tensor_tensor(B["sc"][:, :, :], B["ex"][:, :, :], over(B["r"][:, :], SH, 2), ALU.mult).then_inc(dve_done, 1)
        dve.wait_ge(dve_done, dve_done_so_far())
        top_entries(dve, B, dve_done, dve_done_so_far, B["sc"], 8)
        dve.tensor_scalar(B["pos"][:, :, :], B["vals"][:, :, :], 0.0, None, ALU.is_gt).then_inc(dve_done, 1)
        dve.wait_ge(dve_done, dve_done_so_far())
        dve.tensor_scalar(B["idxf"][:, :, :], B["idxf"][:, :, :], 1.0, None, ALU.add).then_inc(dve_done, 1)
        dve.wait_ge(dve_done, dve_done_so_far())
        dve.tensor_tensor(B["idxf"][:, :, :], B["idxf"][:, :, :], B["pos"][:, :, :], ALU.mult).then_inc(dve_done, 1)
        dve.wait_ge(dve_done, dve_done_so_far())
        dve.tensor_tensor(B["w"][:, :], B["idxf"][:, :, 0], B["idxf"][:, :, 1], ALU.max).then_inc(dve_done, 1)
        dve.wait_ge(dve_done, dve_done_so_far())
        dve.tensor_scalar(B["w"][:, :], B["w"][:, :], -1.0, None, ALU.add).then_inc(dve_done, 1)
        dve.wait_ge(dve_done, dve_done_so_far())
        dve.tensor_tensor(win[:, :, :], over(iota, SH, 1), over(B["w"][:, :], SH, 2), ALU.is_equal).then_inc(dve_done, 1)
        dve.wait_ge(dve_done, dve_done_so_far())
        dve.tensor_tensor(gate[:, :, :], win[:, :, :], B["sc"][:, :, :], ALU.mult).then_inc(ready, 2)

    def act_part(act, core, B, dve_done, act_done):
        act.wait_ge(dve_done, 3 + CREDIT)
        act.activation(B["ex"][:, :, :], B["lg"][:, :, :], ACT.Exp).then_inc(act_done, 1)

    gate_stage(core, ctx, 3, weight(core, 3, "l1_gw"), 8, dve_part, act_part, [(win, winT), (gate, gateT)], setup)


def l1_ffn(core, ctx, next_weights=()):
    nc, X, XT = core.nc, core.X, core.XT
    credited = []
    sem = lambda s: new_sem(core, ctx, f"f1_{s}", credited)
    with ExitStack() as mem:
        mem.callback(retire, core, credited)
        sb = lambda s, shape, dt=F32: mem.enter_context(nc.sbuf_tensor(f"f1_{s}", shape, dt))
        win, winT, gate, gateT = sb("win", SH), sb("winT", [8, TOK]), sb("gate", SH), sb("gateT", [8, TOK])
        l1_gates(core, ctx, win, winT, gate, gateT)
        winS = [sb(f"winS{i}", [8, BANK]) for i in range(2)]
        xg = [sb(f"xg{i}", [P, 8, BANK]) for i in range(2)]
        hid = [sb(f"hid{i}", [P, 4, BANK]) for i in range(2)]
        won = [sb(f"won{i}", [P, 8, P]) for i in range(2)]
        ysum = sb("ysum", [P, P])
        B = {"stat": sb("stat", [P, 6]), "mv": sb("mv", [P, 2])}
        names = ("win_copied", "gate_mm", "gated", "up", "hidden", "down", "picked", "summed", "biased",
                 "residual", "stats", "aggregated", "kept", "bias_mm")
        (win_copied, gate_mm, gated, up, hidden, down, picked, summed, biased, residual, stats, aggregated, kept,
         bias_mm) = [sem(s) for s in names]
        w = lambda s: weight(core, 3, s)
        ident = core.const("ident")
        bank = core.bank
        GB, HB, YB, BB = bank[0:2], bank[2:4], bank[4:8], None
        block = mem.enter_context(nc.Block())

        @block.sync
        def _(sp):
            give_credit(sp, credited)
            for k in next_weights:
                load_weights(core, sp, k)

        @block.gpsimd
        def _(pool):
            with pool.Fori(0, 4) as i:
                for g in range(2):
                    pool.wait_ge(bias_mm, i * 8 + CREDIT)
                    carry_waits(core, pool)
                    pool.tensor_copy(winS[g][:, :], winT[:, bass.ds((2 * i + g) * BANK, BANK)]
                                     ).then_inc(win_copied, 1)

        @block.tensor
        def _(pe):
            def gates_of(i, g):
                pe.wait_ge(biased, (2 * i + g) * 4 + CREDIT)
                for e in range(8):
                    pe.wait_ge(gated, (2 * i + g) * 8 + max(e - 1, 0) + CREDIT)
                    carry_waits(core, pe)
                    pe.matmul(GB[e % 2][:, :], ident[0:8, e:e + 1].to_broadcast([8, P]),
                              gateT[:, bass.ds((2 * i + g) * BANK, BANK)], start=True, stop=True).then_inc(gate_mm, 1)

            def ups(i, g):
                pe.wait_ge(gated, (2 * i + g + 1) * 8 + CREDIT)
                pe.wait_ge(win_copied, 2 * i + g + 1 + CREDIT)
                for c in range(4):
                    pe.wait_ge(hidden, (2 * i + g) * 4 + max(c - 1, 0) + CREDIT)
                    for e in range(8):
                        pe.matmul(HB[c % 2][:, :], w("l1_w1")[:, (e * 4 + c) * P:(e * 4 + c + 1) * P], xg[g][:, e, :],
                                  start=(e == 0), stop=False)
                    pe.matmul(HB[c % 2][:, :], w("l1_b1")[:, c * P:(c + 1) * P], winS[g][:, :],
                              start=False, stop=True).then_inc(up, 1)

            def downs(i, g):
                pe.wait_ge(hidden, (2 * i + g + 1) * 4 + CREDIT)
                for t in range(4):
                    n = (2 * i + g) * 4 + t
                    pe.wait_ge(picked, i * 8 + max(g * 4 + t - 1, 0) + CREDIT)
                    y = YB[2 * (t % 2):2 * (t % 2) + 2]
                    for half in range(2):
                        for c in range(4):
                            mm = pe.matmul(y[half][:, :], hid[g][:, c, t * P:(t + 1) * P],
                                           w("l1_w2")[:, c * 1024 + half * BANK:c * 1024 + (half + 1) * BANK],
                                           start=(c == 0), stop=(c == 3))
                    mm.then_inc(down, 1)
                    pe.wait_ge(biased, n + CREDIT)
                    pe.matmul(GB[t % 2][:, 0:P], winS[g][:, t * P:(t + 1) * P], w("l1_b2"),
                              start=True, stop=True).then_inc(bias_mm, 1)

            with pe.Fori(0, 4) as i:
                for g in range(2):
                    gates_of(i, g)
                    ups(i, g)
                    downs(i, g)

        @block.scalar
        def _(act):
            with act.Fori(0, 4) as i:
                for g in range(2):
                    for c in range(4):
                        act.wait_ge(up, (2 * i + g) * 4 + c + 1 + CREDIT)
                        act.wait_ge(down, i * 8 + CREDIT)
                        act.activation(hid[g][:, c, :], HB[c % 2][:, :], ACT.Relu).then_inc(hidden, 1)

        @block.vector
        def _(dve):
            with dve.Fori(0, 4) as i:
                for g in range(2):
                    for e in range(8):
                        dve.wait_ge(gate_mm, (2 * i + g) * 8 + e + 1 + CREDIT)
                        dve.wait_ge(up, i * 8 + CREDIT)
                        dve.tensor_tensor(xg[g][:, e, :], GB[e % 2][:, :], XT[:, bass.ds((2 * i + g) * BANK, BANK)],
                                          ALU.mult).then_inc(gated, 1)
                    for t in range(4):
                        n = (2 * i + g) * 4 + t
                        y = YB[2 * (t % 2):2 * (t % 2) + 2]
                        dve.wait_ge(down, n + 1 + CREDIT)
                        xt = joined(X[:, bass.ds(n, 1), :])
                        wn = win[:, bass.ds(n, 1), :]
                        for half in range(2):
                            ins = dve.tensor_tensor(
                                won[t % 2][:, 4 * half:4 * half + 4, :],
                                y[half][:, :].rearrange("p (e d) -> p e d", e=4),
                                over(joined(wn)[:, 4 * half:4 * half + 4], [P, 4, P], 2), ALU.mult)
                        ins.then_inc(picked, 1)
                        dve.wait_ge(picked, n + 1 + CREDIT)
                        dve.wait_ge(residual, n + CREDIT)
                        dve.tensor_reduce(ysum[:, :], won[t % 2][:, :, :].rearrange("p e d -> p d e"), AX.X, ALU.add
                                          ).then_inc(summed, 1)
                        dve.wait_ge(bias_mm, n + 1 + CREDIT)
                        dve.tensor_tensor(xt, GB[t % 2][:, 0:P], xt, ALU.add).then_inc(biased, 1)
                        dve.wait_ge(summed, n + 1 + CREDIT)
                        dve.wait_ge(biased, n + 1 + CREDIT)
                        dve.tensor_tensor(xt, ysum[:, :], xt, ALU.add).then_inc(residual, 1)
                        dve.wait_ge(residual, n + 1 + CREDIT)
                        tile_moments(dve, core, B, xt, n, n, (stats, aggregated, kept))


NSEL = 256
SELT = NSEL // P


def selected_stage(core, ctx, M):
    nc = core.nc
    credited = []
    sem = lambda s: new_sem(core, ctx, f"sel_{s}", credited)
    loaded, done = sem("loaded"), sem("done")
    with ExitStack() as mem:
        mem.callback(retire, core, credited)
        sb = lambda s, shape, dt=F32: mem.enter_context(nc.sbuf_tensor(f"sel_{s}", shape, dt))
        C = SELT + NSEL
        raw = sb("raw", [P, 2, C], mybir.dt.int32)
        num, low, size = sb("num", [P, 2, C]), sb("low", [P, 2, C]), (BATCH, SEQ)
        block = mem.enter_context(nc.Block())

        @block.sync
        def _(sp):
            give_credit(sp, credited)
            for k, name in enumerate(("l3_ib", "l3_it")):
                sp.dma_start(raw[:, k, 0:SELT], core.dram[name + "col"]).then_inc(loaded, 16)
                sp.dma_start(raw[:, k, SELT:C], core.dram[name + "row"].to_broadcast([P, NSEL])).then_inc(loaded, 16)

        @block.vector
        def _(dve):
            dve.wait_ge(loaded, 64 + CREDIT)
            done_so_far = counter(CREDIT)
            dve.tensor_copy(num[:, :, :], raw[:, :, :]).then_inc(done, 1)
            dve.wait_ge(done, done_so_far())
            dve.tensor_scalar(low[:, :, :], num[:, :, :], 0.0, None, ALU.is_lt).then_inc(done, 1)
            dve.wait_ge(done, done_so_far())
            for k in range(2):
                ins = dve.scalar_tensor_tensor(num[:, k, :], low[:, k, :], float(size[k]), num[:, k, :],
                                               ALU.mult, ALU.add)
            ins.then_inc(done, 1)
            dve.wait_ge(done, done_so_far())
            dve.scalar_tensor_tensor(M["jcol"][:, :], num[:, 0, 0:SELT], float(SEQ), num[:, 1, 0:SELT],
                                     ALU.mult, ALU.add).then_inc(done, 1)
            dve.scalar_tensor_tensor(M["jrow"][:, :], num[:, 0, SELT:C], float(SEQ), num[:, 1, SELT:C],
                                     ALU.mult, ALU.add).then_inc(done, 1)


def l3_ffn(core, ctx, next_weights=()):
    nc, X, XT = core.nc, core.X, core.XT
    HF = 64
    GR = TOK // BANK
    NZ = TILES + 8 * SELT
    w = lambda s: weight(core, 7, s)
    ident, bank = core.const("ident"), core.bank
    with ExitStack() as outer:
        osb = lambda s, shape, dt=F32: outer.enter_context(nc.sbuf_tensor(f"f3_{s}", shape, dt))
        M = {"jcol": osb("jcol", [P, SELT]), "jrow": osb("jrow", [P, NSEL])}
        U = osb("U", [P, NZ, HF])
        YS = osb("YS", [P, SELT, P + 1])
        jshift = osb("jshift", [P, SELT, GR])
        selected_stage(core, ctx, M)

        credited = []
        sem = lambda s: new_sem(core, ctx, f"f3a_{s}", credited)
        with ExitStack() as mem:
            mem.callback(retire, core, credited)
            sb = lambda s, shape, dt=F32: mem.enter_context(nc.sbuf_tensor(f"f3a_{s}", shape, dt))
            xs = [sb(f"xs{i}", [P, BANK]) for i in range(2)]
            hb = [sb(f"hb{i}", [P, 4, 2 * HF]) for i in range(2)]
            sl = [sb(f"sl{i}", [P, 4, HF]) for i in range(2)]
            pick = [sb(f"pick{i}", [P, NSEL]) for i in range(2)]
            xm, xmT = sb("xm", [P, SELT, P]), sb("xmT", [P, NSEL])
            eh, es = sb("eh", [P, SELT, 2, 8 * HF]), sb("es", [P, SELT, 8 * HF])
            cen, mean, var, std, rstd = (sb("cen", [P, NZ, HF]), sb("mean", [P, NZ]), sb("var", [P, NZ]),
                                         sb("std", [P, NZ]), sb("rstd", [P, NZ]))
            n8 = [P, SELT, 8]
            lg, sc, bs, vals, idxf, oh = (sb("lg", [P, SELT, 9]), sb("sc", [P, SELT, 9]), sb("bs", n8),
                                          sb("vals", n8), sb("idxf", n8), sb("oh", n8))
            idx = sb("idx", n8, U32)
            ts, dif, ex, sw, ew, same, cnt, rcnt = [sb(s, [P, SELT]) for s in
                                                    ("ts", "dif", "ex", "sw", "ew", "same", "cnt", "rcnt")]
            eq = sb("eq", [P, NSEL])
            ohT, zT = sb("ohT", [8, NSEL]), sb("zT", [P, SELT, 4, P])
            (x_copied, up, added, silu_out, hidden, made, gathered, set_out, set_turned, set_copied, set_up, set_added,
             gates_mm, gates_done, gates_act, experts_act, experts_done, normed, std_ready, z_turned, z_out, oh_turned,
             oh_out, down, chain) = [sem(s) for s in (
                 "x_copied", "up", "added", "silu_out", "hidden", "made", "gathered", "set_out", "set_turned",
                 "set_copied", "set_up", "set_added", "gates_mm", "gates_done", "gates_act", "experts_act",
                 "experts_done", "normed", "std_ready", "z_turned", "z_out", "oh_turned", "oh_out", "down",
                 "chain")]
            GB, EB = bank[7], bank[3:7]
            block = mem.enter_context(nc.Block())

            @block.sync
            def _(sp):
                give_credit(sp, credited)

            @block.gpsimd
            def _(pool):
                with pool.Fori(0, GR // 2) as i:
                    for g in range(2):
                        pool.wait_ge(up, 2 * i + CREDIT)
                        carry_waits(core, pool)
                        pool.tensor_copy(xs[g][:, :], XT[:, bass.ds((2 * i + g) * BANK, BANK)]).then_inc(x_copied, 1)

            @block.tensor
            def _(pe):
                pe.wait_ge(core.weights_in[7], loaded_count(7))
                pe.wait_ge(credited[-1], CREDIT)
                with pe.Fori(0, GR // 2) as i:
                    for g in range(2):
                        pe.wait_ge(x_copied, 2 * i + g + 1 + CREDIT)
                        pe.wait_ge(added, 2 * i + CREDIT)
                        for t in range(4):
                            mm = pe.matmul(bank[g][:, t * P:(t + 1) * P], xs[g][:, t * P:(t + 1) * P], w("l3_s1"),
                                           start=True, stop=True)
                        mm.then_inc(up, 1)
                for t in range(TILES):
                    pe.wait_ge(made, t + 1 + CREDIT)
                    for j in range(SELT):
                        if t == 0:
                            pe.wait_ge(added, GR - 1 + j + CREDIT)
                        mm = pe.matmul(bank[j][:, 0:P], pick[t % 2][:, j * P:(j + 1) * P], X[:, t, :],
                                       start=(t == 0), stop=(t == TILES - 1))
                    mm.then_inc(gathered, 1)
                pe.wait_ge(set_out, 1 + CREDIT)
                for j in range(SELT):
                    mm = pe.transpose(bank[2][:, j * P:(j + 1) * P], xm[:, j, :], ident)
                mm.then_inc(set_turned, 1)
                pe.wait_ge(set_copied, 1 + CREDIT)
                for j in range(SELT):
                    mm = pe.matmul(GB[:, j * 16:j * 16 + 9], xmT[:, j * P:(j + 1) * P], w("l3_gw"), start=True, stop=True)
                mm.then_inc(gates_mm, 1)
                for j in range(SELT):
                    for k in range(2):
                        pe.matmul(EB[2 * j + k][:, :], xmT[:, j * P:(j + 1) * P], w(f"l3_e{k + 1}"),
                                  start=True, stop=True).then_inc(set_up, 1)
                pe.wait_ge(gates_done, 3 + CREDIT)
                for j in range(SELT):
                    mm = pe.transpose(bank[2][0:8, j * P:(j + 1) * P], oh[:, j, :], ident)
                mm.then_inc(oh_turned, 1)
                pe.wait_ge(set_added, 4 + CREDIT)
                for j in range(SELT):
                    pe.wait_ge(experts_done, j + 1 + CREDIT)
                    for c in range(4):
                        mm = pe.transpose(EB[j][:, c * P:(c + 1) * P],
                                          U[:, TILES + 8 * j + 2 * c:TILES + 8 * j + 2 * c + 2, :].rearrange("p a b -> p (a b)"),
                                          ident)
                    mm.then_inc(z_turned, 1)
                pe.wait_ge(oh_out, 1 + CREDIT)
                for j in range(SELT):
                    pe.wait_ge(z_out, j + 1 + CREDIT)
                    for c in range(4):
                        pe.matmul(bank[j][:, 0:P], zT[:, j, c, :], w("l3_e3")[:, c * P:(c + 1) * P],
                                  start=(c == 0), stop=False)
                    pe.matmul(bank[j][:, 0:P], ohT[:, j * P:(j + 1) * P], w("l3_eb3"),
                              start=False, stop=True).then_inc(down, 1)

            @block.scalar
            def _(act):
                with act.Fori(0, GR // 2) as i:
                    for g in range(2):
                        act.wait_ge(added, 2 * i + g + 1 + CREDIT)
                        act.wait_ge(hidden, 2 * i + CREDIT)
                        act.activation(sl[g][:, :, :], hb[g][:, :, 0:HF], ACT.Silu).then_inc(silu_out, 1)
                act.wait_ge(gathered, TILES + CREDIT)
                for j in range(SELT):
                    ins = act.activation(xm[:, j, :], bank[j][:, 0:P], ACT.Copy)
                ins.then_inc(set_out, 1)
                act.wait_ge(set_turned, 1 + CREDIT)
                act.activation(xmT[:, :], bank[2][:, 0:NSEL], ACT.Copy).then_inc(set_copied, 1)
                act.wait_ge(set_added, 4 + CREDIT)
                act.activation(es[:, :, :], eh[:, :, 0, :], ACT.Silu).then_inc(experts_act, 1)
                act.wait_ge(gates_done, 1 + CREDIT)
                act.activation(sc[:, :, :], lg[:, :, :], ACT.Sigmoid).then_inc(gates_act, 1)
                act.wait_ge(gates_done, 2 + CREDIT)
                act.activation(ex[:, :], dif[:, :], ACT.Exp).then_inc(gates_act, 1)
                act.wait_ge(normed, 5 + CREDIT)
                act.activation(std[:, :], var[:, :], ACT.Sqrt).then_inc(std_ready, 1)
                act.wait_ge(oh_turned, 1 + CREDIT)
                act.activation(ohT[:, :], bank[2][0:8, 0:NSEL], ACT.Copy).then_inc(oh_out, 1)
                for j in range(SELT):
                    act.wait_ge(z_turned, j + 1 + CREDIT)
                    act.activation(zT[:, j, :, :].rearrange("p a b -> p (a b)"), EB[j][:, :], ACT.Copy).then_inc(z_out, 1)
                for j in range(SELT):
                    act.wait_ge(down, j + 1 + CREDIT)
                    ins = act.activation(YS[:, j, 0:P], bank[j][:, 0:P], ACT.Copy)

            @block.vector
            def _(dve):
                dve.wait_ge(core.weights_in[7], loaded_count(7))
                with dve.Fori(0, GR // 2) as i:
                    for g in range(2):
                        dve.wait_ge(up, 2 * i + g + 1 + CREDIT)
                        dve.tensor_tensor(hb[g][:, :, :], bank[g][:, :].rearrange("p (t h) -> p t h", t=4),
                                          over(w("l3_sb"), [P, 4, 2 * HF], 1), ALU.add).then_inc(added, 1)
                        dve.wait_ge(silu_out, 2 * i + g + 1 + CREDIT)
                        dve.tensor_tensor(U[:, bass.ds((2 * i + g) * 4, 4), :], sl[g][:, :, :], hb[g][:, :, HF:2 * HF],
                                          ALU.mult).then_inc(hidden, 1)
                for t in range(TILES):
                    if t >= 2:
                        dve.wait_ge(gathered, t - 1 + CREDIT)
                    dve.tensor_tensor(pick[t % 2][:, :], M["jrow"][:, :], w("l3_token")[:, t:t + 1].to_broadcast([P, NSEL]),
                                      ALU.is_equal).then_inc(made, 1)
                normed_so_far = counter(CREDIT)
                for j in range(SELT):
                    dve.tensor_tensor(eq[:, :], M["jrow"][:, :], M["jcol"][:, j:j + 1].to_broadcast([P, NSEL]),
                                      ALU.is_equal).then_inc(normed, 1)
                    dve.wait_ge(normed, normed_so_far())
                    dve.tensor_reduce(cnt[:, j:j + 1], eq[:, :], AX.X, ALU.add).then_inc(normed, 1)
                    dve.wait_ge(normed, normed_so_far())
                dve.reciprocal(rcnt[:, :], cnt[:, :])
                dve.tensor_tensor(jshift[:, :, :], over(M["jcol"][:, :], [P, SELT, GR], 2),
                                  over(w("l3_base"), [P, SELT, GR], 1), ALU.subtract)
                chain_so_far = counter(CREDIT)
                dve.wait_ge(gates_mm, 1 + CREDIT)
                dve.tensor_tensor(lg[:, :, :], GB[:, 0:32].rearrange("p (j e) -> p j e", j=2)[:, :, 0:9],
                                  over(w("l3_gb"), [P, SELT, 9], 1), ALU.add).then_inc(chain, 1)
                dve.wait_ge(chain, chain_so_far())
                dve.sem_inc(gates_done, 1)
                for j in range(SELT):
                    for k in range(2):
                        dve.wait_ge(set_up, 2 * j + k + 1 + CREDIT)
                        dve.tensor_tensor(eh[:, j, k, :], EB[2 * j + k][:, :], w(f"l3_eb{k + 1}"), ALU.add
                                          ).then_inc(set_added, 1)
                dve.wait_ge(gates_act, 1 + CREDIT)
                dve.tensor_tensor(bs[:, :, :], sc[:, :, 1:9], over(w("l3_eb"), n8, 1), ALU.add).then_inc(chain, 1)
                dve.wait_ge(chain, chain_so_far())
                for j in range(SELT):
                    ins = dve.max(vals[:, j, :], bs[:, j, :])
                ins.then_inc(chain, 1)
                dve.wait_ge(chain, chain_so_far())
                for j in range(SELT):
                    ins = dve.max_index(idx[:, j, :], vals[:, j, :], bs[:, j, :])
                ins.then_inc(chain, 1)
                dve.wait_ge(chain, chain_so_far())
                dve.tensor_copy(idxf[:, :, :], idx[:, :, :]).then_inc(chain, 1)
                dve.wait_ge(chain, chain_so_far())
                dve.tensor_tensor(oh[:, :, :], over(core.const("iota8"), n8, 1), over(idxf[:, :, 0], n8, 2),
                                  ALU.is_equal).then_inc(chain, 1)
                dve.wait_ge(chain, chain_so_far())
                dve.tensor_tensor(bs[:, :, :], oh[:, :, :], sc[:, :, 1:9], ALU.mult).then_inc(chain, 1)
                dve.wait_ge(chain, chain_so_far())
                dve.tensor_reduce(ts[:, :], bs[:, :, :], AX.X, ALU.add).then_inc(chain, 1)
                dve.wait_ge(chain, chain_so_far())
                dve.tensor_tensor(dif[:, :], ts[:, :], sc[:, :, 0], ALU.subtract).then_inc(chain, 1)
                dve.wait_ge(chain, chain_so_far())
                dve.sem_inc(gates_done, 1)
                dve.wait_ge(gates_act, 2 + CREDIT)
                dve.tensor_scalar(ew[:, :], ex[:, :], 1.0, None, ALU.add).then_inc(chain, 1)
                dve.wait_ge(chain, chain_so_far())
                dve.reciprocal(sw[:, :], ew[:, :]).then_inc(chain, 1)
                dve.wait_ge(chain, chain_so_far())
                dve.tensor_tensor(ew[:, :], ex[:, :], sw[:, :], ALU.mult).then_inc(chain, 1)
                dve.wait_ge(chain, chain_so_far())
                dve.tensor_tensor(ew[:, :], ew[:, :], rcnt[:, :], ALU.mult).then_inc(chain, 1)
                dve.wait_ge(chain, chain_so_far())
                dve.tensor_scalar(sw[:, :], sw[:, :], -1.0, None, ALU.add).then_inc(chain, 1)
                dve.wait_ge(chain, chain_so_far())
                dve.tensor_tensor(YS[:, :, P], sw[:, :], rcnt[:, :], ALU.mult)
                dve.tensor_tensor(oh[:, :, :], oh[:, :, :], over(ew[:, :], n8, 2), ALU.mult).then_inc(chain, 1)
                dve.wait_ge(chain, chain_so_far())
                dve.sem_inc(gates_done, 1)
                dve.wait_ge(experts_act, 1 + CREDIT)
                dve.tensor_tensor(U[:, TILES:, :].rearrange("p (j e) h -> p j (e h)", j=SELT), es[:, :, :],
                                  eh[:, :, 1, :], ALU.mult).then_inc(chain, 1)
                dve.wait_ge(chain, chain_so_far())
                dve.tensor_reduce(mean[:, :], U[:, :, :], AX.X, ALU.add).then_inc(chain, 1)
                dve.wait_ge(chain, chain_so_far())
                dve.tensor_scalar(mean[:, :], mean[:, :], 1.0 / HF, None, ALU.mult).then_inc(chain, 1)
                dve.wait_ge(chain, chain_so_far())
                nz = [P, NZ, HF]
                dve.tensor_tensor(cen[:, :, :], U[:, :, :], over(mean[:, :], nz, 2), ALU.subtract).then_inc(chain, 1)
                dve.wait_ge(chain, chain_so_far())
                dve.tensor_tensor(U[:, :, :], cen[:, :, :], cen[:, :, :], ALU.mult).then_inc(chain, 1)
                dve.wait_ge(chain, chain_so_far())
                dve.tensor_reduce(var[:, :], U[:, :, :], AX.X, ALU.add).then_inc(chain, 1)
                dve.wait_ge(chain, chain_so_far())
                dve.tensor_scalar(var[:, :], var[:, :], 1.0 / HF, 1e-5, ALU.mult, ALU.add).then_inc(normed, 1)
                dve.wait_ge(std_ready, 1 + CREDIT)
                dve.reciprocal(rstd[:, :], std[:, :]).then_inc(chain, 1)
                dve.wait_ge(chain, chain_so_far())
                dve.tensor_tensor(U[:, :, :], cen[:, :, :], over(rstd[:, :], nz, 2), ALU.mult).then_inc(chain, 1)
                dve.wait_ge(chain, chain_so_far())
                for j in range(SELT):
                    z = U[:, TILES + 8 * j:TILES + 8 * (j + 1), :]
                    z8 = [P, 8, HF]
                    dve.tensor_tensor(z, z, over(w("l3_eln")[:, 0:HF], z8, 1), ALU.mult).then_inc(chain, 1)
                    dve.wait_ge(chain, chain_so_far())
                    dve.tensor_tensor(z, z, over(w("l3_eln")[:, HF:], z8, 1), ALU.add).then_inc(chain, 1)
                    dve.wait_ge(chain, chain_so_far())
                    dve.tensor_tensor(z, z, over(oh[:, j, :], z8, 2), ALU.mult).then_inc(experts_done, 1)

        credited = []
        with ExitStack() as mem:
            mem.callback(retire, core, credited)
            sb = lambda s, shape, dt=F32: mem.enter_context(nc.sbuf_tensor(f"f3b_{s}", shape, dt))
            zg = [sb(f"zg{i}", [P, 4, HF]) for i in range(2)]
            zr = [sb(f"zr{i}", [P, 4, HF]) for i in range(2)]
            zT = [sb(f"zT{i}", [HF, BANK]) for i in range(2)]
            place = [sb(f"place{i}", [P, SELT, BANK]) for i in range(2)]
            fac, sh, sc = sb("fac", [P, 4]), sb("sh", [P, 4, P]), sb("scaled", [P, 4, P])
            B = {"stat": sb("stat", [P, 6]), "mv": sb("mv", [P, 2])}
            sem = lambda s: new_sem(core, ctx, f"f3b_{s}", credited)
            (zoomed, scaled, turned, turned_out, placed, out_mm, biased, factor, weighted, joined_x, residual, stats,
             aggregated, kept) = [sem(s) for s in (
                 "zoomed", "scaled", "turned", "turned_out", "placed", "out_mm", "biased", "factor", "weighted",
                 "joined", "residual", "stats", "aggregated", "kept")]
            ZB, SB, YB, FB = bank[0:2], bank[2:4], bank[4:6], bank[6:8]
            block = mem.enter_context(nc.Block())

            @block.sync
            def _(sp):
                give_credit(sp, credited)

            @block.gpsimd
            def _(pool):
                with pool.Fori(0, GR // 2) as i:
                    for g in range(2):
                        G = 2 * i + g
                        pool.wait_ge(scaled, 2 * i + CREDIT)
                        pool.tensor_tensor(zg[g][:, :, :], U[:, bass.ds(G * 4, 4), :],
                                           over(w("l3_sln")[:, 0:HF], [P, 4, HF], 1), ALU.mult).then_inc(zoomed, 1)
                        pool.wait_ge(zoomed, G + 1 + CREDIT)
                        pool.wait_ge(turned, 2 * i + CREDIT)
                        pool.tensor_tensor(zr[g][:, :, :], zg[g][:, :, :], over(w("l3_sln")[:, HF:], [P, 4, HF], 1),
                                           ALU.add).then_inc(scaled, 1)

            @block.tensor
            def _(pe):
                with pe.Fori(0, GR // 2) as i:
                    for g in range(2):
                        G = 2 * i + g
                        pe.wait_ge(scaled, G + 1 + CREDIT)
                        pe.wait_ge(turned_out, 2 * i + CREDIT)
                        carry_waits(core, pe)
                        for t in range(4):
                            mm = pe.transpose(ZB[g][0:HF, t * P:(t + 1) * P], zr[g][:, t, :], ident)
                        mm.then_inc(turned, 1)
                    for g in range(2):
                        G = 2 * i + g
                        pe.wait_ge(turned_out, G + 1 + CREDIT)
                        pe.wait_ge(placed, G + 1 + CREDIT)
                        pe.wait_ge(residual, 2 * i + CREDIT)
                        carry_waits(core, pe)
                        for t in range(4):
                            tk = slice(t * P, (t + 1) * P)
                            pe.matmul(YB[g][:, tk], zT[g][:, tk], w("l3_s3"), start=True, stop=True)
                            for j in range(SELT):
                                pe.matmul(SB[g][:, tk], place[g][:, j, tk], YS[:, j, 0:P],
                                          start=(j == 0), stop=(j == SELT - 1))
                            for j in range(SELT):
                                mm = pe.matmul(FB[g][:, t:t + 1], place[g][:, j, tk], YS[:, j, P:P + 1],
                                               start=(j == 0), stop=(j == SELT - 1))
                        mm.then_inc(out_mm, 1)

            @block.scalar
            def _(act):
                with act.Fori(0, GR // 2) as i:
                    for g in range(2):
                        G = 2 * i + g
                        act.wait_ge(turned, G + 1 + CREDIT)
                        act.wait_ge(out_mm, 2 * i + CREDIT)
                        act.activation(zT[g][:, :], ZB[g][0:HF, :], ACT.Copy).then_inc(turned_out, 1)

            @block.vector
            def _(dve):
                def place_set(i, g):
                    G = 2 * i + g
                    dve.wait_ge(out_mm, 2 * i + CREDIT)
                    for j in range(SELT):
                        ins = dve.tensor_tensor(place[g][:, j, :], w("l3_iota"),
                                                joined(jshift[:, j:j + 1, bass.ds(G, 1)]).to_broadcast([P, BANK]),
                                                ALU.is_equal)
                    ins.then_inc(placed, 1)

                with dve.Fori(0, GR // 2) as i:
                    place_set(i, 0)
                    place_set(i, 1)
                    for g in range(2):
                        G = 2 * i + g
                        dve.wait_ge(out_mm, G + 1 + CREDIT)
                        yb = YB[g][:, :].rearrange("p (t d) -> p t d", t=4)
                        xg = X[:, bass.ds(G * 4, 4), :]
                        four = [P, 4, P]
                        dve.tensor_tensor(sh[:, :, :], yb, over(w("l3_sb3"), four, 1), ALU.add).then_inc(biased, 1)
                        dve.tensor_scalar(fac[:, :], FB[g][:, 0:4], 1.0, None, ALU.add).then_inc(factor, 1)
                        dve.wait_ge(biased, G + 1 + CREDIT)
                        dve.wait_ge(factor, G + 1 + CREDIT)
                        dve.tensor_tensor(sc[:, :, :], sh[:, :, :], over(fac[:, :], four, 2), ALU.mult).then_inc(weighted, 1)
                        dve.tensor_tensor(xg, SB[g][:, :].rearrange("p (t d) -> p t d", t=4), xg, ALU.add
                                          ).then_inc(joined_x, 1)
                        dve.wait_ge(weighted, G + 1 + CREDIT)
                        dve.wait_ge(joined_x, G + 1 + CREDIT)
                        dve.tensor_tensor(xg, sc[:, :, :], xg, ALU.add).then_inc(residual, 1)
                        dve.wait_ge(residual, G + 1 + CREDIT)
                        for t in range(4):
                            tile_moments(dve, core, B, joined(X[:, bass.ds(G * 4 + t, 1), :]), G * 4 + t, G * 4 + t,
                                         (stats, aggregated, kept))


NQ = 128
DESCENTS = 50


def routing_stage(core, ctx, VS, SQ):
    nc, XT = core.nc, core.XT
    R = 2 * BATCH
    credited = []
    sem = lambda s: new_sem(core, ctx, f"r_{s}", credited)
    with ExitStack() as mem:
        mem.callback(retire, core, credited)
        sb = lambda s, shape, dt=F32: mem.enter_context(nc.sbuf_tensor(f"r_{s}", shape, dt))
        s, t, junk, sc, u, sel = [sb(n, [R, SEQ]) for n in ("s", "t", "junk", "sc", "u", "sel")]
        smax, na, m, S, L = [sb(n, [R, 1]) for n in ("smax", "na", "m", "S", "L")]
        ones = sb("ones", [R, P])
        row = [sb(f"row{i}", [R, SEQ]) for i in range(2)]
        own, prod, tie, ahead = sb("own", [P, 2]), sb("prod", [P, P]), sb("tie", [P, 2, SEQ]), sb("ahead", [P, 2, SEQ])
        rank, chosen = sb("rank", [P, TILES]), sb("chosen", [P, TILES])
        (products, s_ready, low_ready, shifted, summed, logged, na_ready, scored, exped, selected, turned, turned_out,
         spread, row_ready, owned, tied, counted, ranked, picked, scaled) = [sem(n) for n in (
             "products", "s_ready", "low_ready", "shifted", "summed", "logged", "na_ready", "scored", "exped", "selected",
             "turned", "turned_out", "spread", "row_ready", "owned", "tied", "counted", "ranked", "picked", "scaled")]
        logk, before, ident = core.const("logk", R), core.const("before"), core.const("ident")
        bank = core.bank
        block = mem.enter_context(nc.Block())

        @block.sync
        def _(sp):
            give_credit(sp, credited)

        @block.tensor
        def _(pe):
            pe.wait_ge(core.weights_in[5], loaded_count(5))
            pe.wait_ge(credited[-1], CREDIT)
            tok = weight(core, 5, "l2_tok")
            for b in range(BATCH):
                mm = pe.matmul(bank[0][0:R, 0:SEQ], tok[:, 15 - b:15 - b + R], XT[:, b * SEQ:(b + 1) * SEQ],
                               start=(b == 0), stop=(b == BATCH - 1))
            mm.then_inc(products, 1)
            pe.wait_ge(selected, 2 + CREDIT)
            for h in range(2):
                mm = pe.transpose(bank[1][:, h * R:(h + 1) * R], sel[:, h * P:(h + 1) * P], ident[0:R, 0:R])
            mm.then_inc(turned, 1)
            with pe.Fori(0, BATCH // 2) as i:
                for b in range(2):
                    pe.wait_ge(row_ready, 2 * i + b + 1 + CREDIT)
                    pe.wait_ge(counted, 2 * i + CREDIT)
                    carry_waits(core, pe)
                    pe.matmul(bank[2 + b][:, 0:SEQ], ones[:, :], row[b][:, :], start=True, stop=True
                              ).then_inc(spread, 1)

        @block.gpsimd
        def _(pool):
            pool.wait_ge(exped, 1 + CREDIT)
            with pool.Fori(0, BATCH // 2) as i:
                for b in range(2):
                    pool.wait_ge(spread, 2 * i + CREDIT)
                    pool.tensor_tensor(row[b][:, :], sc[:, :],
                                       ident[0:R, bass.ds(2 * i + b, 1)].to_broadcast([R, SEQ]),
                                       ALU.mult).then_inc(row_ready, 1)

        @block.scalar
        def _(act):
            nc.scalar.preload_act_table_set("natural_log_exp_and_others")
            def log_sum(n):
                act.wait_ge(shifted, n + 1 + CREDIT)
                act.activation(junk[:, :], t[:, :], ACT.Exp, accum_out=S[:, :]).then_inc(summed, 1)
                act.wait_ge(summed, n + 1 + CREDIT)
                act.activation(L[:, :], S[:, :], ACT.Ln).then_inc(logged, 1)

            log_sum(0)
            with act.Fori(1, DESCENTS) as n:
                log_sum(n)
            act.wait_ge(scored, 1 + CREDIT)
            act.activation(sc[:, :], t[:, :], ACT.Exp).then_inc(exped, 1)

        @block.vector
        def _(dve):
            dve.wait_ge(core.weights_in[5], loaded_count(5))
            for k, names in (("l2_gl", ("l2_wql", "l2_wkl", "l2_wvl")), ("l2_gh", ("l2_wqh", "l2_wkh", "l2_wvh"))):
                for n in names:
                    w = weight(core, 5, n)
                    dve.tensor_scalar(w, w, weight(core, 5, k), None, ALU.mult)
            dve.memset(ones[:, :], 1.0)
            dve.memset(VS[:, BATCH, :], 0.0)
            dve.memset(t[:, :], 0.0).then_inc(shifted, 1)
            dve.wait_ge(products, 1 + CREDIT)
            dve.tensor_copy(s[:, :], bank[0][0:R, 0:SEQ]).then_inc(s_ready, 1)
            dve.wait_ge(s_ready, 1 + CREDIT)
            dve.tensor_reduce(smax[:, :], s[:, :], AX.X, ALU.max).then_inc(s_ready, 1)
            dve.memset(m[:, :], 0.0).then_inc(low_ready, 1)
            dve.wait_ge(low_ready, 1 + CREDIT)
            dve.wait_ge(logged, 1 + CREDIT)
            dve.tensor_scalar(na[:, :], L[:, :], m[:, :], logk, ALU.add, ALU.subtract).then_inc(na_ready, 1)
            dve.wait_ge(s_ready, 2 + CREDIT)
            with dve.Fori(1, DESCENTS) as n:
                dve.wait_ge(na_ready, n + CREDIT)
                dve.tensor_tensor(m[:, :], smax[:, :], na[:, :], ALU.min).then_inc(low_ready, 1)
                dve.wait_ge(low_ready, n + 1 + CREDIT)
                dve.tensor_scalar(t[:, :], s[:, :], na[:, :], m[:, :], ALU.min, ALU.subtract).then_inc(shifted, 1)
                dve.wait_ge(logged, n + 1 + CREDIT)
                dve.tensor_scalar(na[:, :], L[:, :], m[:, :], logk, ALU.add, ALU.subtract).then_inc(na_ready, 1)
            dve.wait_ge(na_ready, DESCENTS + CREDIT)
            dve.tensor_scalar(t[:, :], s[:, :], na[:, :], 0.0, ALU.subtract, ALU.min).then_inc(scored, 1)
            dve.wait_ge(exped, 1 + CREDIT)
            dve.tensor_scalar(u[:, :], sc[:, :], -1.0, 1.0, ALU.mult, ALU.add).then_inc(selected, 1)
            dve.wait_ge(selected, 1 + CREDIT)
            dve.tensor_tensor(sel[:, :], sc[:, :], u[:, :], ALU.add).then_inc(selected, 1)
            dve.wait_ge(turned, 1 + CREDIT)
            by_row = bank[1][:, 0:2 * R].rearrange("p (h r) -> p r h", h=2)
            dve.tensor_copy(SQ[:, :].rearrange("p (b h) -> p b h", h=2), by_row[:, 0:BATCH, :]).then_inc(turned_out, 1)
            dve.tensor_copy(VS[:, 0:BATCH, :], by_row[:, BATCH:R, :]).then_inc(turned_out, 1)
            with dve.Fori(0, BATCH // 2) as i:
                for b in range(2):
                    q = 2 * i + b
                    dve.wait_ge(spread, q + 1 + CREDIT)
                    carry_waits(core, dve)
                    for h in range(2):
                        ins = dve.tensor_tensor_reduce(prod[:, :], bank[2 + b][:, h * P:(h + 1) * P], ident, 1.0, 0.0,
                                                       ALU.mult, ALU.add, own[:, h:h + 1])
                        ins.then_inc(owned, 1)
                        dve.wait_ge(owned, 2 * q + h + 1 + CREDIT)
                        carry_waits(core, dve)
                    dve.wait_ge(ranked, q + CREDIT)
                    for h in range(2):
                        dve.scalar_tensor_tensor(tie[:, h, :], bank[2 + b][:, 0:SEQ], own[:, h:h + 1],
                                                 before[:, h * SEQ:(h + 1) * SEQ], ALU.is_equal, ALU.mult
                                                 ).then_inc(tied, 1)
                    dve.wait_ge(tied, 2 * q + 2 + CREDIT)
                    for h in range(2):
                        ins = dve.scalar_tensor_tensor(ahead[:, h, :], bank[2 + b][:, 0:SEQ], own[:, h:h + 1],
                                                       tie[:, h, :], ALU.is_gt, ALU.add)
                    ins.then_inc(counted, 1)
                    dve.wait_ge(counted, q + 1 + CREDIT)
                    dve.tensor_reduce(rank[:, bass.ds(2 * q, 2)], ahead[:, :, :], AX.X, ALU.add).then_inc(ranked, 1)
            dve.wait_ge(ranked, BATCH + CREDIT)
            dve.tensor_scalar(chosen[:, :], rank[:, :], float(NQ), None, ALU.is_lt).then_inc(picked, 1)
            dve.wait_ge(picked, 1 + CREDIT)
            dve.wait_ge(turned_out, 1 + CREDIT)
            dve.tensor_tensor(SQ[:, :], SQ[:, :], chosen[:, :], ALU.mult).then_inc(scaled, 1)


class ScaledEpilogue(Epilogue):

    def __init__(self, wo, factors):
        self.wo, self.factors = wo, factors

    def alloc(self, sb, B):
        B["yb"] = sb("yb", [P, DM])

    def dve(self, dve, core, B, S, i, e, xt, y):
        t = 4 * i + e
        dve.tensor_scalar(B["yb"][:, :], y, self.factors[:, bass.ds(t, 1)], None, ALU.mult).then_inc(S["epilogue"], 1)
        dve.wait_ge(S["epilogue"], t + 1 + CREDIT)
        dve.tensor_tensor(xt, B["yb"][:, :], xt, ALU.add).then_inc(S["residual"], 1)


def l2_ffn(core, ctx, next_weights=()):
    with ExitStack() as mem:
        VS = mem.enter_context(core.nc.sbuf_tensor("VS", [P, BATCH + 1, 2], F32))
        SQ = mem.enter_context(core.nc.sbuf_tensor("SQ", [P, TILES], F32))
        routing_stage(core, ctx, VS, SQ)
        normalize_stage(core, ctx, "u", unit=True)
        light = Heads(8, 64, 64, [(0, P), (P, P)])
        attention_stage(core, ctx, "5l", light, PlainSteps(5, ("l2_wql", "l2_wkl", "l2_wvl"), 512, 512, 64, -1.0 / 8.0),
                        Epilogue(weight(core, 5, "l2_wol")), moments=False, weights_of=5)
        heavy = Heads(8, 64, 64, [(0, SEQ), (0, SEQ)])
        attention_stage(core, ctx, "5h", heavy,
                        PlainSteps(5, ("l2_wqh", "l2_wkh", "l2_wvh"), 512, 512, 64, -1.0 / 8.0, value_scale=VS),
                        ScaledEpilogue(weight(core, 5, "l2_woh"), SQ), weights_of=5, next_weights=next_weights)



def build(nc, dram):
    with ExitStack() as ctx:
        core = Core(nc, ctx, dram)
        normalize_stage(core, ctx, 0, first=True, next_weights=(0, 1))
        l0_attention(core, ctx)
        normalize_stage(core, ctx, 1, next_weights=(2,))
        l0_ffn(core, ctx)
        normalize_stage(core, ctx, 2, next_weights=(3,))
        l1_attention(core, ctx)
        normalize_stage(core, ctx, 3, next_weights=(4,))
        l1_ffn(core, ctx)
        normalize_stage(core, ctx, 4, next_weights=(5,))
        l2_attention(core, ctx)
        normalize_stage(core, ctx, 5, next_weights=(6,))
        l2_ffn(core, ctx)
        normalize_stage(core, ctx, 6, next_weights=(7,))
        l3_attention(core, ctx)
        normalize_stage(core, ctx, 7)
        l3_ffn(core, ctx)
        normalize_stage(core, ctx, 8, last=True)


def spaced(a, H, dv, dvp):
    n = a.shape[1]
    out = np.zeros((H, dvp, n), np.float32)
    out[:, :dv] = a.reshape(H, dv, n)
    return out.reshape(-1, P, n).transpose(1, 0, 2).reshape(P, -1)


def half_swapped(a, H, d):
    return a.reshape(a.shape[0], H, 2, d // 2)[:, :, ::-1].reshape(a.shape)


def chunked(a):
    return a.reshape(-1, P, a.shape[1]).transpose(1, 0, 2).reshape(P, -1)


def lay_out(v):
    o = {}
    head_cat = lambda c, r: np.concatenate([c.reshape(-1, 16, 8), r.reshape(-1, 16, 32)], 2).reshape(-1, 640)
    zero = lambda rows, d: np.zeros((rows, 16 * d), np.float32)
    o["l0_wkv"], o["l0_wq"], o["l0_gkv"] = v["L0_attn_W_kv"], v["L0_attn_W_q"], v["L0_attn_g_kv"].reshape(32, 1)
    qr, kr = v["L0_attn_W_qrope"], v["L0_attn_W_krope"]
    o["l0_wqall"] = head_cat(v["L0_attn_W_qdec"], qr)
    o["l0_wqrot"] = head_cat(zero(64, 8), half_swapped(qr, 16, 32))
    o["l0_wkdec"] = head_cat(v["L0_attn_W_kdec"], zero(32, 32))
    o["l0_wkrope"] = head_cat(zero(128, 8), kr)
    o["l0_wkrot"] = head_cat(zero(128, 8), half_swapped(kr, 16, 32))
    o["l0_wvdec"] = v["L0_attn_W_vdec"]
    o["l0_wo"] = spaced(v["L0_attn_W_o"], 16, 8, 32)

    o["l0_rw"], o["l0_rb"] = v["L0_ffn_router_w"], v["L0_ffn_router_b"].reshape(1, 8)
    for k in "13":
        w = np.concatenate([v[f"L0_ffn_routed_w{k}"], v[f"L0_ffn_shared_w{k}"]], 0)
        o[f"l0_w{k}"] = w.transpose(1, 0, 2).reshape(P, 640)
    o["l0_w2"] = chunked(np.concatenate([v["L0_ffn_routed_w2"], v["L0_ffn_shared_w2"]], 0).reshape(640, P))

    for k in "qk":
        o[f"l1_w{k}"] = v[f"L1_attn_W{k}"]
        o[f"l1_w{k}rot"] = half_swapped(v[f"L1_attn_W{k}"], 16, 8)
    o["l1_wv"], o["l1_rel"] = v["L1_attn_Wv"], v["L1_attn_rel_emb"]
    o["l1_wo"] = spaced(v["L1_attn_Wo"], 16, 8, 32)

    o["l1_gw"], o["l1_gb"] = v["L1_ffn_gate_w"].T, v["L1_ffn_gate_b"].reshape(1, 8)
    o["l1_w1"] = v["L1_ffn_w1"].transpose(2, 0, 1).reshape(P, 4096)
    o["l1_b1"] = v["L1_ffn_b1"]
    o["l1_w2"] = v["L1_ffn_w2"].transpose(2, 0, 1).reshape(4, P, 8 * P).transpose(1, 0, 2).reshape(P, 4096)
    o["l1_b2"] = v["L1_ffn_b2"]

    for k in "qkv":
        o[f"l2_w{k}"] = v[f"L2_attn_W{k}"]
    o["l2_wo"] = spaced(v["L2_attn_Wo"], 16, 16, 32)

    for s, kind in (("l", "light"), ("h", "heavy")):
        o[f"l2_g{s}"] = v[f"L2_ffn_gamma_{kind}"].reshape(P, 1)
        o[f"l2_wq{s}"] = v[f"L2_ffn_wq_{kind}"]
        wkv = v[f"L2_ffn_wkv_{kind}"]
        if s == "l":
            k, w = wkv[:, 0:512], wkv[:, 512:1024]
        else:
            w = wkv.T.reshape(P, 8, 2, 64)
            k, w = w[:, :, 0].reshape(P, 512), w[:, :, 1].reshape(P, 512)
        o[f"l2_wk{s}"], o[f"l2_wv{s}"] = k, w
        o[f"l2_wo{s}"] = chunked(v[f"L2_ffn_wo_{kind}"])
    tok = np.zeros((P, 64), np.float32)
    tok[:, 15], tok[:, 31] = v["L2_ffn_q_routing_token"], v["L2_ffn_kv_routing_token"]
    o["l2_tok"] = tok

    w, bias = v["L3_attn_Wqkv_w"].T, v["L3_attn_Wqkv_b"]
    for j, k in enumerate("qkv"):
        o[f"l3_w{k}"] = w[:, j * 1024:(j + 1) * 1024]
        b = bias[j * 1024:(j + 1) * 1024]
        o[f"l3_b{k}"] = b.reshape(1, 1024) if k == "v" else b.reshape(8, P).T
    o["l3_wo"] = chunked(v["L3_attn_Wo_w"].T)
    o["l3_bo"], o["l3_ghost"] = v["L3_attn_Wo_b"].reshape(1, P), v["L3_attn_ghost"].reshape(1, 16)

    row = lambda *names: np.concatenate([v[s].reshape(-1) for s in names]).reshape(1, -1)
    o["l3_s1"] = np.concatenate([v["L3_ffn_sw1"].T, v["L3_ffn_sw2"].T], 1)
    o["l3_sb"] = row("L3_ffn_sb1", "L3_ffn_sb2")
    o["l3_s3"], o["l3_sb3"] = v["L3_ffn_sw3"].T, row("L3_ffn_sb3")
    o["l3_sln"] = row("L3_ffn_s_ln_g", "L3_ffn_s_ln_b")
    o["l3_gw"] = np.concatenate([v["L3_ffn_sg_w"], v["L3_ffn_eg_w"]], 0).T
    o["l3_gb"], o["l3_eb"] = row("L3_ffn_sg_b", "L3_ffn_eg_b"), row("L3_ffn_exp_bias")
    for k in "12":
        o[f"l3_e{k}"] = v[f"L3_ffn_ew{k}"].transpose(2, 0, 1).reshape(P, 512)
        o[f"l3_eb{k}"] = row(f"L3_ffn_eb{k}")
    o["l3_e3"] = chunked(v["L3_ffn_ew3"].transpose(0, 2, 1).reshape(512, P))
    o["l3_eb3"] = v["L3_ffn_eb3"]
    o["l3_eln"] = row("L3_ffn_sel_ln_g", "L3_ffn_sel_ln_b")
    for k in "bt":
        index = v[f"L3_ffn_index_{k}"]
        o[f"l3_i{k}col"], o[f"l3_i{k}row"] = index.reshape(2, P).T, index.reshape(1, 2 * P)
    o["l3_token"] = np.arange(TOK, dtype=np.float32).reshape(TILES, P).T
    o["l3_base"] = np.arange(0, TOK, BANK, dtype=np.float32).reshape(1, 8)
    o["l3_iota"] = np.arange(BANK, dtype=np.float32).reshape(1, BANK)
    return o


def kernel(**inputs):
    import concourse.bacc as bacc
    from concourse.bass_utils import run_bass_kernel_spmd

    nc = bacc.Bacc("TRN2", target_bir_lowering=False, num_devices=1)
    v = {k: np.asarray(a) for k, a in inputs.items()}
    arrays = lay_out(v)
    arrays["x"] = v["L0_attn_x"].reshape(TOK, DM)
    _, arrays["consts"], staged = shape_constants()
    arrays.update(staged)
    given, dram = {}, {}
    for name, a in arrays.items():
        a = np.ascontiguousarray(a)
        given["in_" + name] = a
        dram[name] = nc.dram_tensor("in_" + name, a.shape, mybir.dt.from_np(a.dtype), kind="ExternalInput").ap()
    dram["out"] = nc.dram_tensor("out_x", (TOK, DM), F32, kind="ExternalOutput").ap()
    build(nc, dram)
    r = run_bass_kernel_spmd(nc, [given], core_ids=[0])
    return r.results[0]["out_x"].reshape(BATCH, SEQ, DM)
```

```python
import math
from contextlib import ExitStack

import numpy as np

import concourse.bass as bass
from concourse import mybir

ALU = mybir.AluOpType
ACT = mybir.ActivationFunctionType
AX = mybir.AxisListType
F32 = mybir.dt.float32
U32 = mybir.dt.uint32

P = 128
BATCH, SEQ, DM = 16, 256, 128
TILES = BATCH * SEQ // P
TOK = BATCH * SEQ
BIG = 1.0e30
LN_EPS = 1e-5
CREDIT = 1
BANK = 512
W_COLS = (5760, 8864)


def rope_tables(dim, heads_rows, content, scale, through=1.0):
    inv = (1.0 / 10000.0 ** (np.arange(0, dim, 2, dtype=np.float32) / np.float32(dim))).astype(np.float32)
    f = np.outer(np.arange(SEQ, dtype=np.float32), inv)
    emb = np.concatenate([f, f], -1).astype(np.float32)
    c, s = np.cos(emb).T, np.sin(emb).T.copy()
    s[: dim // 2] *= -1.0
    one = np.concatenate([np.full((content, SEQ), through, np.float32), c], 0)
    two = np.concatenate([np.zeros((content, SEQ), np.float32), s], 0)
    pad = np.zeros((P, 2, SEQ), np.float32)
    n = heads_rows * (content + dim)
    pad[:n, 0] = np.tile(one, (heads_rows, 1)) * np.float32(scale)
    pad[:n, 1] = np.tile(two, (heads_rows, 1)) * np.float32(scale)
    return pad.reshape(P, 2 * SEQ)


def head_rows(D):
    hpc = P // D
    m = np.zeros((P, hpc), np.float32)
    for h in range(hpc):
        m[h * D:(h + 1) * D, h] = 1.0
    return m


def shape_constants():
    q = np.arange(P)[:, None]
    c = np.arange(2 * P)[None, :]
    dist = 255 - np.arange(383)
    n = np.maximum(dist, 0)
    large = 16 + (np.log(np.maximum(n, 1).astype(np.float32) / np.float32(16)) / np.float32(math.log(8.0))
                  * np.float32(16)).astype(np.int32)
    bucket = np.where(n < 16, n, np.minimum(large, 31))
    onehot = np.zeros((P, 383), np.float32)
    onehot[bucket, np.arange(383)] = 1.0
    onehot[:, dist < 0] = 0.0
    neg = np.zeros((P, 383), np.float32)
    neg[:, dist < 0] = BIG
    logk = np.zeros((P, 1), np.float32)
    logk[0:BATCH] = np.log(np.float32(144.0))
    logk[BATCH:2 * BATCH] = np.log(np.float32(256.0))
    before = np.concatenate([(c < q), (c < q + P)], 1).astype(np.float32)
    parts = [
        ("ident", np.eye(P, dtype=np.float32)),
        ("flip", np.ascontiguousarray(np.eye(P, dtype=np.float32)[::-1])),
        ("causal", np.where(c - P > q, np.float32(BIG), np.float32(0.0)).astype(np.float32)),
        ("rope40q", rope_tables(32, 3, 8, -1.0 / math.sqrt(40.0))),
        ("rope40k", rope_tables(32, 3, 8, 1.0, 0.0)),
        ("content40", np.tile(np.pad(np.tile(np.arange(40) < 8, 3), (0, P - 120)).astype(np.float32), (P, 1))),
        ("rope8q", rope_tables(8, 16, 0, -1.0 / math.sqrt(8.0))),
        ("rope8k", rope_tables(8, 16, 0, 1.0)),
        ("heads40", head_rows(40)), ("heads8", head_rows(8)), ("heads16", head_rows(16)), ("heads64", head_rows(64)),
        ("bucket", onehot), ("future", neg), ("logk", logk), ("before", before),
        ("iota8", np.tile(np.arange(8, dtype=np.float32), (P, 1))),
    ]
    at, out, resident, staged = 0, {}, [], {}
    for name, a in parts:
        if name in STAGED:
            staged[name] = a
            continue
        out[name] = (at, a.shape[1])
        at += a.shape[1]
        resident.append(a)
    return out, np.ascontiguousarray(np.concatenate(resident, 1)), staged


STAGED = {"rope40q": 0, "content40": 0, "rope40k": 0, "rope8q": 2, "rope8k": 2, "bucket": 2, "future": 2, "before": 5}


class Core:

    def __init__(self, nc, ctx, dram):
        self.nc, self.dram = nc, dram
        self.at, table, _ = shape_constants()
        self.X = ctx.enter_context(nc.sbuf_tensor("X", [P, TILES, DM], F32))
        self.XT = ctx.enter_context(nc.sbuf_tensor("XT", [P, (BATCH + 2) * SEQ], F32))
        self.cst = ctx.enter_context(nc.sbuf_tensor("cst", [P, table.shape[1]], F32))
        self.mv = ctx.enter_context(nc.sbuf_tensor("mv", [P, TILES, 2], F32))
        self.rstd = ctx.enter_context(nc.sbuf_tensor("rstd", [P, TILES], F32))
        self.W = [ctx.enter_context(nc.sbuf_tensor(f"W{i}", [P, W_COLS[i]], F32)) for i in range(2)]
        self.bank = [ctx.enter_context(nc.psum_tensor(f"bank{i}", [P, BANK], F32)) for i in range(8)]
        self.weights_in = [ctx.enter_context(nc.semaphore(f"weights_in{k}")) for k in range(8)]
        self.carried = ctx.enter_context(nc.semaphore("carried"))
        self.consts_in = ctx.enter_context(nc.semaphore("consts_in"))

    def const(self, name, rows=P):
        if name in STAGED:
            return weight(self, STAGED[name], name)[0:rows, :]
        a, n = self.at[name]
        return self.cst[0:rows, a:a + n]


def place_weights(items, region_cols):
    at, out = 0, {}
    for name, rows, cols in items:
        out[name] = (rows, at, cols)
        at += cols
    assert at <= region_cols, (at, region_cols)
    return out


WEIGHTS = {
    0: [("l0_wkv", 128, 32), ("l0_wqT", 64, 128), ("l0_wkvT", 32, 128), ("l0_gkv", 32, 1), ("l0_wqall", 64, 640), ("l0_wqrot", 64, 640),
        ("l0_wkdec", 32, 640), ("l0_wkrope", 128, 640), ("l0_wkrot", 128, 640), ("l0_wvdec", 32, 128),
        ("l0_wo", 128, 512), ("rope40q", 128, 512), ("rope40k", 128, 512), ("content40", 128, 128)],
    1: [("l0_rw", 128, 8), ("l0_rb", 128, 8), ("l0_w1", 128, 640), ("l0_w3", 128, 640), ("l0_w2", 128, 640)],
    2: [("l1_wq", 128, 128), ("l1_wqrot", 128, 128), ("l1_wk", 128, 128), ("l1_wkrot", 128, 128),
        ("l1_wv", 128, 128), ("l1_rel", 32, 16), ("l1_wo", 128, 512), ("rope8q", 128, 512), ("rope8k", 128, 512), ("bucket", 128, 383),
        ("future", 128, 383)],
    3: [("l1_gw", 128, 8), ("l1_gb", 128, 8), ("l1_w1", 128, 4096), ("l1_b1", 128, 32), ("l1_w2", 128, 4096),
        ("l1_lower", 128, 128), ("l1_ones", 128, 128), ("l1_multiples", 128, 32), ("l1_earlier", 128, 64),
        ("l1_iota", 128, 40)],
    4: [("l2_wq", 128, 256), ("l2_wk", 128, 256), ("l2_wv", 128, 256), ("l2_wo", 128, 512)],
    5: [("l2_gl", 128, 1), ("l2_wql", 128, 512), ("l2_wkl", 128, 512), ("l2_wvl", 128, 512), ("l2_wol", 128, 512),
        ("l2_tok", 128, 64), ("before", 128, 512),
        ("l2_gh", 128, 1), ("l2_wqh", 128, 512), ("l2_wkh", 128, 512), ("l2_wvh", 128, 512), ("l2_woh", 128, 512)],
    6: [("l3_wq", 128, 1024), ("l3_wk", 128, 1024), ("l3_wv", 128, 1024), ("l3_bq", 128, 8), ("l3_bk", 128, 8),
        ("l3_bv", 128, 1024), ("l3_wo", 128, 1024), ("l3_bo", 128, 128), ("l3_ghost", 128, 16)],
    7: [("l3_s1", 128, 128), ("l3_sb", 128, 128), ("l3_s3", 64, 128), ("l3_sb3", 128, 128), ("l3_sln", 128, 128),
        ("l3_gw", 128, 9), ("l3_gb", 128, 9), ("l3_eb", 128, 8), ("l3_e1", 128, 512), ("l3_e2", 128, 512),
        ("l3_eb1", 128, 512), ("l3_eb2", 128, 512), ("l3_e3", 128, 512), ("l3_eb3", 8, 128), ("l3_eln", 128, 128),
        ("l3_token", 128, 32), ("l3_base", 128, 8), ("l3_iota", 128, 512)],
}
LAYOUT = {k: place_weights(v, W_COLS[k % 2]) for k, v in WEIGHTS.items()}


def weight(core, k, name):
    rows, at, cols = LAYOUT[k][name]
    return core.W[k % 2][0:rows, at:at + cols]


def load_weights(core, eng, k):
    for name, rows, cols in WEIGHTS[k]:
        src = core.dram[name]
        if src.shape[0] == 1 and rows > 1:
            src = src.to_broadcast([rows, cols])
        eng.dma_start(weight(core, k, name), src).then_inc(core.weights_in[k], 16)


def new_sem(core, ctx, name, credited):
    s = core.nc.alloc_semaphore(name)
    credited.append(s)
    return s


def retire(core, credited):
    core.nc.clear_and_free_semaphores(credited)
    core.nc.all_engine_barrier()


def give_credit(sp, credited):
    for s in credited:
        sp.sem_inc(s, 1)


def counter(start):
    total = [start]

    def one_more():
        total[0] += 1
        return total[0]

    return one_more


def carry_waits(core, eng):
    eng.sem_inc(core.carried, 1)


def loaded_count(k):
    return 16 * len(WEIGHTS[k])


def normalize_stage(core, ctx, n, first=False, last=False, unit=False, next_weights=()):
    nc, X, XT = core.nc, core.X, core.XT
    G = 4
    GROUPS = TILES // G
    SQUARES = 8
    LOADS = 4 if first else 0
    BY_ACT = 5
    credited = []
    sem = lambda s: new_sem(core, ctx, f"n{n}_{s}", credited)
    with ExitStack() as mem:
        mem.callback(retire, core, credited)
        std = mem.enter_context(nc.sbuf_tensor(f"n{n}_std", [P, TILES], F32))
        sq = mem.enter_context(nc.sbuf_tensor(f"n{n}_sq", [P, SQUARES, DM], F32)) if unit else None
        normed = mem.enter_context(nc.sbuf_tensor(f"n{n}_unit", [P, TILES, DM], F32)) if unit else X
        x_loaded = [sem(f"x_loaded{k}") for k in range(LOADS)]
        var_ready, std_ready, rstd_ready = sem("var_ready"), sem("std_ready"), sem("rstd_ready")
        group_normed, group_turned, out_stored, squared = (
            sem("group_normed"), sem("group_turned"), sem("out_stored"), sem("squared"))
        ident = core.const("ident")
        block = mem.enter_context(nc.Block())

        @block.sync
        def _(sp):
            give_credit(sp, credited)
            if first:
                sp.dma_start(core.cst[:, :], core.dram["consts"]).then_inc(core.consts_in, 16)
                x = core.dram["x"].rearrange("(t p) d -> p t d", p=P)
                for k in range(LOADS):
                    part = slice(k * TILES // LOADS, (k + 1) * TILES // LOADS)
                    sp.dma_start(X[:, part, :], x[:, part, :]).then_inc(x_loaded[k], 16)
            for k in next_weights:
                load_weights(core, sp, k)
            if last:
                out = core.dram["out"].rearrange("(t p) d -> p t d", p=P)
                for g in range(GROUPS):
                    sp.wait_ge(group_normed, g + 1 + CREDIT)
                    sp.dma_start(out[:, g * G:(g + 1) * G, :], X[:, g * G:(g + 1) * G, :]).then_inc(out_stored, 16)
                sp.wait_ge(out_stored, 16 * GROUPS + CREDIT)

        @block.vector
        def _(dve):
            dve.wait_ge(credited[-1], CREDIT)
            if first:
                dve.memset(XT[:, TOK:], 0.0)
            elif unit:
                squared_so_far = counter(CREDIT)
                for c in range(0, TILES, SQUARES):
                    dve.tensor_tensor(sq[:, :, :], X[:, c:c + SQUARES, :], X[:, c:c + SQUARES, :], ALU.mult
                                      ).then_inc(squared, 1)
                    dve.wait_ge(squared, squared_so_far())
                    dve.tensor_reduce(core.rstd[:, c:c + SQUARES], sq[:, :, :], AX.X, ALU.add).then_inc(squared, 1)
                    dve.wait_ge(squared, squared_so_far())
                dve.tensor_scalar(core.rstd[:, :], core.rstd[:, :], 1.0 / DM, None, ALU.mult).then_inc(var_ready, 1)
                dve.wait_ge(std_ready, 1 + CREDIT)
                dve.tensor_scalar(std[:, :], std[:, :], 1e-12 / math.sqrt(DM), None, ALU.max).then_inc(var_ready, 1)
                dve.wait_ge(var_ready, 2 + CREDIT)
                dve.reciprocal(core.rstd[:, :], std[:, :]).then_inc(rstd_ready, 1)
                dve.wait_ge(rstd_ready, 1 + CREDIT)
            else:
                dve.tensor_scalar(core.rstd[:, :], core.mv[:, :, 1], LN_EPS, None, ALU.add).then_inc(var_ready, 1)
                dve.wait_ge(std_ready, 1 + CREDIT)
                dve.reciprocal(core.rstd[:, :], std[:, :]).then_inc(rstd_ready, 1)
                dve.wait_ge(rstd_ready, 1 + CREDIT)
            for t in range(TILES):
                if first:
                    break
                if unit:
                    ins = dve.tensor_scalar(normed[:, t, :], X[:, t, :], core.rstd[:, t:t + 1], None, ALU.mult)
                else:
                    ins = dve.tensor_scalar(X[:, t, :], X[:, t, :], core.mv[:, t, 0:1], core.rstd[:, t:t + 1],
                                            ALU.subtract, ALU.mult)
                if t % G == G - 1:
                    ins.then_inc(group_normed, 1)
            if not last:
                for g in range(BY_ACT, GROUPS):
                    dve.wait_ge(group_turned, g + 1 + CREDIT)
                    dve.tensor_copy(XT[:, g * BANK:(g + 1) * BANK], core.bank[g][:, :])

        @block.tensor
        def _(pe):
            pe.wait_ge(core.consts_in, 16)
            if last:
                return
            for g in range(GROUPS):
                if first:
                    pe.wait_ge(x_loaded[g * LOADS // GROUPS], 16 + CREDIT)
                else:
                    pe.wait_ge(group_normed, g + 1 + CREDIT)
                for t in range(G):
                    mm = pe.transpose(core.bank[g][:, t * P:(t + 1) * P], normed[:, g * G + t, :], ident)
                mm.then_inc(group_turned, 1)

        @block.scalar
        def _(act):
            if not first:
                act.wait_ge(var_ready, 1 + CREDIT)
                act.activation(std[:, :], core.rstd[:, :], ACT.Sqrt).then_inc(std_ready, 1)
            if not last:
                for g in range(BY_ACT):
                    act.wait_ge(group_turned, g + 1 + CREDIT)
                    act.activation(XT[:, g * BANK:(g + 1) * BANK], core.bank[g][:, :], ACT.Copy)


class Heads:

    def __init__(self, H, D, dv, keys, causal=False):
        self.H, self.D, self.dv, self.causal = H, D, dv, causal
        self.hpc = P // D
        self.chunks = -(-H // self.hpc)
        self.dvp = 32 if dv <= 32 else 64
        self.hps = P // self.dvp
        self.slots = H // self.hps
        self.keys = keys
        self.units = [(qt, h, BANK // keys[qt][1]) for qt in range(2)
                      for h in range(0, H, BANK // keys[qt][1])]
        self.two_banks = self.slots > 4

    def rows(self, c):
        return min(self.hpc, self.H - c * self.hpc) * self.D


def attention_stage(core, ctx, n, hd, steps, epilogue, moments=True,
                    next_weights=(), head_bias=False, ghost=None, weights_of=None, beside=None):
    nc, X, XT = core.nc, core.X, core.XT
    wk = n if weights_of is None else weights_of
    H, dv, dvp, hps, slots, keys, units = hd.H, hd.dv, hd.dvp, hd.hps, hd.slots, hd.keys, hd.units
    U = len(units)
    LT, LV = (3, 5) if U >= 8 else (2, 3)
    LE = LV - 1 if hd.two_banks else LV
    TAIL = LE + (6 if moments else 3)
    per_qt = [sum(1 for u in units if u[0] == qt) for qt in range(2)]
    last_of = [per_qt[0] - 1, U - 1]
    credited = []
    sem = lambda s: new_sem(core, ctx, f"a{n}_{s}", credited)
    mem = ExitStack()
    sb = lambda s, shape, dt=F32: mem.enter_context(nc.sbuf_tensor(f"a{n}_{s}", shape, dt))
    with mem:
        mem.callback(retire, core, credited)
        S0, S1, T0, T1, O0, O1, PRE, EPI = core.bank
        sbank, tbank, obank = [S0, S1], [T0, T1], [O0, O1]
        FIRST = [PRE, EPI, O0, O1]
        B = {}
        B["xs"] = [sb(f"xs{i}", [P, SEQ]) for i in range(2)]
        B["q"] = [sb(f"q{i}", [P, hd.chunks, SEQ]) for i in range(2)]
        B["k"] = sb("k", [P, hd.chunks, SEQ])
        B["kx"] = [sb(f"kx{i}", [P, H, SEQ]) for i in range(2)]
        B["v"] = [sb(f"v{i}", [P, 2, H, dvp]) for i in range(2)]
        masked = hd.causal
        R = 4
        sm = [sb(f"sm{i}", [P, BANK]) for i in range(R)] if masked else None
        pr = [sb(f"pr{i}", [P, BANK]) for i in range(R)]
        pt = [sb(f"pt{i}", [P, BANK]) for i in range(R)]
        top = sb("top", [P, 2, H])
        den = sb("den", [P, 2, H])
        rden = sb("rden", [P, 2, H])
        RX = 1 if masked else 2
        rx = [sb(f"rx{i}", [P, H, dvp]) for i in range(RX)]
        rt = sb("rt", [P, slots, P])
        on = sb("on", [P, slots, P])
        B["bias"] = sb("bias", [P, H, SEQ]) if head_bias else None
        S = {}
        for s in ("x_copied", "step_mm", "step_out", "k_spread", "scores", "masked", "probs", "turned", "turned_out0",
                  "turned_out1", "values", "recip", "repeated", "rep_turned", "rep_out", "normed", "projected",
                  "residual", "stats", "aggregated", "v_zero", "ghosted",
                  "rope_added", "epilogue", "moments_kept"):
            S[s] = sem(s)
        steps.alloc(sb, sem, B, S)
        B["stat"] = sb("stat", [P, 6])
        B["mv"] = sb("mv", [P, 2])
        epilogue.alloc(sb, B)
        if beside:
            beside.alloc(sem, S)
        S["credits"] = sem("credits")
        if head_bias:
            bias_setup_stage(core, ctx, B["bias"][:, :, :])
        ident = core.const("ident")
        causal = core.const("causal")
        hmask = core.const(f"heads{hd.D}")
        NS = steps.count
        NK = steps.kinds.count("k")
        NR = NK + steps.kinds.count("q")
        NB = steps.kinds.index("v")
        EW = 2 if hd.two_banks else 1
        block = mem.enter_context(nc.Block())

        at_slot = [[] for _ in range(U)]
        for j in range(NS):
            at_slot[j * U // NS].append(j)

        def unit_runs(u):
            qt, h0, nh = units[u]
            h = h0
            while h < h0 + nh:
                c = h // hd.hpc
                m = min(h0 + nh, (c + 1) * hd.hpc) - h
                yield h, m, c
                h += m

        def end_of(e):
            return (e // 2) * U + last_of[e % 2]

        def slots_of_pair(eng, slot):
            for s in range(2 * U):
                slot(0, s)
            with eng.Fori(1, BATCH // 2) as i:
                for s in range(2 * U):
                    slot(i, s)
            for s in range(TAIL):
                slot(BATCH // 2, s)

        def lagging(i, s, lag):
            u = s - lag
            if (u >= 0 and in_pair(i, s)) or (u < 0 and not (isinstance(i, int) and i == 0)):
                return [u]
            return []

        def in_pair(i, s):
            return not (isinstance(i, int) and i == BATCH // 2)

        def ending(i, s, lag):
            return [e for e in range(-4, 4) if end_of(e) == s - lag and lagging(i, s, lag)]

        @block.sync
        def _(sp):
            give_credit(sp, credited)
            for k in next_weights:
                load_weights(core, sp, k)

        @block.tensor
        def _(pe):
            pe.wait_ge(core.weights_in[wk], loaded_count(wk))

            def scores(i, s):
                b, u = divmod(s % (2 * U), U)
                qt, h0, nh = units[u]
                k0, kw = keys[qt]
                read = S["masked"] if masked else S["probs"]
                pe.wait_ge(read, total(i, 2 * U, s - 1) + CREDIT)
                if u == 0:
                    pe.wait_ge(S["k_spread"], (2 * i + b + 1) * NK + CREDIT)
                    pe.wait_ge(S["step_out"], (2 * i + b) * NS + NB + CREDIT)
                    if steps.roped:
                        pe.wait_ge(S["rope_added"], (2 * i + b + 1) * NR + CREDIT)
                for h, m, c in unit_runs(u):
                    rows = hd.rows(c)
                    mm = pe.matmul(sbank[s % 2][:, (h - h0) * kw:(h - h0 + m) * kw],
                                   B["q"][b][0:rows, c, qt * P:(qt + 1) * P],
                                   B["kx"][b][0:rows, h:h + m, k0:k0 + kw], start=True, stop=True)
                mm.then_inc(S["scores"], 1)

            def turn(i, s):
                b, u = divmod(s % (2 * U), U)
                pe.wait_ge(S["probs"], i * 2 * U + s + 1 + CREDIT)
                out = S["turned_out%d" % (s % 2)]
                pe.wait_ge(out, i * U + s // 2 + CREDIT)
                for j in range(4):
                    mm = pe.transpose(tbank[s % 2][:, j * P:(j + 1) * P], pr[s % R][:, j * P:(j + 1) * P], ident)
                mm.then_inc(S["turned"], 1)

            def values(i, s):
                b, u = divmod(s % (2 * U), U)
                qt, h0, nh = units[u]
                k0, kw = keys[qt]
                pe.wait_ge(S["turned_out%d" % (s % 2)], i * U + s // 2 + 1 + CREDIT)
                if u == 0:
                    pe.wait_ge(S["step_out"], total(i, 2 * NS, (s // U + 1) * NS) + CREDIT)
                if h0 == 0:
                    e = s // U * 2 + qt
                    pe.wait_ge(S["normed"], total(i, 4, e - (0 if hd.two_banks else 1)) + CREDIT)
                nb = kw // P
                for h in range(h0, h0 + nh):
                    slot, j = divmod(h, hps)
                    ob = obank[slot // 4] if hd.two_banks else obank[qt]
                    o = ob[j * dvp:(j + 1) * dvp, (slot % 4) * P:(slot % 4 + 1) * P]
                    for kb in range(nb):
                        col = ((h - h0) * nb + kb) * P
                        mm = pe.matmul(o, B["v"][b][:, k0 // P + kb, h, :], pt[s % R][:, col:col + P],
                                       start=(kb == 0), stop=(kb == nb - 1))
                mm.then_inc(S["values"], 1)

            def epi_turn(i, e, r):
                ne = (4 * i + e) * EW + r
                if r == 0:
                    pe.wait_ge(S["repeated"], 4 * i + e + 1 + CREDIT)
                    pe.wait_ge(S["residual"], 4 * i + e + CREDIT)
                pe.wait_ge(S["rep_out"], ne + CREDIT)
                for j in range(4):
                    mm = pe.transpose(EPI[:, j * P:(j + 1) * P],
                                      rx[e % RX][:, (r * 4 + j) * hps:(r * 4 + j + 1) * hps, :].rearrange("p a b -> p (a b)"),
                                      ident)
                mm.then_inc(S["rep_turned"], 1)

            def epi_project(i, e):
                pe.wait_ge(S["normed"], 4 * i + e + 1 + CREDIT)
                wo = epilogue.wo
                for j in range(slots):
                    mm = pe.matmul(EPI[:, 0:DM], on[:, j, :], wo[:, j * DM:(j + 1) * DM],
                                   start=(j == 0), stop=(j == slots - 1))
                mm.then_inc(S["projected"], 1)

            def step(i, b, j, first=False):
                seq = 2 * i + b
                pe.wait_ge(S["step_out"], (max(j - len(FIRST) + 1, 0) if first else seq * NS + j) + CREDIT)
                if j == 0:
                    pe.wait_ge(S["x_copied"], seq + 1 + CREDIT)
                steps.pe(pe, core, B, S, FIRST[j % len(FIRST)] if first else PRE, j, b % 2, seq).then_inc(S["step_mm"], 1)

            for j in range(NS):
                step(0, 0, j, True)

            def slot(i, s):
                if in_pair(i, s):
                    scores(i, s)
                for v in lagging(i, s, LT):
                    turn(i, v)
                if in_pair(i, s):
                    for j in at_slot[s % U][:-1]:
                        step(i, s // U + 1, j)
                for v in lagging(i, s, LV):
                    values(i, v)
                for e in ending(i, s, LE + 2):
                    epi_project(i, e)
                for r in range(EW):
                    for e in ending(i, s, LE - (EW - 1 - r)):
                        epi_turn(i, e, r)
                if in_pair(i, s):
                    for j in at_slot[s % U][-1:]:
                        step(i, s // U + 1, j)

            slots_of_pair(pe, slot)

        @block.vector
        def _(dve):
            dve.wait_ge(core.weights_in[wk], loaded_count(wk))
            for b in range(2):
                dve.memset(B["v"][b][:, :, :, :], 0.0).then_inc(S["v_zero"], 1)

            def mask(i, s):
                b, u = divmod(s % (2 * U), U)
                qt, h0, nh = units[u]
                k0, kw = keys[qt]
                dve.wait_ge(S["scores"], i * 2 * U + s + 1 + CREDIT)
                if masked:
                    dve.wait_ge(S["probs"], total(i, 2 * U, s - R + 1) + CREDIT)
                    carry_waits(core, dve)
                    m0 = SEQ - kw
                    for h in range(nh):
                        mk = B["bias"][:, h0 + h, m0:SEQ] if head_bias else causal[:, m0:SEQ]
                        ins = dve.tensor_tensor_reduce(
                            sm[s % R][:, h * kw:(h + 1) * kw], sbank[s % 2][:, h * kw:(h + 1) * kw], mk,
                            1.0, 3.0e38, ALU.add, ALU.min, top[:, qt, h0 + h:h0 + h + 1])
                    ins.then_inc(S["masked"], 1)
                else:
                    dve.tensor_reduce(top[:, qt, h0:h0 + nh],
                                      sbank[s % 2][:, :].rearrange("p (h k) -> p h k", k=kw), AX.X, ALU.min
                                      ).then_inc(S["masked"], 1)

            def turn_out(i, s):
                dve.wait_ge(S["turned"], i * 2 * U + s + 1 + CREDIT)
                dve.wait_ge(S["values"], total(i, 2 * U, s - R + 1) + CREDIT)
                dve.tensor_copy(pt[s % R][:, :], tbank[s % 2][:, :]).then_inc(S["turned_out0"], 1)

            def recip(i, e):
                qt = e % 2
                dve.wait_ge(S["probs"], i * 2 * U + end_of(e) + 1 + CREDIT)
                dve.wait_ge(S["repeated"], total(i, 4, e - 1) + CREDIT)
                if ghost:
                    dve.tensor_tensor(rden[:, qt, :], den[:, qt, :], weight(core, wk, ghost), ALU.add).then_inc(S["ghosted"], 1)
                    dve.wait_ge(S["ghosted"], 4 * i + e + 1 + CREDIT)
                    dve.reciprocal(rden[:, qt, :], rden[:, qt, :]).then_inc(S["recip"], 1)
                else:
                    dve.reciprocal(rden[:, qt, :], den[:, qt, :]).then_inc(S["recip"], 1)

            def norm(i, e):
                qt = e % 2
                dve.wait_ge(S["values"], i * 2 * U + end_of(e) + 1 + CREDIT)
                dve.wait_ge(S["rep_out"], (4 * i + e + 1) * EW + CREDIT)
                dve.wait_ge(S["projected"], 4 * i + e + CREDIT)
                if hd.two_banks:
                    for r in range(2):
                        ins = dve.tensor_tensor(on[:, 4 * r:4 * r + 4, :].rearrange("p a b -> p (a b)"),
                                                obank[r][:, :], rt[:, 4 * r:4 * r + 4, :].rearrange("p a b -> p (a b)"),
                                                ALU.mult)
                else:
                    ins = dve.tensor_tensor(on[:, :, :].rearrange("p a b -> p (a b)"), obank[qt][:, :],
                                            rt[:, :, :].rearrange("p a b -> p (a b)"), ALU.mult)
                ins.then_inc(S["normed"], 1)

            def residual(i, e):
                t = 4 * i + e
                dve.wait_ge(S["projected"], 4 * i + e + 1 + CREDIT)
                xt = X[:, bass.ds(t, 1), :].rearrange("p t d -> p (t d)")
                epilogue.dve(dve, core, B, S, i, e, xt, EPI[:, 0:DM])

            def tile_stats(i, e):
                t = 4 * i + e
                dve.wait_ge(S["residual"], t + 1 + CREDIT)
                dve.wait_ge(S["moments_kept"], t + CREDIT)
                carry_waits(core, dve)
                dve.bn_stats(B["stat"][:, :], joined(X[:, bass.ds(t, 1), :])).then_inc(S["stats"], 1)

            def tile_aggregate(i, e):
                dve.wait_ge(S["stats"], 4 * i + e + 1 + CREDIT)
                carry_waits(core, dve)
                dve.bn_aggr(B["mv"][:, :], B["stat"][:, :]).then_inc(S["aggregated"], 1)

            def keep_moments(i, e):
                t = 4 * i + e
                dve.wait_ge(S["aggregated"], t + 1 + CREDIT)
                dve.tensor_copy(joined(core.mv[:, bass.ds(t, 1), :]), B["mv"][:, :]).then_inc(S["moments_kept"], 1)

            def step(i, b, j, first=False):
                seq = 2 * i + b
                if steps.engine[j] == "dve":
                    dve.wait_ge(S["step_mm"], seq * NS + j + 1 + CREDIT)
                    if first and steps.engine[j - 1] == "act":
                        dve.wait_ge(S["step_out"], j + CREDIT)
                    if steps.kinds[j] == "v":
                        dve.wait_ge(S["v_zero"], 2 + CREDIT)
                        dve.wait_ge(S["values"], total(i, 2 * U, (b - 1) * U) + CREDIT)
                    if steps.kinds[j] == "k" and not steps.roped:
                        dve.wait_ge(S["k_spread"], seq * NK + CREDIT)
                    if steps.roped and steps.kinds[j] in "qk":
                        dve.wait_ge(S["rope_added"], seq * NR + max(steps.rank(j) - 1, 0) + CREDIT)
                    steps.dve(dve, core, B, S, FIRST[j % len(FIRST)] if first else PRE, j, b % 2, seq).then_inc(S["step_out"], 1)

            steps.before(dve, core, B, S)
            for j in range(NS):
                step(0, 0, j, True)

            def slot(i, s):
                if in_pair(i, s):
                    mask(i, s)
                    if beside and beside.has(i, s):
                        beside.dve(dve, S, i, s)
                if in_pair(i, s):
                    for j in at_slot[s % U][:-1]:
                        step(i, s // U + 1, j)
                for v in lagging(i, s, LT):
                    if v % 2 == 0:
                        turn_out(i, v)
                for e in ending(i, s, 1):
                    recip(i, e)
                if moments:
                    for e in ending(i, s, LE + 5):
                        keep_moments(i, e)
                    for e in ending(i, s, LE + 4):
                        tile_aggregate(i, e)
                    for e in ending(i, s, LE + 3):
                        tile_stats(i, e)
                for e in ending(i, s, LE + 2):
                    residual(i, e)
                for e in ending(i, s, LE + 1):
                    norm(i, e)
                if in_pair(i, s):
                    for j in at_slot[s % U][-1:]:
                        step(i, s // U + 1, j)

            slots_of_pair(dve, slot)

        @block.scalar
        def _(act):
            if beside:
                beside.preload(nc)
            act.wait_ge(core.weights_in[wk], loaded_count(wk))

            def probs(i, s):
                b, u = divmod(s % (2 * U), U)
                qt, h0, nh = units[u]
                k0, kw = keys[qt]
                act.wait_ge(S["masked"], i * 2 * U + s + 1 + CREDIT)
                act.wait_ge(S["turned"], total(i, 2 * U, s - R + 1) + CREDIT)
                if u in (0, per_qt[0]):
                    e = s // U * 2 + qt
                    act.wait_ge(S["recip"], total(i, 4, e - 1) + CREDIT)
                src = sm[s % R] if masked else sbank[s % 2]
                for h in range(nh):
                    ins = act.activation(pr[s % R][:, h * kw:(h + 1) * kw], src[:, h * kw:(h + 1) * kw], ACT.Exp,
                                         bias=top[:, qt, h0 + h:h0 + h + 1], scale=-1.0,
                                         accum_out=den[:, qt, h0 + h:h0 + h + 1])
                ins.then_inc(S["probs"], 1)

            def turn_out(i, s):
                act.wait_ge(S["turned"], i * 2 * U + s + 1 + CREDIT)
                act.wait_ge(S["values"], total(i, 2 * U, s - R + 1) + CREDIT)
                act.activation(pt[s % R][:, :], tbank[s % 2][:, :], ACT.Copy).then_inc(S["turned_out1"], 1)

            def rep_out(i, e, r):
                act.wait_ge(S["rep_turned"], (4 * i + e) * EW + r + 1 + CREDIT)
                if r == 0:
                    act.wait_ge(S["normed"], 4 * i + e + CREDIT)
                act.activation(rt[:, 4 * r:4 * r + 4, :].rearrange("p a b -> p (a b)"), EPI[:, :],
                               ACT.Copy).then_inc(S["rep_out"], 1)

            def step(i, b, j, first=False):
                seq = 2 * i + b
                if steps.engine[j] == "act":
                    act.wait_ge(S["step_mm"], seq * NS + j + 1 + CREDIT)
                    if steps.kinds[j] == "k":
                        act.wait_ge(S["k_spread"], seq * NK + CREDIT)
                    steps.act(act, core, B, S, FIRST[j % len(FIRST)] if first else PRE, j, b % 2, seq).then_inc(S["step_out"], 1)

            for j in range(NS):
                step(0, 0, j, True)

            def slot(i, s):
                if in_pair(i, s):
                    probs(i, s)
                    if beside and beside.has(i, s):
                        beside.act(act, S, i, s)
                if in_pair(i, s):
                    for j in at_slot[s % U][:-1]:
                        step(i, s // U + 1, j)
                for v in lagging(i, s, LT):
                    if v % 2 == 1:
                        turn_out(i, v)
                for r in range(EW):
                    for e in ending(i, s, LE - (EW - 1 - r)):
                        rep_out(i, e, r)
                if in_pair(i, s):
                    for j in at_slot[s % U][-1:]:
                        step(i, s // U + 1, j)

            slots_of_pair(act, slot)

        @block.gpsimd
        def _(pool):
            def copy_x(i, b):
                seq = 2 * i + b
                pool.wait_ge(S["step_mm"], total(i, 2 * NS, (b - 1) * NS) + CREDIT)
                carry_waits(core, pool)
                steps.copy_x(pool, core, B, S, b % 2, seq)
                pool.tensor_copy(B["xs"][b % 2][:, :], XT[:, bass.ds(seq * SEQ, SEQ)]).then_inc(S["x_copied"], 1)

            def step(i, b, j):
                seq = 2 * i + b
                kind = steps.kinds[j]
                if kind not in "qk":
                    return
                c0, c1 = steps.chunks_of[j]
                if steps.roped:
                    r = steps.rank(j)
                    rows = hd.rows(c0)
                    pool.wait_ge(S["step_out"], seq * NS + j + 1 + CREDIT)
                    dst = (B["q"][b % 2] if kind == "q" else B["k"])[0:rows, c0, :]
                    if kind == "k":
                        pool.wait_ge(S["k_spread"], seq * NK + CREDIT)
                    tt = B["tt"][j % 2]
                    pool.tensor_tensor(dst, tt[0:rows, 0, :], tt[0:rows, 1, :], ALU.add).then_inc(S["rope_added"], 1)
                if kind == "k":
                    if steps.roped:
                        pool.wait_ge(S["rope_added"], seq * NR + r + 1 + CREDIT)
                    else:
                        pool.wait_ge(S["step_out"], seq * NS + j + 1 + CREDIT)
                    for c in range(c0, c1):
                        a, z, rows = c * hd.hpc, min(H, (c + 1) * hd.hpc), hd.rows(c)
                        ins = pool.tensor_tensor(
                            B["kx"][b % 2][0:rows, a:z, :],
                            B["k"][0:rows, c:c + 1, :].to_broadcast([rows, z - a, SEQ]),
                            hmask[0:rows, 0:z - a].unsqueeze(2).to_broadcast([rows, z - a, SEQ]), ALU.mult)
                    ins.then_inc(S["k_spread"], 1)

            def repeat(i, e):
                pool.wait_ge(S["recip"], 4 * i + e + 1 + CREDIT)
                pool.wait_ge(S["rep_turned"], total(i, 4 * EW, (e - RX + 1) * EW) + CREDIT)
                carry_waits(core, pool)
                pool.tensor_copy(rx[e % RX][:, :, :], rden[:, e % 2, :].unsqueeze(2).to_broadcast([P, H, dvp])
                                 ).then_inc(S["repeated"], 1)

            pool.wait_ge(credited[-1], CREDIT)
            copy_x(0, 0)
            copy_x(0, 1)
            for j in range(NS):
                step(0, 0, j)

            def slot(i, s):
                for e in ending(i, s, 1):
                    repeat(i, e)
                if in_pair(i, s):
                    b, u = divmod(s, U)
                    for j in at_slot[u]:
                        step(i, b + 1, j)
                    if u == U // 2:
                        copy_x(i, b + 2)

            slots_of_pair(pool, slot)


def total(i, each, k):
    return max(i * each + k, 0) if isinstance(i, int) else i * each + k


def joined(ap):
    return ap.rearrange("p t d -> p (t d)")


class Steps:

    roped = False

    def alloc(self, sb, sem, B, S):
        if self.roped:
            B["tt"] = [sb(f"tt{i}", [P, 2, SEQ]) for i in range(2)]

    def before(self, dve, core, B, S):
        pass

    def copy_x(self, pool, core, B, S, b, seq):
        pass

    @property
    def count(self):
        return len(self.kinds)

    def rank(self, j):
        return sum(1 for k in self.kinds[:j] if k in "qk")


def value_out(dve, B, PRE, b, dv, H):
    return dve.tensor_copy(B["v"][b][:, :, :, 0:dv], PRE[:, 0:2 * H * dv].rearrange("p (t h d) -> p t h d", t=2, h=H))


class RotarySteps(Steps):

    roped = True

    def __init__(self, stage):
        self.kinds = ["q", "k", "v"]
        self.engine = ["dve"] * 3
        self.chunks_of = [(0, 1), (0, 1), None]
        self.stage = stage

    def pe(self, pe, core, B, S, PRE, j, b, seq):
        w = lambda s: weight(core, self.stage, s)
        if self.kinds[j] in "qk":
            k = self.kinds[j]
            pe.matmul(PRE[:, 0:SEQ], w(f"l1_w{k}"), B["xs"][b][:, :], start=True, stop=True)
            return pe.matmul(PRE[:, SEQ:2 * SEQ], w(f"l1_w{k}rot"), B["xs"][b][:, :], start=True, stop=True)
        for t in range(2):
            mm = pe.matmul(PRE[:, t * P:(t + 1) * P], B["xs"][b][:, t * P:(t + 1) * P], w("l1_wv"), start=True, stop=True)
        return mm

    def dve(self, dve, core, B, S, PRE, j, b, seq):
        if self.kinds[j] in "qk":
            table = core.const("rope8" + self.kinds[j])
            return dve.tensor_tensor(B["tt"][j % 2][:, :, :].rearrange("p a b -> p (a b)"), PRE[:, :], table, ALU.mult)
        return value_out(dve, B, PRE, b, 8, 16)


class Epilogue:

    def __init__(self, wo):
        self.wo = wo

    def alloc(self, sb, B):
        pass

    def dve(self, dve, core, B, S, i, e, xt, y):
        dve.tensor_tensor(xt, y, xt, ALU.add).then_inc(S["residual"], 1)


def bias_setup_stage(core, ctx, bias):
    nc = core.nc
    credited = []
    sem = lambda s: new_sem(core, ctx, f"bias_{s}", credited)
    rows_mm, rows_out, rows_stored, bias_in = sem("rows_mm"), sem("rows_out"), sem("rows_stored"), sem("loaded")
    flip_mm, flip_out = sem("flip_mm"), sem("flip_out")
    scratch = nc.dram_tensor("bias_rows", (16, 383), F32, kind="Internal").ap()
    with ExitStack() as mem:
        mem.callback(retire, core, credited)
        rows = mem.enter_context(nc.sbuf_tensor("bias_rows_sb", [16, 383], F32))
        block = mem.enter_context(nc.Block())

        @block.tensor
        def _(pe):
            pe.wait_ge(core.weights_in[2], loaded_count(2))
            pe.matmul(core.bank[2][0:16, 0:383], weight(core, 2, "l1_rel"), core.const("bucket", 32),
                      start=True, stop=True).then_inc(rows_mm, 1)
            pe.wait_ge(bias_in, 16 + CREDIT)
            for g in range(8):
                if g >= 2:
                    pe.wait_ge(flip_out, g - 1 + CREDIT)
                pe.matmul(core.bank[g % 2][:, :], core.const("flip"), bias[:, 2 * g:2 * g + 2, :],
                          start=True, stop=True).then_inc(flip_mm, 1)

        @block.vector
        def _(dve):
            dve.wait_ge(rows_mm, 1 + CREDIT)
            dve.scalar_tensor_tensor(rows[:, :], core.bank[2][0:16, 0:383], -1.0, core.const("future", 16),
                                     ALU.mult, ALU.add).then_inc(rows_out, 1)

        @block.sync
        def _(sp):
            give_credit(sp, credited)
            sp.wait_ge(rows_out, 1 + CREDIT)
            sp.dma_start(scratch, rows[:, :]).then_inc(rows_stored, 16)
            sp.wait_ge(rows_stored, 16 + CREDIT)
            window = bass.AP(scratch.tensor, 0, [[1, P], [383, 16], [1, SEQ]])
            sp.dma_start(bias, window).then_inc(bias_in, 16)

        @block.scalar
        def _(act):
            for g in range(8):
                act.wait_ge(flip_mm, g + 1 + CREDIT)
                act.activation(bias[:, 2 * g:2 * g + 2, :].rearrange("p h c -> p (h c)"), core.bank[g % 2][:, :],
                               ACT.Copy).then_inc(flip_out, 1)


def l1_attention(core, ctx, next_weights=()):
    hd = Heads(16, 8, 8, [(0, P), (0, SEQ)], causal=True)
    attention_stage(core, ctx, 2, hd, RotarySteps(2), Epilogue(weight(core, 2, "l1_wo")),
                    next_weights=next_weights, head_bias=True)


class PlainSteps(Steps):

    def __init__(self, stage, names, width, vwidth, dv, scale, biases=None, value_scale=None):
        self.stage, self.names, self.scale, self.biases = stage, names, scale, biases
        n = width // P // 2
        nv = 1 if 2 * vwidth <= BANK else 2 * vwidth // BANK
        self.nv, self.dv, self.vwidth, self.value_scale = nv, dv, vwidth, value_scale
        self.kinds = ["q"] * n + ["k"] * n + ["v"] * nv
        self.engine = ["act"] * n + ["act"] * n + ["dve"] * nv
        self.chunks_of = [(2 * j, 2 * j + 2) for j in range(n)] * 2 + [None] * nv

    def alloc(self, sb, sem, B, S):
        if self.biases:
            B["nbq"] = sb("nbq", [P, 8])
            S["bias_scaled"] = sem("bias_scaled")

    def before(self, dve, core, B, S):
        if self.biases:
            dve.tensor_scalar(B["nbq"][:, :], weight(core, self.stage, self.biases[0]), self.scale, None,
                              ALU.mult).then_inc(S["bias_scaled"], 1)

    def pe(self, pe, core, B, S, PRE, j, b, seq):
        kind = self.kinds[j]
        w = weight(core, self.stage, self.names["qkv".index(kind)])
        if kind in "qk":
            c0, c1 = self.chunks_of[j]
            for c in (c0, c0 + 1):
                mm = pe.matmul(PRE[:, (c - c0) * SEQ:(c - c0 + 1) * SEQ], w[:, c * P:(c + 1) * P], B["xs"][b][:, :],
                               start=True, stop=True)
            return mm
        r = j - self.kinds.index("v")
        if self.nv == 1:
            for t in range(2):
                mm = pe.matmul(PRE[:, t * self.vwidth:(t + 1) * self.vwidth], B["xs"][b][:, t * P:(t + 1) * P],
                               w, start=True, stop=True)
            return mm
        per = self.nv // 2
        t, part = divmod(r, per)
        return pe.matmul(PRE[:, :], B["xs"][b][:, t * P:(t + 1) * P], w[:, part * BANK:(part + 1) * BANK],
                         start=True, stop=True)

    def act(self, act, core, B, S, PRE, j, b, seq):
        c0, c1 = self.chunks_of[j]
        q = self.kinds[j] == "q"
        dst = B["q"][b] if q else B["k"]
        if not self.biases:
            return act.activation(dst[:, c0:c1, :].rearrange("p c t -> p (c t)"), PRE[:, :], ACT.Copy,
                                  scale=self.scale if q else 1.0)
        act.wait_ge(S["bias_scaled"], 1 + CREDIT)
        for c in range(c0, c1):
            bias = B["nbq"][:, c:c + 1] if q else weight(core, self.stage, self.biases[1])[:, c:c + 1]
            ins = act.activation(dst[:, c, :], PRE[:, (c - c0) * SEQ:(c - c0 + 1) * SEQ], ACT.Identity,
                                 bias=bias, scale=self.scale if q else 1.0)
        return ins

    def dve(self, dve, core, B, S, PRE, j, b, seq):
        H = self.vwidth // self.dv
        if self.nv == 1:
            return value_out(dve, B, PRE, b, self.dv, H)
        r = j - self.kinds.index("v")
        per = self.nv // 2
        t, part = divmod(r, per)
        h0, h1 = part * BANK // self.dv, (part + 1) * BANK // self.dv
        dst = B["v"][b][:, t, h0:h1, :].rearrange("p h d -> p (h d)")
        if self.biases:
            bv = weight(core, self.stage, self.biases[2])[:, part * BANK:(part + 1) * BANK]
            return dve.tensor_tensor(dst, PRE[:, :], bv, ALU.add)
        if self.value_scale is not None:
            return dve.tensor_scalar(dst, PRE[:, :], self.value_scale[:, bass.ds(seq, 1), t], None, ALU.mult)
        return dve.tensor_copy(dst, PRE[:, :])


def l2_attention(core, ctx, next_weights=()):
    hd = Heads(16, 16, 16, [(0, P), (0, SEQ)], causal=True)
    steps = PlainSteps(4, ("l2_wq", "l2_wk", "l2_wv"), 256, 256, 16, -1.0 / math.sqrt(8.0))
    attention_stage(core, ctx, 4, hd, steps, Epilogue(weight(core, 4, "l2_wo")), next_weights=next_weights)


class BiasedEpilogue(Epilogue):

    def __init__(self, wo, bo):
        self.wo, self.bo = wo, bo

    def alloc(self, sb, B):
        B["yb"] = sb("yb", [P, DM])

    def dve(self, dve, core, B, S, i, e, xt, y):
        dve.tensor_tensor(B["yb"][:, :], y, self.bo, ALU.add).then_inc(S["epilogue"], 1)
        dve.wait_ge(S["epilogue"], 4 * i + e + 1 + CREDIT)
        dve.tensor_tensor(xt, B["yb"][:, :], xt, ALU.add).then_inc(S["residual"], 1)


def l3_attention(core, ctx, next_weights=()):
    hd = Heads(16, 64, 64, [(0, P), (0, SEQ)], causal=True)
    steps = PlainSteps(6, ("l3_wq", "l3_wk", "l3_wv"), 1024, 1024, 64, -1.0 / 8.0, biases=("l3_bq", "l3_bk", "l3_bv"))
    attention_stage(core, ctx, 6, hd, steps, BiasedEpilogue(weight(core, 6, "l3_wo"), weight(core, 6, "l3_bo")),
                    next_weights=next_weights, ghost="l3_ghost")


class LatentSteps(Steps):

    roped = True

    def __init__(self, rkv, F):
        self.kinds = ["pre"] + ["q"] * 6 + ["k"] * 6 + ["v"]
        self.engine = ["dve"] * 14
        self.chunks_of = [None] + [(c, c + 1) for c in range(6)] * 2 + [None]
        self.rkv, self.F = rkv, F

    def alloc(self, sb, sem, B, S):
        Steps.alloc(self, sb, sem, B, S)
        B["rms_diagonal"] = [sb(f"rms_diagonal{i}", [P, 2, P]) for i in range(2)]
        B["table"] = [sb(f"table{i}", [P, 2 * SEQ]) for i in range(2)]
        S["diagonal"] = sem("diagonal")
        S["sines"] = sem("sines")

    def before(self, dve, core, B, S):
        for b in range(2):
            dve.tensor_copy(B["table"][b][:, SEQ:], core.const("rope40k")[:, SEQ:]).then_inc(S["sines"], 1)

    def copy_x(self, pool, core, B, S, b, seq):
        two = [P, 2, P]
        pool.tensor_tensor(B["rms_diagonal"][b][:, :, :], over(core.const("ident"), two, 1),
                           over(self.rkv[:, bass.ds(seq * 2, 2)], two, 2), ALU.mult).then_inc(S["diagonal"], 1)

    def pe(self, pe, core, B, S, PRE, j, b, seq):
        kind = self.kinds[j]
        if kind == "pre":
            pe.wait_ge(S["diagonal"], seq + 1 + CREDIT)
            return pe.matmul(PRE[:, 0:SEQ], core.const("content40"), B["rms_diagonal"][b][:, :, :], start=True, stop=True)
        if kind == "v":
            for t in range(2):
                mm = pe.matmul(PRE[:, t * P:(t + 1) * P], B["xs"][b][:, t * P:(t + 1) * P], self.F["v"][:, :],
                               start=True, stop=True)
            return mm
        c = self.chunks_of[j][0]
        a, z = c * 120, min(640, (c + 1) * 120)
        m = z - a
        if m <= 64:
            carry_waits(core, pe)
        rot = self.F["qrot"][:, a:z] if kind == "q" else weight(core, 0, "l0_wkrot")[:, a:z]
        pe.matmul(PRE[0:m, 0:SEQ], self.F[kind][:, a:z], B["xs"][b][:, :], start=True, stop=True)
        return pe.matmul(PRE[0:m, SEQ:2 * SEQ], rot, B["xs"][b][:, :], start=True, stop=True)

    def dve(self, dve, core, B, S, PRE, j, b, seq):
        kind = self.kinds[j]
        if kind == "pre":
            return dve.tensor_tensor(B["table"][b][:, 0:SEQ], PRE[:, 0:SEQ], core.const("rope40k")[:, 0:SEQ], ALU.add)
        if kind == "v":
            for t in range(2):
                ins = dve.tensor_scalar(B["v"][b][:, t, :, 0:8], PRE[:, t * P:(t + 1) * P].rearrange("p (h d) -> p h d", d=8),
                                        self.rkv[:, bass.ds(seq * 2 + t, 1)], None, ALU.mult)
            return ins
        c = self.chunks_of[j][0]
        m = min(640, (c + 1) * 120) - c * 120
        if kind == "k":
            dve.wait_ge(S["sines"], 2 + CREDIT)
            dve.wait_ge(S["step_out"], seq * self.count + 1 + CREDIT)
        table = B["table"][b][0:m, :] if kind == "k" else core.const("rope40q", m)
        return dve.tensor_tensor(B["tt"][j % 2][0:m, :, :].rearrange("p a b -> p (a b)"), PRE[0:m, :], table, ALU.mult)


def fold_stage(core, ctx, F):
    nc, bank = core.nc, core.bank
    credited = []
    sem = lambda s: new_sem(core, ctx, f"fold_{s}", credited)
    gained, products, out = sem("gained"), sem("products"), sem("out")
    w = lambda s: weight(core, 0, s)
    with ExitStack() as mem:
        mem.callback(retire, core, credited)
        kdec = mem.enter_context(nc.sbuf_tensor("fold_kdec", [32, 640], F32))
        vdec = mem.enter_context(nc.sbuf_tensor("fold_vdec", [32, P], F32))
        HALVES = ((0, BANK), (BANK, 640))
        block = mem.enter_context(nc.Block())

        @block.sync
        def _(sp):
            give_credit(sp, credited)

        @block.tensor
        def _(pe):
            pe.wait_ge(core.weights_in[0], loaded_count(0))
            pe.wait_ge(gained, 2 + CREDIT)
            for n, (first, second) in enumerate(((w("l0_wqT"), w("l0_wqall")), (w("l0_wqT"), w("l0_wqrot")),
                                                 (w("l0_wkvT"), kdec[:, :]))):
                for h, (a, z) in enumerate(HALVES):
                    mm = pe.matmul(bank[2 * n + h][:, 0:z - a], first, second[:, a:z], start=True, stop=True)
            pe.matmul(bank[6][:, 0:P], w("l0_wkvT"), vdec[:, :], start=True, stop=True).then_inc(products, 1)

        @block.vector
        def _(dve):
            dve.wait_ge(core.weights_in[0], loaded_count(0))
            dve.tensor_scalar(kdec[:, :], w("l0_wkdec"), w("l0_gkv"), None, ALU.mult).then_inc(gained, 1)
            dve.tensor_scalar(vdec[:, :], w("l0_wvdec"), w("l0_gkv"), None, ALU.mult).then_inc(gained, 1)
            dve.wait_ge(products, 1 + CREDIT)
            for h, (a, z) in enumerate(HALVES):
                dve.tensor_copy(F["q"][:, a:z], bank[h][:, 0:z - a])
                dve.tensor_copy(F["qrot"][:, a:z], bank[2 + h][:, 0:z - a])
                dve.tensor_tensor(F["k"][:, a:z], bank[4 + h][:, 0:z - a], w("l0_wkrope")[:, a:z], ALU.add)
            dve.tensor_copy(F["v"][:, :], bank[6][:, 0:P])


def latent_stage(core, ctx, KV, rkv):
    nc = core.nc
    credited = []
    sem = lambda s: new_sem(core, ctx, f"kv_{s}", credited)
    x_copied, kv_mm, kv_out, squared, mean_ready, std_ready, rkv_ready, pad_zero = (
        sem("x_copied"), sem("mm"), sem("out"), sem("squared"), sem("mean"), sem("std"), sem("rkv"), sem("pad_zero"))
    with ExitStack() as mem:
        mem.callback(retire, core, credited)
        xs = [mem.enter_context(nc.sbuf_tensor(f"kv_xs{i}", [P, SEQ], F32)) for i in range(2)]
        sq = mem.enter_context(nc.sbuf_tensor("kv_sq", [P, 2, 32], F32))
        std = mem.enter_context(nc.sbuf_tensor("kv_std", [P, TILES], F32))
        block = mem.enter_context(nc.Block())

        @block.sync
        def _(sp):
            give_credit(sp, credited)

        @block.gpsimd
        def _(pool):
            pool.memset(KV[:, TILES:, :], 0.0).then_inc(pad_zero, 1)
            pool.memset(rkv[:, TILES:], 0.0).then_inc(pad_zero, 1)
            with pool.Fori(0, BATCH // 2) as i:
                for b in range(2):
                    pool.wait_ge(kv_mm, 2 * i + CREDIT)
                    carry_waits(core, pool)
                    pool.tensor_copy(xs[b][:, :], core.XT[:, bass.ds((2 * i + b) * SEQ, SEQ)]).then_inc(x_copied, 1)

        @block.tensor
        def _(pe):
            pe.wait_ge(core.weights_in[0], loaded_count(0))
            with pe.Fori(0, BATCH // 2) as i:
                for b in range(2):
                    pe.wait_ge(x_copied, 2 * i + b + 1 + CREDIT)
                    pe.wait_ge(kv_out, 2 * i + CREDIT)
                    for t in range(2):
                        mm = pe.matmul(core.bank[b][:, t * 32:(t + 1) * 32], xs[b][:, t * P:(t + 1) * P],
                                       weight(core, 0, "l0_wkv"), start=True, stop=True)
                    mm.then_inc(kv_mm, 1)

        @block.vector
        def _(dve):
            with dve.Fori(0, BATCH // 2) as i:
                for b in range(2):
                    s = 2 * i + b
                    dve.wait_ge(kv_mm, s + 1 + CREDIT)
                    dst = KV[:, bass.ds(2 * s, 2), :]
                    dve.tensor_copy(dst, core.bank[b][:, 0:64].rearrange("p (t r) -> p t r", t=2)).then_inc(kv_out, 1)
                    dve.wait_ge(kv_out, s + 1 + CREDIT)
                    dve.wait_ge(squared, s + CREDIT)
                    dve.tensor_tensor(sq[:, :, :], dst, dst, ALU.mult).then_inc(mean_ready, 1)
                    dve.wait_ge(mean_ready, s + 1 + CREDIT)
                    dve.tensor_reduce(rkv[:, bass.ds(2 * s, 2)], sq[:, :, :], AX.X, ALU.add).then_inc(squared, 1)
            dve.wait_ge(squared, BATCH + CREDIT)
            dve.tensor_scalar(rkv[:, 0:TILES], rkv[:, 0:TILES], 1.0 / 32, 1e-6, ALU.mult, ALU.add).then_inc(mean_ready, 1)
            dve.wait_ge(std_ready, 1 + CREDIT)
            dve.reciprocal(rkv[:, 0:TILES], std[:, :]).then_inc(rkv_ready, 1)

        @block.scalar
        def _(act):
            act.wait_ge(mean_ready, BATCH + 1 + CREDIT)
            act.activation(std[:, :], rkv[:, 0:TILES], ACT.Sqrt).then_inc(std_ready, 1)


def l0_attention(core, ctx, next_weights=()):
    with ExitStack() as mem:
        KV = mem.enter_context(core.nc.sbuf_tensor("KV", [P, TILES + 4, 32], F32))
        rkv = mem.enter_context(core.nc.sbuf_tensor("rkv", [P, TILES + 4], F32))
        F = {s: mem.enter_context(core.nc.sbuf_tensor(f"folded_{s}", [P, n], F32))
             for s, n in (("q", 640), ("qrot", 640), ("k", 640), ("v", P))}
        fold_stage(core, ctx, F)
        latent_stage(core, ctx, KV, rkv)
        hd = Heads(16, 40, 8, [(0, P), (0, SEQ)], causal=True)
        attention_stage(core, ctx, 0, hd, LatentSteps(rkv, F), Epilogue(weight(core, 0, "l0_wo")),
                        next_weights=next_weights)


def over(ap, shape, axis):
    return ap.unsqueeze(axis).to_broadcast(shape)


def gate_stage(core, ctx, n, w, m, dve_part, act_part, outs, setup=None):
    nc = core.nc
    credited = []
    sem = lambda s: new_sem(core, ctx, f"g{n}_{s}", credited)
    logits_mm, logits_out, logits_turned, dve_done, act_done, ready, turned, turned_out, extra = [
        sem(s) for s in ("logits_mm", "logits_out", "logits_turned", "dve_done", "act_done", "ready", "turned",
                         "turned_out", "extra")]
    GR = TOK // BANK
    with ExitStack() as mem:
        mem.callback(retire, core, credited)
        LT = mem.enter_context(nc.sbuf_tensor(f"g{n}_LT", [m, TOK], F32))
        sb = lambda s, shape, dt=F32: mem.enter_context(nc.sbuf_tensor(f"g{n}_{s}", shape, dt))
        B = {"logits": core.bank[0][:, 0:TILES * m].rearrange("p (t e) -> p t e", e=m), "sb": sb}
        if setup:
            setup(B)
        ident = core.const("ident")
        block = mem.enter_context(nc.Block())

        @block.sync
        def _(sp):
            give_credit(sp, credited)

        @block.tensor
        def _(pe):
            pe.wait_ge(core.weights_in[n], loaded_count(n))
            pe.wait_ge(credited[-1], CREDIT)
            for g in range(GR):
                pe.matmul(core.bank[g][0:m, :], w, core.XT[:, g * BANK:(g + 1) * BANK],
                          start=True, stop=True).then_inc(logits_mm, 1)
            pe.wait_ge(logits_out, GR + CREDIT)
            for t in range(TILES):
                mm = pe.transpose(core.bank[0][:, t * m:(t + 1) * m], LT[:, t * P:(t + 1) * P], ident[0:m, 0:m])
            mm.then_inc(logits_turned, 1)
            if "pe" in B:
                B["pe"](pe, extra)
            for j, (nat, dst) in enumerate(outs):
                r = nat.shape[2]
                pe.wait_ge(ready, j + 1 + CREDIT)
                for g in range(GR):
                    if j:
                        pe.wait_ge(turned_out, (j - 1) * GR + g + 1 + CREDIT)
                    for t in range(4):
                        mm = pe.transpose(core.bank[g][0:r, t * P:(t + 1) * P], nat[:, g * 4 + t, :], ident)
                    mm.then_inc(turned, 1)

        @block.vector
        def _(dve):
            dve.wait_ge(core.weights_in[n], loaded_count(n))
            dve.wait_ge(logits_turned, 1 + CREDIT)
            dve_done_so_far = counter(CREDIT)
            dve_part(dve, core, B, dve_done, dve_done_so_far, act_done, ready, extra)

        @block.scalar
        def _(act):
            for g in range(GR):
                act.wait_ge(logits_mm, g + 1 + CREDIT)
                act.activation(LT[:, g * BANK:(g + 1) * BANK], core.bank[g][0:m, :], ACT.Copy).then_inc(logits_out, 1)
            act_part(act, core, B, dve_done, act_done)
            for j, (nat, dst) in enumerate(outs):
                r = nat.shape[2]
                for g in range(GR):
                    act.wait_ge(turned, j * GR + g + 1 + CREDIT)
                    act.activation(dst[:, g * BANK:(g + 1) * BANK], core.bank[g][0:r, :], ACT.Copy
                                   ).then_inc(turned_out, 1)


def top_entries(dve, B, dve_done, dve_done_so_far, scores, TE):
    for t in range(TILES):
        ins = dve.max(B["vals"][:, t, :], scores[:, t, :])
    ins.then_inc(dve_done, 1)
    dve.wait_ge(dve_done, dve_done_so_far())
    for t in range(TILES):
        ins = dve.max_index(B["idx"][:, t, :], B["vals"][:, t, :], scores[:, t, :])
    ins.then_inc(dve_done, 1)
    dve.wait_ge(dve_done, dve_done_so_far())
    dve.tensor_copy(B["idxf"][:, :, :], B["idx"][:, :, :]).then_inc(dve_done, 1)
    dve.wait_ge(dve_done, dve_done_so_far())


def group_moments(dve, core, B, G, sems):
    stats, aggregated, kept = sems
    dve.wait_ge(kept, G + CREDIT)
    carry_waits(core, dve)
    for t in range(4):
        ins = dve.bn_stats(B["stat"][:, t, :], joined(core.X[:, bass.ds(4 * G + t, 1), :]))
    ins.then_inc(stats, 1)
    dve.wait_ge(stats, G + 1 + CREDIT)
    carry_waits(core, dve)
    for t in range(4):
        ins = dve.bn_aggr(B["mv"][:, t, :], B["stat"][:, t, :])
    ins.then_inc(aggregated, 1)
    dve.wait_ge(aggregated, G + 1 + CREDIT)
    dve.tensor_copy(core.mv[:, bass.ds(4 * G, 4), :], B["mv"][:, :, :]).then_inc(kept, 1)


SH = [P, TILES, 8]


def l0_gates(core, ctx, gates, gatesT):
    def setup(B):
        for s in ("lg", "vals", "idxf", "one", "two"):
            B[s] = B["sb"](s, SH)
        B["idx"] = B["sb"]("idx", SH, U32)
        for s in ("d", "e", "den", "p1", "p2"):
            B[s] = B["sb"](s, [P, TILES])

    def dve_part(dve, core, B, dve_done, dve_done_so_far, act_done, ready, extra):
        iota = core.const("iota8")
        rb = weight(core, 1, "l0_rb")
        dve.tensor_tensor(B["lg"][:, :, :], B["logits"], over(rb, SH, 1), ALU.add).then_inc(dve_done, 1)
        dve.wait_ge(dve_done, dve_done_so_far())
        top_entries(dve, B, dve_done, dve_done_so_far, B["lg"], 8)
        dve.tensor_tensor(B["d"][:, :], B["vals"][:, :, 1], B["vals"][:, :, 0], ALU.subtract).then_inc(dve_done, 1)
        dve.wait_ge(dve_done, dve_done_so_far())
        dve.tensor_tensor(B["one"][:, :, :], over(iota, SH, 1), over(B["idxf"][:, :, 0], SH, 2), ALU.is_equal).then_inc(dve_done, 1)
        dve.wait_ge(dve_done, dve_done_so_far())
        dve.tensor_tensor(B["two"][:, :, :], over(iota, SH, 1), over(B["idxf"][:, :, 1], SH, 2), ALU.is_equal).then_inc(dve_done, 1)
        dve.wait_ge(dve_done, dve_done_so_far())
        dve.wait_ge(act_done, 1 + CREDIT)
        dve.tensor_scalar(B["den"][:, :], B["e"][:, :], 1.0, None, ALU.add).then_inc(dve_done, 1)
        dve.wait_ge(dve_done, dve_done_so_far())
        dve.reciprocal(B["p1"][:, :], B["den"][:, :]).then_inc(dve_done, 1)
        dve.wait_ge(dve_done, dve_done_so_far())
        dve.tensor_tensor(B["p2"][:, :], B["e"][:, :], B["p1"][:, :], ALU.mult).then_inc(dve_done, 1)
        dve.wait_ge(dve_done, dve_done_so_far())
        dve.tensor_tensor(B["one"][:, :, :], B["one"][:, :, :], over(B["p1"][:, :], SH, 2), ALU.mult).then_inc(dve_done, 1)
        dve.wait_ge(dve_done, dve_done_so_far())
        dve.tensor_tensor(B["two"][:, :, :], B["two"][:, :, :], over(B["p2"][:, :], SH, 2), ALU.mult).then_inc(dve_done, 1)
        dve.wait_ge(dve_done, dve_done_so_far())
        dve.tensor_tensor(gates[:, :, :], B["one"][:, :, :], B["two"][:, :, :], ALU.add).then_inc(ready, 1)

    def act_part(act, core, B, dve_done, act_done):
        act.wait_ge(dve_done, 5 + CREDIT)
        act.activation(B["e"][:, :], B["d"][:, :], ACT.Exp).then_inc(act_done, 1)

    gate_stage(core, ctx, 1, weight(core, 1, "l0_rw"), 8, dve_part, act_part, [(gates, gatesT)], setup)


def l0_ffn(core, ctx, next_weights=()):
    nc, X, XT = core.nc, core.X, core.XT
    credited = []
    sem = lambda s: new_sem(core, ctx, f"f0_{s}", credited)
    with ExitStack() as mem:
        mem.callback(retire, core, credited)
        sb = lambda s, shape, dt=F32: mem.enter_context(nc.sbuf_tensor(f"f0_{s}", shape, dt))
        gates, gatesT = sb("gates", SH), sb("gatesT", [8, TOK])
        l0_gates(core, ctx, gates, gatesT)
        act_sb = [sb(f"act{i}", [P, BANK]) for i in range(2)]
        prod = [sb(f"prod{i}", [P, BANK]) for i in range(2)]
        hid = [sb(f"hid{i}", [P, 5, BANK]) for i in range(2)]
        spread = [sb(f"spread{i}", [P, 4, BANK]) for i in range(2)]
        gate_rows = nc.dram_tensor("gate_rows", (8, TOK), F32, kind="Internal").ap()
        rows_stored, gates_in = sem("rows_stored"), [sem(f"gates_in{i}") for i in range(2)]
        B = {"stat": sb("stat", [P, 4, 6]), "mv": sb("mv", [P, 4, 2])}
        up, silu_out, product, hidden, down, residual, stats, aggregated, kept = [
            sem(s) for s in ("up", "silu_out", "product", "hidden", "down", "residual", "stats", "aggregated", "kept")]
        w = lambda s: weight(core, 1, s)
        ident = core.const("ident")
        PAIRS = 5
        bank = core.bank
        block = mem.enter_context(nc.Block())

        @block.sync
        def _(sp):
            give_credit(sp, credited)
            sp.dma_start(gate_rows, gatesT[:, :]).then_inc(rows_stored, 16)
            sp.wait_ge(rows_stored, 16 + CREDIT)

            def load(G, g):
                for half in range(2):
                    src = gate_rows.rearrange("(p a) t -> a p t", a=2)[half:half + 1, :, bass.ds(G * BANK, BANK)]
                    sp.dma_start(spread[g][64 * half:64 * half + 64, :, :], src.to_broadcast([64, 4, BANK])
                                 ).then_inc(gates_in[g], 16)

            load(0, 0)
            load(1, 1)
            for k in next_weights:
                load_weights(core, sp, k)
            with sp.Fori(0, 3) as i:
                for g in range(2):
                    sp.wait_ge(hidden, i * 10 + (g + 1) * PAIRS + CREDIT)
                    load(2 * i + g + 2, g)

        @block.tensor
        def _(pe):
            def ups(i, g):
                for p in range(PAIRS):
                    u = g * PAIRS + p
                    pe.wait_ge(hidden, i * 10 + max(u - 2, 0) + CREDIT)
                    carry_waits(core, pe)
                    b = bank[2 * (u % 3):2 * (u % 3) + 2]
                    x = XT[:, bass.ds((2 * i + g) * BANK, BANK)]
                    pe.matmul(b[0][:, :], w("l0_w1")[:, p * P:(p + 1) * P], x, start=True, stop=True)
                    mm = pe.matmul(b[1][:, :], w("l0_w3")[:, p * P:(p + 1) * P], x, start=True, stop=True)
                    mm.then_inc(up, 1)

            def downs(i, g):
                pe.wait_ge(hidden, i * 10 + (g + 1) * PAIRS + CREDIT)
                pe.wait_ge(residual, 2 * i + CREDIT)
                for t in range(4):
                    for p in range(PAIRS):
                        mm = pe.matmul(bank[6 + g][:, t * P:(t + 1) * P], hid[g][:, p, t * P:(t + 1) * P],
                                       w("l0_w2")[:, p * P:(p + 1) * P], start=(p == 0), stop=(p == PAIRS - 1))
                mm.then_inc(down, 1)

            with pe.Fori(0, 4) as i:
                ups(i, 0)
                ups(i, 1)
                downs(i, 0)
                downs(i, 1)

        @block.scalar
        def _(act):
            with act.Fori(0, 4) as i:
                for u in range(2 * PAIRS):
                    act.wait_ge(up, i * 10 + u + 1 + CREDIT)
                    act.wait_ge(hidden, i * 10 + max(u - 1, 0) + CREDIT)
                    act.activation(act_sb[u % 2][:, :], bank[2 * (u % 3)][:, :], ACT.Silu).then_inc(silu_out, 1)

        @block.vector
        def _(dve):
            with dve.Fori(0, 4) as i:
                for g in range(2):
                    for p in range(PAIRS):
                        u = g * PAIRS + p
                        b = bank[2 * (u % 3):2 * (u % 3) + 2]
                        dve.wait_ge(silu_out, i * 10 + u + 1 + CREDIT)
                        dst = prod[u % 2][:, :] if p < 4 else hid[g][:, p, :]
                        if p == 0 or p == 4:
                            dve.wait_ge(down, 2 * i + CREDIT)
                        dve.tensor_tensor(dst, act_sb[u % 2][:, :], b[1][:, :], ALU.mult
                                          ).then_inc(product if p < 4 else hidden, 1)
                        if p == 0:
                            dve.wait_ge(gates_in[g], 32 * (i + 1) + CREDIT)
                        if p < 4:
                            dve.wait_ge(product, i * 8 + g * 4 + p + 1 + CREDIT)
                            dve.tensor_tensor(hid[g][:, p, :], dst, spread[g][:, p, :], ALU.mult).then_inc(hidden, 1)
                for g in range(2):
                    dve.wait_ge(down, 2 * i + g + 1 + CREDIT)
                    xg = X[:, bass.ds((2 * i + g) * 4, 4), :]
                    dve.tensor_tensor(xg, bank[6 + g][:, :].rearrange("p (t d) -> p t d", t=4), xg, ALU.add
                                      ).then_inc(residual, 1)
                    dve.wait_ge(residual, 2 * i + g + 1 + CREDIT)
                    group_moments(dve, core, B, 2 * i + g, (stats, aggregated, kept))


def l1_gates(core, ctx, win, gate):
    def setup(B):
        for s in ("lg", "ex", "sc", "vals", "idxf", "pos"):
            B[s] = B["sb"](s, SH)
        B["idx"] = B["sb"]("idx", SH, U32)
        for s in ("m", "sum", "r", "w"):
            B[s] = B["sb"](s, [P, TILES])

    def dve_part(dve, core, B, dve_done, dve_done_so_far, act_done, ready, extra):
        iota = core.const("iota8")
        dve.tensor_tensor(B["lg"][:, :, :], B["logits"], over(weight(core, 3, "l1_gb"), SH, 1), ALU.add).then_inc(dve_done, 1)
        dve.wait_ge(dve_done, dve_done_so_far())
        dve.tensor_reduce(B["m"][:, :], B["lg"][:, :, :], AX.X, ALU.max).then_inc(dve_done, 1)
        dve.wait_ge(dve_done, dve_done_so_far())
        dve.tensor_tensor(B["lg"][:, :, :], B["lg"][:, :, :], over(B["m"][:, :], SH, 2), ALU.subtract).then_inc(dve_done, 1)
        dve.wait_ge(dve_done, dve_done_so_far())
        dve.wait_ge(act_done, 1 + CREDIT)
        dve.tensor_reduce(B["sum"][:, :], B["ex"][:, :, :], AX.X, ALU.add).then_inc(dve_done, 1)
        dve.wait_ge(dve_done, dve_done_so_far())
        dve.reciprocal(B["r"][:, :], B["sum"][:, :]).then_inc(dve_done, 1)
        dve.wait_ge(dve_done, dve_done_so_far())
        dve.tensor_tensor(B["sc"][:, :, :], B["ex"][:, :, :], over(B["r"][:, :], SH, 2), ALU.mult).then_inc(dve_done, 1)
        dve.wait_ge(dve_done, dve_done_so_far())
        top_entries(dve, B, dve_done, dve_done_so_far, B["sc"], 8)
        dve.tensor_scalar(B["pos"][:, :, :], B["vals"][:, :, :], 0.0, None, ALU.is_gt).then_inc(dve_done, 1)
        dve.wait_ge(dve_done, dve_done_so_far())
        dve.tensor_scalar(B["idxf"][:, :, :], B["idxf"][:, :, :], 1.0, None, ALU.add).then_inc(dve_done, 1)
        dve.wait_ge(dve_done, dve_done_so_far())
        dve.tensor_tensor(B["idxf"][:, :, :], B["idxf"][:, :, :], B["pos"][:, :, :], ALU.mult).then_inc(dve_done, 1)
        dve.wait_ge(dve_done, dve_done_so_far())
        dve.tensor_tensor(B["w"][:, :], B["idxf"][:, :, 0], B["idxf"][:, :, 1], ALU.max).then_inc(dve_done, 1)
        dve.wait_ge(dve_done, dve_done_so_far())
        dve.tensor_scalar(B["w"][:, :], B["w"][:, :], -1.0, None, ALU.add).then_inc(dve_done, 1)
        dve.wait_ge(dve_done, dve_done_so_far())
        dve.tensor_tensor(win[:, :, :], over(iota, SH, 1), over(B["w"][:, :], SH, 2), ALU.is_equal).then_inc(dve_done, 1)
        dve.wait_ge(dve_done, dve_done_so_far())
        dve.tensor_tensor(gate[:, :, :], win[:, :, :], B["sc"][:, :, :], ALU.mult).then_inc(ready, 1)

    def act_part(act, core, B, dve_done, act_done):
        act.wait_ge(dve_done, 3 + CREDIT)
        act.activation(B["ex"][:, :, :], B["lg"][:, :, :], ACT.Exp).then_inc(act_done, 1)

    gate_stage(core, ctx, 3, weight(core, 3, "l1_gw"), 8, dve_part, act_part, [], setup)


SORTED = 40


def l1_places(core, ctx, win, gate, R, x_sorted):
    nc, bank = core.nc, core.bank
    credited = []
    sem = lambda s: new_sem(core, ctx, f"p1_{s}", credited)
    zeroed, filled, counted, done = sem("zeroed"), sem("filled"), sem("counted"), sem("done")
    sem("credits")
    FILLS = 4
    with ExitStack() as mem:
        mem.callback(retire, core, credited)
        sb = lambda s, shape, dt=F32: mem.enter_context(nc.sbuf_tensor(f"p1_{s}", shape, dt))
        tot, before = sb("tot", SH), [sb(f"before{i}", SH) for i in range(2)]
        n, full, tiles, part, start, shift = (sb("n", [P, 8]), sb("full", [P, 8, TILES]), sb("tiles", [P, 8]),
                                              sb("part", [P, 8, 8]), sb("start", [P, 8]), sb("shift", [P, 8]))
        past, expert, place = sb("past", [P, SORTED, 8]), sb("expertf", [P, SORTED]), sb("placef", [P, TILES])
        pos = sb("pos", SH)
        rows = x_sorted.shape[0] // FILLS
        zero = sb("zero", [P, rows // P * DM])
        w = lambda s: weight(core, 3, s)
        flat = lambda a: a[:, :, :].rearrange("p t e -> p (t e)")
        block = mem.enter_context(nc.Block())

        @block.sync
        def _(sp):
            give_credit(sp, credited)
            sp.wait_ge(zeroed, 1 + CREDIT)
            for k in range(FILLS):
                sp.dma_start(x_sorted[k * rows:(k + 1) * rows, :].rearrange("(p a) d -> p (a d)", p=P), zero[:, :]
                             ).then_inc(filled, 16)
            sp.wait_ge(filled, 16 * FILLS + CREDIT)

        @block.gpsimd
        def _(pool):
            pool.wait_ge(credited[-1], CREDIT)
            pool.memset(zero[:, :], 0.0).then_inc(zeroed, 1)

        @block.tensor
        def _(pe):
            pe.wait_ge(credited[-1], CREDIT)
            pe.matmul(bank[0][:, 0:TILES * 8], w("l1_lower"), flat(win), start=True, stop=True)
            pe.matmul(bank[1][:, 0:TILES * 8], w("l1_ones"), flat(win), start=True, stop=True).then_inc(counted, 1)

        @block.vector
        def _(dve):
            so_far = counter(CREDIT)
            dve.wait_ge(counted, 1 + CREDIT)
            dve.tensor_copy(flat(tot), bank[1][:, 0:TILES * 8]).then_inc(done, 1)
            dve.wait_ge(done, so_far())
            dve.memset(before[0][:, 0, :], 0.0)
            dve.tensor_copy(before[0][:, 1:, :], tot[:, 0:TILES - 1, :]).then_inc(done, 1)
            dve.wait_ge(done, so_far())
            for k in range(5):
                a, z, s = before[k % 2], before[(k + 1) % 2], 1 << k
                dve.tensor_copy(z[:, 0:s, :], a[:, 0:s, :])
                dve.tensor_tensor(z[:, s:, :], a[:, s:, :], a[:, 0:TILES - s, :], ALU.add).then_inc(done, 1)
                dve.wait_ge(done, so_far())
            sums = before[1]
            dve.tensor_tensor(n[:, :], sums[:, TILES - 1, :], tot[:, TILES - 1, :], ALU.add).then_inc(done, 1)
            dve.wait_ge(done, so_far())
            dve.tensor_tensor(full[:, :, :], over(n[:, :], [P, 8, TILES], 2), over(w("l1_multiples"), [P, 8, TILES], 1),
                              ALU.is_gt).then_inc(done, 1)
            dve.wait_ge(done, so_far())
            dve.tensor_reduce(tiles[:, :], full[:, :, :], AX.X, ALU.add).then_inc(done, 1)
            dve.wait_ge(done, so_far())
            dve.tensor_tensor(part[:, :, :], w("l1_earlier").rearrange("p (a b) -> p a b", a=8),
                              over(tiles[:, :], [P, 8, 8], 1), ALU.mult).then_inc(done, 1)
            dve.wait_ge(done, so_far())
            dve.tensor_reduce(start[:, :], part[:, :, :], AX.X, ALU.add).then_inc(done, 1)
            dve.wait_ge(done, so_far())
            dve.tensor_tensor(past[:, :, :], over(w("l1_iota"), [P, SORTED, 8], 2), over(start[:, :], [P, SORTED, 8], 1),
                              ALU.is_ge).then_inc(done, 1)
            dve.tensor_scalar(shift[:, :], start[:, :], float(P), None, ALU.mult).then_inc(done, 1)
            so_far()
            dve.wait_ge(done, so_far())
            dve.tensor_reduce(expert[:, :], past[:, :, :], AX.X, ALU.add).then_inc(done, 1)
            dve.tensor_tensor(flat(pos), bank[0][:, 0:TILES * 8], flat(sums), ALU.add).then_inc(done, 1)
            so_far()
            dve.wait_ge(done, so_far())
            dve.tensor_scalar(expert[:, :], expert[:, :], -1.0, None, ALU.add).then_inc(done, 1)
            dve.tensor_tensor(pos[:, :, :], pos[:, :, :], over(shift[:, :], SH, 1), ALU.add).then_inc(done, 1)
            so_far()
            dve.wait_ge(done, so_far())
            dve.tensor_copy(R["expert"][:, :], expert[:, :])
            dve.tensor_tensor(pos[:, :, :], pos[:, :, :], win[:, :, :], ALU.mult).then_inc(done, 1)
            dve.wait_ge(done, so_far())
            dve.tensor_reduce(place[:, :], pos[:, :, :], AX.X, ALU.add).then_inc(done, 1)
            dve.tensor_reduce(R["gval"][:, :], gate[:, :, :], AX.X, ALU.add).then_inc(done, 1)
            so_far()
            dve.wait_ge(done, so_far())
            dve.tensor_copy(R["place"][:, :], place[:, :])


def l1_ffn(core, ctx, next_weights=()):
    nc, X = core.nc, core.X
    GROUPS = SORTED // 4
    ROWS = (SORTED + 8) * P
    PARTS = 4
    x_sorted = nc.dram_tensor("x_sorted", (ROWS, DM), F32, kind="Internal").ap()
    y_sorted = nc.dram_tensor("y_sorted", (SORTED * P, DM), F32, kind="Internal").ap()
    with ExitStack() as outer:
        osb = lambda s, shape, dt=F32: outer.enter_context(nc.sbuf_tensor(f"f1_{s}", shape, dt))
        win, gate = osb("win", SH), osb("gate", SH)
        R = {"expert": osb("expert", [P, SORTED], mybir.dt.int32), "place": osb("place", [P, TILES], U32),
             "gval": osb("gval", [P, TILES])}
        l1_gates(core, ctx, win, gate)
        l1_places(core, ctx, win, gate, R, x_sorted)
        credited = []
        sem = lambda s: new_sem(core, ctx, f"f1_{s}", credited)
        with ExitStack() as mem:
            plain = []
            mem.callback(retire, core, plain)
            mem.callback(retire, core, credited)
            sb = lambda s, shape, dt=F32: mem.enter_context(nc.sbuf_tensor(f"f1_{s}", shape, dt))
            moved = sb("moved", [P, TILES, DM])
            b2 = sb("b2", [P, 8 * DM])
            xin = [sb(f"xin{i}", [P, 4, DM]) for i in range(2)]
            xT = [sb(f"xT{i}", [P, BANK]) for i in range(2)]
            h = [sb(f"h{i}", [P, BANK]) for i in range(2)]
            hT = [sb(f"hT{i}", [P, BANK]) for i in range(2)]
            yout = [sb(f"yout{i}", [P, 4, DM]) for i in range(2)]
            stat = sb("stat", [P, TILES, 6])
            b2_in, gated = sem("b2_in"), sem("gated")
            scattered = new_sem(core, ctx, "f1_scattered", plain)
            loaded, stored = [sem(f"loaded{i}") for i in range(2)], [sem(f"stored{i}") for i in range(2)]
            gathered = [new_sem(core, ctx, f"f1_gathered{i}", plain) for i in range(PARTS)]
            x_turned, x_out, h_mm, h_out, h_turned, hidden, down, y_ready, residual, stats, chain = [sem(s) for s in (
                "x_turned", "x_out", "h_mm", "h_out", "h_turned", "hidden", "down", "y_ready", "residual", "stats", "chain")]
            w = lambda s: weight(core, 3, s)
            ident, bank = core.const("ident"), core.bank
            XB, HB, TB, YB = bank[0:2], bank[2:4], bank[4:6], bank[6:8]
            block = mem.enter_context(nc.Block())

            @block.sync
            def _(sp):
                give_credit(sp, credited)
                sp.dma_start(b2[:, :], core.dram["l1_b2"].to_broadcast([P, 8 * DM])).then_inc(b2_in, 16)
                for k in next_weights:
                    load_weights(core, sp, k)

                def load(G, k):
                    rows = x_sorted[bass.ds(G * BANK, BANK), :].rearrange("(t p) d -> p t d", p=P)
                    sp.dma_start(xin[k][:, :, :], rows).then_inc(loaded[k], 16)

                sp.wait_ge(scattered, 16 * TILES)
                load(0, 0)
                load(1, 1)
                with sp.Fori(0, GROUPS // 2) as i:
                    for k in range(2):
                        sp.wait_ge(y_ready, 8 * i + 4 * k + 4 + CREDIT)
                        rows = y_sorted[bass.ds((2 * i + k) * BANK, BANK), :].rearrange("(t p) d -> p t d", p=P)
                        sp.dma_start(rows, yout[k][:, :, :]).then_inc(stored[k], 16)
                        sp.wait_ge(x_turned, 2 * i + k + 1 + CREDIT)
                        load(2 * i + k + 2, k)
                for k in range(2):
                    sp.wait_ge(loaded[k], 16 * (GROUPS // 2 + 1) + CREDIT)
                    sp.wait_ge(stored[k], 16 * (GROUPS // 2) + CREDIT)

            @block.gpsimd
            def _(pool):
                for t in range(TILES):
                    if t % 8 == 0:
                        pool.wait_ge(gated, t // 8 + 1 + CREDIT)
                    pool.indirect_dma_start(
                        x_sorted[:, :], bass.IndirectOffsetOnAxis(ap=R["place"][:, t:t + 1], axis=0),
                        moved[:, t, :], None).then_inc(scattered, 16)
                pool.wait_ge(scattered, 16 * TILES)
                for k in range(2):
                    pool.wait_ge(stored[k], 16 * (GROUPS // 2) + CREDIT)
                for t in range(TILES):
                    pool.indirect_dma_start(
                        moved[:, t, :], None, y_sorted[:, :],
                        bass.IndirectOffsetOnAxis(ap=R["place"][:, t:t + 1], axis=0)
                    ).then_inc(gathered[t * PARTS // TILES], 16)

            @block.tensor
            def _(pe):
                def x_turn(i, k):
                    pe.wait_ge(loaded[k], 16 * (i + 1) + CREDIT)
                    pe.wait_ge(x_out, 2 * i + CREDIT)
                    for t in range(4):
                        mm = pe.transpose(XB[k][:, t * P:(t + 1) * P], xin[k][:, t, :], ident)
                    mm.then_inc(x_turned, 1)

                def up(i, t, e):
                    pe.wait_ge(x_out, 2 * i + t // 4 + 1 + CREDIT)
                    pe.wait_ge(h_out, 8 * i + max(t - 1, 0) + CREDIT)
                    carry_waits(core, pe)
                    pe.matmul(HB[t % 2][:, :], xT[t // 4][:, (t % 4) * P:(t % 4 + 1) * P],
                              w("l1_w1")[:, bass.ds(e * BANK, BANK)], start=True, stop=True).then_inc(h_mm, 1)

                def turn(i, t):
                    pe.wait_ge(h_out, 8 * i + t + 1 + CREDIT)
                    pe.wait_ge(hidden, 8 * i + max(t - 1, 0) + CREDIT)
                    for c in range(4):
                        mm = pe.transpose(TB[t % 2][:, c * P:(c + 1) * P], h[t % 2][:, c * P:(c + 1) * P], ident)
                    mm.then_inc(h_turned, 1)

                def out(i, t, e):
                    pe.wait_ge(hidden, 8 * i + t + 1 + CREDIT)
                    pe.wait_ge(y_ready, 8 * i + max(t - 1, 0) + CREDIT)
                    carry_waits(core, pe)
                    for c in range(4):
                        mm = pe.matmul(YB[t % 2][:, 0:DM], hT[t % 2][:, c * P:(c + 1) * P],
                                       w("l1_w2")[:, bass.ds(c * 8 * DM + e * DM, DM)], start=(c == 0), stop=(c == 3))
                    mm.then_inc(down, 1)

                with pe.Fori(0, GROUPS // 2) as i:
                    x_turn(i, 0)
                    x_turn(i, 1)
                    e = {}
                    for t in range(10):
                        if t < 8:
                            e[t] = pe.value_load(R["expert"][0:1, bass.ds(8 * i + t, 1)], min_val=0, max_val=7)
                            up(i, t, e[t])
                        if 1 <= t < 9:
                            turn(i, t - 1)
                        if t >= 2:
                            out(i, t - 2, e[t - 2])

            @block.scalar
            def _(act):
                with act.Fori(0, GROUPS // 2) as i:
                    for k in range(2):
                        act.wait_ge(x_turned, 2 * i + k + 1 + CREDIT)
                        act.wait_ge(h_mm, 8 * i + CREDIT)
                        act.activation(xT[k][:, :], XB[k][:, :], ACT.Copy).then_inc(x_out, 1)
                    for t in range(8):
                        e = act.value_load(R["expert"][0:1, bass.ds(8 * i + t, 1)], min_val=0, max_val=7)
                        act.wait_ge(h_turned, 8 * i + t + 1 + CREDIT)
                        act.wait_ge(down, 8 * i + max(t - 1, 0) + CREDIT)
                        for c in range(4):
                            ins = act.activation(hT[t % 2][:, c * P:(c + 1) * P], TB[t % 2][:, c * P:(c + 1) * P],
                                                 ACT.Relu, bias=w("l1_b1")[:, bass.ds(c * 8 + e, 1)])
                        ins.then_inc(hidden, 1)

            @block.vector
            def _(dve):
                dve.wait_ge(credited[-1], CREDIT)
                for k in range(4):
                    dve.tensor_tensor(moved[:, 8 * k:8 * k + 8, :], X[:, 8 * k:8 * k + 8, :],
                                      over(R["gval"][:, 8 * k:8 * k + 8], [P, 8, DM], 2), ALU.mult).then_inc(gated, 1)
                dve.wait_ge(b2_in, 16 + CREDIT)

                def copy_h(i, t):
                    dve.wait_ge(h_mm, 8 * i + t + 1 + CREDIT)
                    dve.wait_ge(h_turned, 8 * i + max(t - 1, 0) + CREDIT)
                    dve.tensor_copy(h[t % 2][:, :], HB[t % 2][:, :]).then_inc(h_out, 1)

                def add_b2(i, t, e):
                    dve.wait_ge(down, 8 * i + t + 1 + CREDIT)
                    dve.wait_ge(stored[t // 4], 16 * i + CREDIT)
                    dve.tensor_tensor(yout[t // 4][:, t % 4, :], YB[t % 2][:, 0:DM], b2[:, bass.ds(e * DM, DM)],
                                      ALU.add).then_inc(y_ready, 1)

                with dve.Fori(0, GROUPS // 2) as i:
                    for t in range(10):
                        if t < 8:
                            copy_h(i, t)
                        if t >= 2:
                            e = dve.value_load(R["expert"][0:1, bass.ds(8 * i + t - 2, 1)], min_val=0, max_val=7)
                            add_b2(i, t - 2, e)
                n = TILES // PARTS
                for k in range(PARTS):
                    dve.wait_ge(gathered[k], 16 * n)
                    part = slice(k * n, (k + 1) * n)
                    dve.tensor_tensor(X[:, part, :], moved[:, part, :], X[:, part, :], ALU.add).then_inc(residual, 1)
                    dve.wait_ge(residual, k + 1 + CREDIT)
                    for t in range(k * n, (k + 1) * n):
                        ins = dve.bn_stats(stat[:, t, :], X[:, t, :])
                    ins.then_inc(stats, 1)
                    dve.wait_ge(stats, k + 1 + CREDIT)
                    for t in range(k * n, (k + 1) * n):
                        dve.bn_aggr(core.mv[:, t, :], stat[:, t, :])


NSEL = 256
SELT = NSEL // P


def selected_stage(core, ctx, M):
    nc = core.nc
    credited = []
    sem = lambda s: new_sem(core, ctx, f"sel_{s}", credited)
    loaded, done = sem("loaded"), sem("done")
    with ExitStack() as mem:
        mem.callback(retire, core, credited)
        sb = lambda s, shape, dt=F32: mem.enter_context(nc.sbuf_tensor(f"sel_{s}", shape, dt))
        C = SELT + NSEL
        raw = sb("raw", [P, 2, C], mybir.dt.int32)
        num, low, size = sb("num", [P, 2, C]), sb("low", [P, 2, C]), (BATCH, SEQ)
        block = mem.enter_context(nc.Block())

        @block.sync
        def _(sp):
            give_credit(sp, credited)
            for k, name in enumerate(("l3_ib", "l3_it")):
                sp.dma_start(raw[:, k, 0:SELT], core.dram[name + "col"]).then_inc(loaded, 16)
                sp.dma_start(raw[:, k, SELT:C], core.dram[name + "row"].to_broadcast([P, NSEL])).then_inc(loaded, 16)

        @block.vector
        def _(dve):
            dve.wait_ge(loaded, 64 + CREDIT)
            done_so_far = counter(CREDIT)
            dve.tensor_copy(num[:, :, :], raw[:, :, :]).then_inc(done, 1)
            dve.wait_ge(done, done_so_far())
            dve.tensor_scalar(low[:, :, :], num[:, :, :], 0.0, None, ALU.is_lt).then_inc(done, 1)
            dve.wait_ge(done, done_so_far())
            for k in range(2):
                ins = dve.scalar_tensor_tensor(num[:, k, :], low[:, k, :], float(size[k]), num[:, k, :],
                                               ALU.mult, ALU.add)
            ins.then_inc(done, 1)
            dve.wait_ge(done, done_so_far())
            dve.scalar_tensor_tensor(M["jcol"][:, :], num[:, 0, 0:SELT], float(SEQ), num[:, 1, 0:SELT],
                                     ALU.mult, ALU.add).then_inc(done, 1)
            dve.scalar_tensor_tensor(M["jrow"][:, :], num[:, 0, SELT:C], float(SEQ), num[:, 1, SELT:C],
                                     ALU.mult, ALU.add).then_inc(done, 1)


def l3_ffn(core, ctx, next_weights=()):
    nc, X, XT = core.nc, core.X, core.XT
    HF = 64
    GR = TOK // BANK
    NZ = TILES + 8 * SELT
    w = lambda s: weight(core, 7, s)
    ident, bank = core.const("ident"), core.bank
    with ExitStack() as outer:
        osb = lambda s, shape, dt=F32: outer.enter_context(nc.sbuf_tensor(f"f3_{s}", shape, dt))
        M = {"jcol": osb("jcol", [P, SELT]), "jrow": osb("jrow", [P, NSEL])}
        U = osb("U", [P, NZ, HF])
        YS = osb("YS", [P, SELT, P + 1])
        jshift = osb("jshift", [P, SELT, GR])
        selected_stage(core, ctx, M)

        credited = []
        sem = lambda s: new_sem(core, ctx, f"f3a_{s}", credited)
        with ExitStack() as mem:
            mem.callback(retire, core, credited)
            sb = lambda s, shape, dt=F32: mem.enter_context(nc.sbuf_tensor(f"f3a_{s}", shape, dt))
            xs = [sb(f"xs{i}", [P, BANK]) for i in range(2)]
            hb = [sb(f"hb{i}", [P, 4, 2 * HF]) for i in range(2)]
            sl = [sb(f"sl{i}", [P, 4, HF]) for i in range(2)]
            pick = [sb(f"pick{i}", [P, NSEL]) for i in range(2)]
            xm, xmT = sb("xm", [P, SELT, P]), sb("xmT", [P, NSEL])
            eh, es = sb("eh", [P, SELT, 2, 8 * HF]), sb("es", [P, SELT, 8 * HF])
            cen, mean, var, std, rstd = (sb("cen", [P, NZ, HF]), sb("mean", [P, NZ]), sb("var", [P, NZ]),
                                         sb("std", [P, NZ]), sb("rstd", [P, NZ]))
            n8 = [P, SELT, 8]
            lg, sc, bs, vals, idxf, oh = (sb("lg", [P, SELT, 9]), sb("sc", [P, SELT, 9]), sb("bs", n8),
                                          sb("vals", n8), sb("idxf", n8), sb("oh", n8))
            idx = sb("idx", n8, U32)
            ts, dif, ex, sw, ew, same, cnt, rcnt = [sb(s, [P, SELT]) for s in
                                                    ("ts", "dif", "ex", "sw", "ew", "same", "cnt", "rcnt")]
            eq = sb("eq", [P, NSEL])
            ohT, zT = sb("ohT", [8, NSEL]), sb("zT", [P, SELT, 4, P])
            (x_copied, up, added, silu_out, hidden, made, gathered, set_out, set_turned, set_copied, set_up, set_added,
             gates_mm, gates_done, gates_act, experts_act, experts_done, normed, std_ready, z_turned, z_out, oh_turned,
             oh_out, down, chain) = [sem(s) for s in (
                 "x_copied", "up", "added", "silu_out", "hidden", "made", "gathered", "set_out", "set_turned",
                 "set_copied", "set_up", "set_added", "gates_mm", "gates_done", "gates_act", "experts_act",
                 "experts_done", "normed", "std_ready", "z_turned", "z_out", "oh_turned", "oh_out", "down",
                 "chain")]
            GB, EB = bank[7], bank[3:7]
            block = mem.enter_context(nc.Block())

            @block.sync
            def _(sp):
                give_credit(sp, credited)

            @block.gpsimd
            def _(pool):
                with pool.Fori(0, GR // 2) as i:
                    for g in range(2):
                        pool.wait_ge(up, 2 * i + CREDIT)
                        carry_waits(core, pool)
                        pool.tensor_copy(xs[g][:, :], XT[:, bass.ds((2 * i + g) * BANK, BANK)]).then_inc(x_copied, 1)

            @block.tensor
            def _(pe):
                pe.wait_ge(core.weights_in[7], loaded_count(7))
                pe.wait_ge(credited[-1], CREDIT)
                with pe.Fori(0, GR // 2) as i:
                    for g in range(2):
                        pe.wait_ge(x_copied, 2 * i + g + 1 + CREDIT)
                        pe.wait_ge(added, 2 * i + CREDIT)
                        for t in range(4):
                            mm = pe.matmul(bank[g][:, t * P:(t + 1) * P], xs[g][:, t * P:(t + 1) * P], w("l3_s1"),
                                           start=True, stop=True)
                        mm.then_inc(up, 1)
                for t in range(TILES):
                    pe.wait_ge(made, t + 1 + CREDIT)
                    for j in range(SELT):
                        if t == 0:
                            pe.wait_ge(added, GR - 1 + j + CREDIT)
                        mm = pe.matmul(bank[j][:, 0:P], pick[t % 2][:, j * P:(j + 1) * P], X[:, t, :],
                                       start=(t == 0), stop=(t == TILES - 1))
                    mm.then_inc(gathered, 1)
                pe.wait_ge(set_out, 1 + CREDIT)
                for j in range(SELT):
                    mm = pe.transpose(bank[2][:, j * P:(j + 1) * P], xm[:, j, :], ident)
                mm.then_inc(set_turned, 1)
                pe.wait_ge(set_copied, 1 + CREDIT)
                for j in range(SELT):
                    mm = pe.matmul(GB[:, j * 16:j * 16 + 9], xmT[:, j * P:(j + 1) * P], w("l3_gw"), start=True, stop=True)
                mm.then_inc(gates_mm, 1)
                for j in range(SELT):
                    for k in range(2):
                        pe.matmul(EB[2 * j + k][:, :], xmT[:, j * P:(j + 1) * P], w(f"l3_e{k + 1}"),
                                  start=True, stop=True).then_inc(set_up, 1)
                pe.wait_ge(gates_done, 3 + CREDIT)
                for j in range(SELT):
                    mm = pe.transpose(bank[2][0:8, j * P:(j + 1) * P], oh[:, j, :], ident)
                mm.then_inc(oh_turned, 1)
                pe.wait_ge(set_added, 4 + CREDIT)
                for j in range(SELT):
                    pe.wait_ge(experts_done, j + 1 + CREDIT)
                    for c in range(4):
                        mm = pe.transpose(EB[j][:, c * P:(c + 1) * P],
                                          U[:, TILES + 8 * j + 2 * c:TILES + 8 * j + 2 * c + 2, :].rearrange("p a b -> p (a b)"),
                                          ident)
                    mm.then_inc(z_turned, 1)
                pe.wait_ge(oh_out, 1 + CREDIT)
                for j in range(SELT):
                    pe.wait_ge(z_out, j + 1 + CREDIT)
                    for c in range(4):
                        pe.matmul(bank[j][:, 0:P], zT[:, j, c, :], w("l3_e3")[:, c * P:(c + 1) * P],
                                  start=(c == 0), stop=False)
                    pe.matmul(bank[j][:, 0:P], ohT[:, j * P:(j + 1) * P], w("l3_eb3"),
                              start=False, stop=True).then_inc(down, 1)

            @block.scalar
            def _(act):
                with act.Fori(0, GR // 2) as i:
                    for g in range(2):
                        act.wait_ge(added, 2 * i + g + 1 + CREDIT)
                        act.wait_ge(hidden, 2 * i + CREDIT)
                        act.activation(sl[g][:, :, :], hb[g][:, :, 0:HF], ACT.Silu).then_inc(silu_out, 1)
                act.wait_ge(gathered, TILES + CREDIT)
                for j in range(SELT):
                    ins = act.activation(xm[:, j, :], bank[j][:, 0:P], ACT.Copy)
                ins.then_inc(set_out, 1)
                act.wait_ge(set_turned, 1 + CREDIT)
                act.activation(xmT[:, :], bank[2][:, 0:NSEL], ACT.Copy).then_inc(set_copied, 1)
                act.wait_ge(set_added, 4 + CREDIT)
                act.activation(es[:, :, :], eh[:, :, 0, :], ACT.Silu).then_inc(experts_act, 1)
                act.wait_ge(gates_done, 1 + CREDIT)
                act.activation(sc[:, :, :], lg[:, :, :], ACT.Sigmoid).then_inc(gates_act, 1)
                act.wait_ge(gates_done, 2 + CREDIT)
                act.activation(ex[:, :], dif[:, :], ACT.Exp).then_inc(gates_act, 1)
                act.wait_ge(normed, 5 + CREDIT)
                act.activation(std[:, :], var[:, :], ACT.Sqrt).then_inc(std_ready, 1)
                act.wait_ge(oh_turned, 1 + CREDIT)
                act.activation(ohT[:, :], bank[2][0:8, 0:NSEL], ACT.Copy).then_inc(oh_out, 1)
                for j in range(SELT):
                    act.wait_ge(z_turned, j + 1 + CREDIT)
                    act.activation(zT[:, j, :, :].rearrange("p a b -> p (a b)"), EB[j][:, :], ACT.Copy).then_inc(z_out, 1)
                for j in range(SELT):
                    act.wait_ge(down, j + 1 + CREDIT)
                    ins = act.activation(YS[:, j, 0:P], bank[j][:, 0:P], ACT.Copy)

            @block.vector
            def _(dve):
                dve.wait_ge(core.weights_in[7], loaded_count(7))
                with dve.Fori(0, GR // 2) as i:
                    for g in range(2):
                        dve.wait_ge(up, 2 * i + g + 1 + CREDIT)
                        dve.tensor_tensor(hb[g][:, :, :], bank[g][:, :].rearrange("p (t h) -> p t h", t=4),
                                          over(w("l3_sb"), [P, 4, 2 * HF], 1), ALU.add).then_inc(added, 1)
                        dve.wait_ge(silu_out, 2 * i + g + 1 + CREDIT)
                        dve.tensor_tensor(U[:, bass.ds((2 * i + g) * 4, 4), :], sl[g][:, :, :], hb[g][:, :, HF:2 * HF],
                                          ALU.mult).then_inc(hidden, 1)
                for t in range(TILES):
                    if t >= 2:
                        dve.wait_ge(gathered, t - 1 + CREDIT)
                    dve.tensor_tensor(pick[t % 2][:, :], M["jrow"][:, :], w("l3_token")[:, t:t + 1].to_broadcast([P, NSEL]),
                                      ALU.is_equal).then_inc(made, 1)
                normed_so_far = counter(CREDIT)
                for j in range(SELT):
                    dve.tensor_tensor(eq[:, :], M["jrow"][:, :], M["jcol"][:, j:j + 1].to_broadcast([P, NSEL]),
                                      ALU.is_equal).then_inc(normed, 1)
                    dve.wait_ge(normed, normed_so_far())
                    dve.tensor_reduce(cnt[:, j:j + 1], eq[:, :], AX.X, ALU.add).then_inc(normed, 1)
                    dve.wait_ge(normed, normed_so_far())
                dve.reciprocal(rcnt[:, :], cnt[:, :])
                dve.tensor_tensor(jshift[:, :, :], over(M["jcol"][:, :], [P, SELT, GR], 2),
                                  over(w("l3_base"), [P, SELT, GR], 1), ALU.subtract)
                chain_so_far = counter(CREDIT)
                dve.wait_ge(gates_mm, 1 + CREDIT)
                dve.tensor_tensor(lg[:, :, :], GB[:, 0:32].rearrange("p (j e) -> p j e", j=2)[:, :, 0:9],
                                  over(w("l3_gb"), [P, SELT, 9], 1), ALU.add).then_inc(chain, 1)
                dve.wait_ge(chain, chain_so_far())
                dve.sem_inc(gates_done, 1)
                for j in range(SELT):
                    for k in range(2):
                        dve.wait_ge(set_up, 2 * j + k + 1 + CREDIT)
                        dve.tensor_tensor(eh[:, j, k, :], EB[2 * j + k][:, :], w(f"l3_eb{k + 1}"), ALU.add
                                          ).then_inc(set_added, 1)
                dve.wait_ge(gates_act, 1 + CREDIT)
                dve.tensor_tensor(bs[:, :, :], sc[:, :, 1:9], over(w("l3_eb"), n8, 1), ALU.add).then_inc(chain, 1)
                dve.wait_ge(chain, chain_so_far())
                for j in range(SELT):
                    ins = dve.max(vals[:, j, :], bs[:, j, :])
                ins.then_inc(chain, 1)
                dve.wait_ge(chain, chain_so_far())
                for j in range(SELT):
                    ins = dve.max_index(idx[:, j, :], vals[:, j, :], bs[:, j, :])
                ins.then_inc(chain, 1)
                dve.wait_ge(chain, chain_so_far())
                dve.tensor_copy(idxf[:, :, :], idx[:, :, :]).then_inc(chain, 1)
                dve.wait_ge(chain, chain_so_far())
                dve.tensor_tensor(oh[:, :, :], over(core.const("iota8"), n8, 1), over(idxf[:, :, 0], n8, 2),
                                  ALU.is_equal).then_inc(chain, 1)
                dve.wait_ge(chain, chain_so_far())
                dve.tensor_tensor(bs[:, :, :], oh[:, :, :], sc[:, :, 1:9], ALU.mult).then_inc(chain, 1)
                dve.wait_ge(chain, chain_so_far())
                dve.tensor_reduce(ts[:, :], bs[:, :, :], AX.X, ALU.add).then_inc(chain, 1)
                dve.wait_ge(chain, chain_so_far())
                dve.tensor_tensor(dif[:, :], ts[:, :], sc[:, :, 0], ALU.subtract).then_inc(chain, 1)
                dve.wait_ge(chain, chain_so_far())
                dve.sem_inc(gates_done, 1)
                dve.wait_ge(gates_act, 2 + CREDIT)
                dve.tensor_scalar(ew[:, :], ex[:, :], 1.0, None, ALU.add).then_inc(chain, 1)
                dve.wait_ge(chain, chain_so_far())
                dve.reciprocal(sw[:, :], ew[:, :]).then_inc(chain, 1)
                dve.wait_ge(chain, chain_so_far())
                dve.tensor_tensor(ew[:, :], ex[:, :], sw[:, :], ALU.mult).then_inc(chain, 1)
                dve.wait_ge(chain, chain_so_far())
                dve.tensor_tensor(ew[:, :], ew[:, :], rcnt[:, :], ALU.mult).then_inc(chain, 1)
                dve.wait_ge(chain, chain_so_far())
                dve.tensor_scalar(sw[:, :], sw[:, :], -1.0, None, ALU.add).then_inc(chain, 1)
                dve.wait_ge(chain, chain_so_far())
                dve.tensor_tensor(YS[:, :, P], sw[:, :], rcnt[:, :], ALU.mult)
                dve.tensor_tensor(oh[:, :, :], oh[:, :, :], over(ew[:, :], n8, 2), ALU.mult).then_inc(chain, 1)
                dve.wait_ge(chain, chain_so_far())
                dve.sem_inc(gates_done, 1)
                dve.wait_ge(experts_act, 1 + CREDIT)
                dve.tensor_tensor(U[:, TILES:, :].rearrange("p (j e) h -> p j (e h)", j=SELT), es[:, :, :],
                                  eh[:, :, 1, :], ALU.mult).then_inc(chain, 1)
                dve.wait_ge(chain, chain_so_far())
                dve.tensor_reduce(mean[:, :], U[:, :, :], AX.X, ALU.add).then_inc(chain, 1)
                dve.wait_ge(chain, chain_so_far())
                dve.tensor_scalar(mean[:, :], mean[:, :], 1.0 / HF, None, ALU.mult).then_inc(chain, 1)
                dve.wait_ge(chain, chain_so_far())
                nz = [P, NZ, HF]
                dve.tensor_tensor(cen[:, :, :], U[:, :, :], over(mean[:, :], nz, 2), ALU.subtract).then_inc(chain, 1)
                dve.wait_ge(chain, chain_so_far())
                dve.tensor_tensor(U[:, :, :], cen[:, :, :], cen[:, :, :], ALU.mult).then_inc(chain, 1)
                dve.wait_ge(chain, chain_so_far())
                dve.tensor_reduce(var[:, :], U[:, :, :], AX.X, ALU.add).then_inc(chain, 1)
                dve.wait_ge(chain, chain_so_far())
                dve.tensor_scalar(var[:, :], var[:, :], 1.0 / HF, 1e-5, ALU.mult, ALU.add).then_inc(normed, 1)
                dve.wait_ge(std_ready, 1 + CREDIT)
                dve.reciprocal(rstd[:, :], std[:, :]).then_inc(chain, 1)
                dve.wait_ge(chain, chain_so_far())
                dve.tensor_tensor(U[:, :, :], cen[:, :, :], over(rstd[:, :], nz, 2), ALU.mult).then_inc(chain, 1)
                dve.wait_ge(chain, chain_so_far())
                for j in range(SELT):
                    z = U[:, TILES + 8 * j:TILES + 8 * (j + 1), :]
                    z8 = [P, 8, HF]
                    dve.tensor_tensor(z, z, over(w("l3_eln")[:, 0:HF], z8, 1), ALU.mult).then_inc(chain, 1)
                    dve.wait_ge(chain, chain_so_far())
                    dve.tensor_tensor(z, z, over(w("l3_eln")[:, HF:], z8, 1), ALU.add).then_inc(chain, 1)
                    dve.wait_ge(chain, chain_so_far())
                    dve.tensor_tensor(z, z, over(oh[:, j, :], z8, 2), ALU.mult).then_inc(experts_done, 1)

        credited = []
        with ExitStack() as mem:
            mem.callback(retire, core, credited)
            sb = lambda s, shape, dt=F32: mem.enter_context(nc.sbuf_tensor(f"f3b_{s}", shape, dt))
            zg = [sb(f"zg{i}", [P, 4, HF]) for i in range(2)]
            zr = [sb(f"zr{i}", [P, 4, HF]) for i in range(2)]
            zT = [sb(f"zT{i}", [HF, BANK]) for i in range(2)]
            place = [sb(f"place{i}", [P, SELT, BANK]) for i in range(2)]
            fac, sh, sc = sb("fac", [P, 4]), sb("sh", [P, 4, P]), sb("scaled", [P, 4, P])
            B = {"stat": sb("stat", [P, 4, 6]), "mv": sb("mv", [P, 4, 2])}
            sem = lambda s: new_sem(core, ctx, f"f3b_{s}", credited)
            (zoomed, scaled, turned, turned_out, placed, out_mm, biased, factor, weighted, joined_x, residual, stats,
             aggregated, kept) = [sem(s) for s in (
                 "zoomed", "scaled", "turned", "turned_out", "placed", "out_mm", "biased", "factor", "weighted",
                 "joined", "residual", "stats", "aggregated", "kept")]
            ZB, SB, YB, FB = bank[0:2], bank[2:4], bank[4:6], bank[6:8]
            block = mem.enter_context(nc.Block())

            @block.sync
            def _(sp):
                give_credit(sp, credited)

            @block.gpsimd
            def _(pool):
                with pool.Fori(0, GR // 2) as i:
                    for g in range(2):
                        G = 2 * i + g
                        pool.wait_ge(scaled, 2 * i + CREDIT)
                        pool.tensor_tensor(zg[g][:, :, :], U[:, bass.ds(G * 4, 4), :],
                                           over(w("l3_sln")[:, 0:HF], [P, 4, HF], 1), ALU.mult).then_inc(zoomed, 1)
                        pool.wait_ge(zoomed, G + 1 + CREDIT)
                        pool.wait_ge(turned, 2 * i + CREDIT)
                        pool.tensor_tensor(zr[g][:, :, :], zg[g][:, :, :], over(w("l3_sln")[:, HF:], [P, 4, HF], 1),
                                           ALU.add).then_inc(scaled, 1)

            @block.tensor
            def _(pe):
                with pe.Fori(0, GR // 2) as i:
                    for g in range(2):
                        G = 2 * i + g
                        pe.wait_ge(scaled, G + 1 + CREDIT)
                        pe.wait_ge(turned_out, 2 * i + CREDIT)
                        carry_waits(core, pe)
                        for t in range(4):
                            mm = pe.transpose(ZB[g][0:HF, t * P:(t + 1) * P], zr[g][:, t, :], ident)
                        mm.then_inc(turned, 1)
                    for g in range(2):
                        G = 2 * i + g
                        pe.wait_ge(turned_out, G + 1 + CREDIT)
                        pe.wait_ge(placed, G + 1 + CREDIT)
                        pe.wait_ge(residual, 2 * i + CREDIT)
                        carry_waits(core, pe)
                        for t in range(4):
                            tk = slice(t * P, (t + 1) * P)
                            pe.matmul(YB[g][:, tk], zT[g][:, tk], w("l3_s3"), start=True, stop=True)
                            for j in range(SELT):
                                pe.matmul(SB[g][:, tk], place[g][:, j, tk], YS[:, j, 0:P],
                                          start=(j == 0), stop=(j == SELT - 1))
                            for j in range(SELT):
                                mm = pe.matmul(FB[g][:, t:t + 1], place[g][:, j, tk], YS[:, j, P:P + 1],
                                               start=(j == 0), stop=(j == SELT - 1))
                        mm.then_inc(out_mm, 1)

            @block.scalar
            def _(act):
                with act.Fori(0, GR // 2) as i:
                    for g in range(2):
                        G = 2 * i + g
                        act.wait_ge(turned, G + 1 + CREDIT)
                        act.wait_ge(out_mm, 2 * i + CREDIT)
                        act.activation(zT[g][:, :], ZB[g][0:HF, :], ACT.Copy).then_inc(turned_out, 1)

            @block.vector
            def _(dve):
                def place_set(i, g):
                    G = 2 * i + g
                    dve.wait_ge(out_mm, 2 * i + CREDIT)
                    for j in range(SELT):
                        ins = dve.tensor_tensor(place[g][:, j, :], w("l3_iota"),
                                                joined(jshift[:, j:j + 1, bass.ds(G, 1)]).to_broadcast([P, BANK]),
                                                ALU.is_equal)
                    ins.then_inc(placed, 1)

                with dve.Fori(0, GR // 2) as i:
                    place_set(i, 0)
                    place_set(i, 1)
                    for g in range(2):
                        G = 2 * i + g
                        dve.wait_ge(out_mm, G + 1 + CREDIT)
                        yb = YB[g][:, :].rearrange("p (t d) -> p t d", t=4)
                        xg = X[:, bass.ds(G * 4, 4), :]
                        four = [P, 4, P]
                        dve.tensor_tensor(sh[:, :, :], yb, over(w("l3_sb3"), four, 1), ALU.add).then_inc(biased, 1)
                        dve.tensor_scalar(fac[:, :], FB[g][:, 0:4], 1.0, None, ALU.add).then_inc(factor, 1)
                        dve.wait_ge(biased, G + 1 + CREDIT)
                        dve.wait_ge(factor, G + 1 + CREDIT)
                        dve.tensor_tensor(sc[:, :, :], sh[:, :, :], over(fac[:, :], four, 2), ALU.mult).then_inc(weighted, 1)
                        dve.tensor_tensor(xg, SB[g][:, :].rearrange("p (t d) -> p t d", t=4), xg, ALU.add
                                          ).then_inc(joined_x, 1)
                        dve.wait_ge(weighted, G + 1 + CREDIT)
                        dve.wait_ge(joined_x, G + 1 + CREDIT)
                        dve.tensor_tensor(xg, sc[:, :, :], xg, ALU.add).then_inc(residual, 1)
                        dve.wait_ge(residual, G + 1 + CREDIT)
                        group_moments(dve, core, B, G, (stats, aggregated, kept))


NQ = 128
DESCENTS = 50


class Descent:

    PER_PAIR = 7

    def __init__(self, core, mem):
        sb = lambda s, cols: mem.enter_context(core.nc.sbuf_tensor(f"d_{s}", [2 * BATCH, cols], F32))
        self.s, self.t, self.junk = sb("s", SEQ), sb("t", SEQ), sb("junk", SEQ)
        self.smax, self.na, self.nm, self.S, self.L = [sb(n, 1) for n in ("smax", "na", "nm", "S", "L")]
        self.logk = core.const("logk", 2 * BATCH)
        assert self.PER_PAIR * (BATCH // 2 - 1) == DESCENTS - 1

    def alloc(self, sem, S):
        for n in ("na_ready", "low_ready", "shifted", "summed", "logged"):
            S[n] = sem(n)

    def preload(self, nc):
        nc.scalar.preload_act_table_set("natural_log_exp_and_others")

    def has(self, i, s):
        return not isinstance(i, int) and s < self.PER_PAIR

    def dve(self, dve, S, i, s):
        m = self.PER_PAIR * i - self.PER_PAIR + s
        dve.wait_ge(S["logged"], m + CREDIT)
        dve.tensor_scalar(self.na[:, :], self.L[:, :], self.nm[:, :], self.logk, ALU.subtract, ALU.subtract
                          ).then_inc(S["na_ready"], 1)
        dve.wait_ge(S["na_ready"], m + 1 + CREDIT)
        dve.tensor_scalar(self.nm[:, :], self.smax[:, :], self.na[:, :], -1.0, ALU.min, ALU.mult
                          ).then_inc(S["low_ready"], 1)
        dve.tensor_scalar(self.t[:, :], self.s[:, :], self.na[:, :], None, ALU.min).then_inc(S["shifted"], 1)

    def act(self, act, S, i, s):
        m = self.PER_PAIR * i - self.PER_PAIR + s
        act.wait_ge(S["low_ready"], m + 1 + CREDIT)
        act.wait_ge(S["shifted"], m + 1 + CREDIT)
        act.activation(self.junk[:, :], self.t[:, :], ACT.Exp, bias=self.nm[:, :], accum_out=self.S[:, :]
                       ).then_inc(S["summed"], 1)
        act.wait_ge(S["summed"], m + 1 + CREDIT)
        act.activation(self.L[:, :], self.S[:, :], ACT.Ln).then_inc(S["logged"], 1)


def routing_start(core, ctx, D):
    nc, XT = core.nc, core.XT
    R = 2 * BATCH
    credited = []
    sem = lambda s: new_sem(core, ctx, f"rs_{s}", credited)
    with ExitStack() as mem:
        mem.callback(retire, core, credited)
        products, s_ready, shifted, summed = [sem(n) for n in ("products", "s_ready", "shifted", "summed")]
        sem("credits")
        block = mem.enter_context(nc.Block())

        @block.sync
        def _(sp):
            give_credit(sp, credited)

        @block.tensor
        def _(pe):
            pe.wait_ge(core.weights_in[5], loaded_count(5))
            pe.wait_ge(credited[-1], CREDIT)
            tok = weight(core, 5, "l2_tok")
            for b in range(BATCH):
                mm = pe.matmul(core.bank[0][0:R, 0:SEQ], tok[:, 15 - b:15 - b + R], XT[:, b * SEQ:(b + 1) * SEQ],
                               start=(b == 0), stop=(b == BATCH - 1))
            mm.then_inc(products, 1)

        @block.scalar
        def _(act):
            nc.scalar.preload_act_table_set("natural_log_exp_and_others")
            act.wait_ge(shifted, 1 + CREDIT)
            act.activation(D.junk[:, :], D.t[:, :], ACT.Exp, bias=D.nm[:, :], accum_out=D.S[:, :]).then_inc(summed, 1)
            act.wait_ge(summed, 1 + CREDIT)
            act.activation(D.L[:, :], D.S[:, :], ACT.Ln)

        @block.vector
        def _(dve):
            dve.wait_ge(credited[-1], CREDIT)
            dve.wait_ge(core.weights_in[5], loaded_count(5))
            dve.memset(D.nm[:, :], 0.0)
            dve.memset(D.t[:, :], 0.0).then_inc(shifted, 1)
            for k, names in (("l2_gl", ("l2_wql", "l2_wkl", "l2_wvl")), ("l2_gh", ("l2_wqh", "l2_wkh", "l2_wvh"))):
                for n in names:
                    w = weight(core, 5, n)
                    dve.tensor_scalar(w, w, weight(core, 5, k), None, ALU.mult)
            dve.wait_ge(products, 1 + CREDIT)
            dve.tensor_copy(D.s[:, :], core.bank[0][0:R, 0:SEQ]).then_inc(s_ready, 1)
            dve.wait_ge(s_ready, 1 + CREDIT)
            dve.tensor_reduce(D.smax[:, :], D.s[:, :], AX.X, ALU.max)


def routing_finish(core, ctx, D, VS, SQ):
    nc = core.nc
    R = 2 * BATCH
    credited = []
    sem = lambda s: new_sem(core, ctx, f"r_{s}", credited)
    with ExitStack() as mem:
        mem.callback(retire, core, credited)
        sb = lambda s, shape, dt=F32: mem.enter_context(nc.sbuf_tensor(f"r_{s}", shape, dt))
        sc, u, sel = [sb(n, [R, SEQ]) for n in ("sc", "u", "sel")]
        ones = sb("ones", [R, P])
        row = [sb(f"row{i}", [R, SEQ]) for i in range(2)]
        prod, own, tie, ahead = [[sb(f"{n}{i}", shape) for i in range(2)]
                           for n, shape in (("prod", [P, 2, P]), ("own", [P, 2]), ("tie", [P, 2, SEQ]), ("ahead", [P, 2, SEQ]))]
        rank, chosen = sb("rank", [P, TILES]), sb("chosen", [P, TILES])
        (na_ready, scored, exped, selected, turned, turned_out,
         spread, row_ready, owned, tied, counted, ranked, picked, scaled, credits) = [sem(n) for n in (
             "na_ready", "scored", "exped", "selected",
             "turned", "turned_out", "spread", "row_ready", "owned", "tied", "counted", "ranked", "picked", "scaled", "credits")]
        before, ident = core.const("before"), core.const("ident")
        bank = core.bank
        block = mem.enter_context(nc.Block())

        @block.sync
        def _(sp):
            give_credit(sp, credited)

        @block.tensor
        def _(pe):
            pe.wait_ge(credited[-1], CREDIT)
            pe.wait_ge(selected, 2 + CREDIT)
            for h in range(2):
                mm = pe.transpose(bank[1][:, h * R:(h + 1) * R], sel[:, h * P:(h + 1) * P], ident[0:R, 0:R])
            mm.then_inc(turned, 1)
            with pe.Fori(0, BATCH // 2) as i:
                for b in range(2):
                    pe.wait_ge(row_ready, 2 * i + b + 1 + CREDIT)
                    pe.wait_ge(counted, 2 * i + CREDIT)
                    carry_waits(core, pe)
                    pe.matmul(bank[2 + b][:, 0:SEQ], ones[:, :], row[b][:, :], start=True, stop=True
                              ).then_inc(spread, 1)

        @block.gpsimd
        def _(pool):
            pool.wait_ge(exped, 1 + CREDIT)
            with pool.Fori(0, BATCH // 2) as i:
                for b in range(2):
                    pool.wait_ge(spread, 2 * i + CREDIT)
                    pool.tensor_tensor(row[b][:, :], sc[:, :],
                                       ident[0:R, bass.ds(2 * i + b, 1)].to_broadcast([R, SEQ]),
                                       ALU.mult).then_inc(row_ready, 1)

        @block.scalar
        def _(act):
            act.wait_ge(scored, 1 + CREDIT)
            act.activation(sc[:, :], D.t[:, :], ACT.Exp).then_inc(exped, 1)

        @block.vector
        def _(dve):
            dve.wait_ge(credited[-1], CREDIT)
            dve.memset(ones[:, :], 1.0)
            dve.memset(VS[:, BATCH, :], 0.0)
            dve.tensor_scalar(D.na[:, :], D.L[:, :], D.nm[:, :], D.logk, ALU.subtract, ALU.subtract).then_inc(na_ready, 1)
            dve.wait_ge(na_ready, 1 + CREDIT)
            dve.tensor_scalar(D.t[:, :], D.s[:, :], D.na[:, :], 0.0, ALU.subtract, ALU.min).then_inc(scored, 1)
            dve.wait_ge(exped, 1 + CREDIT)
            dve.tensor_scalar(u[:, :], sc[:, :], -1.0, 1.0, ALU.mult, ALU.add).then_inc(selected, 1)
            dve.wait_ge(selected, 1 + CREDIT)
            dve.tensor_tensor(sel[:, :], sc[:, :], u[:, :], ALU.add).then_inc(selected, 1)
            dve.wait_ge(turned, 1 + CREDIT)
            by_row = bank[1][:, 0:2 * R].rearrange("p (h r) -> p r h", h=2)
            dve.tensor_copy(SQ[:, :].rearrange("p (b h) -> p b h", h=2), by_row[:, 0:BATCH, :]).then_inc(turned_out, 1)
            dve.tensor_copy(VS[:, 0:BATCH, :], by_row[:, BATCH:R, :]).then_inc(turned_out, 1)
            with dve.Fori(0, BATCH // 2) as i:
                dve.wait_ge(ranked, 2 * i + CREDIT)
                for b in range(2):
                    dve.wait_ge(spread, 2 * i + b + 1 + CREDIT)
                    carry_waits(core, dve)
                    for h in range(2):
                        ins = dve.tensor_tensor_reduce(prod[b][:, h, :], bank[2 + b][:, h * P:(h + 1) * P], ident, 1.0, 0.0,
                                                       ALU.mult, ALU.add, own[b][:, h:h + 1])
                    ins.then_inc(owned, 1)
                for b in range(2):
                    dve.wait_ge(owned, 2 * i + b + 1 + CREDIT)
                    carry_waits(core, dve)
                    for h in range(2):
                        ins = dve.scalar_tensor_tensor(tie[b][:, h, :], bank[2 + b][:, 0:SEQ], own[b][:, h:h + 1],
                                                       before[:, h * SEQ:(h + 1) * SEQ], ALU.is_equal, ALU.mult)
                    ins.then_inc(tied, 1)
                for b in range(2):
                    dve.wait_ge(tied, 2 * i + b + 1 + CREDIT)
                    for h in range(2):
                        ins = dve.scalar_tensor_tensor(ahead[b][:, h, :], bank[2 + b][:, 0:SEQ], own[b][:, h:h + 1],
                                                       tie[b][:, h, :], ALU.is_gt, ALU.add)
                    ins.then_inc(counted, 1)
                for b in range(2):
                    q = 2 * i + b
                    dve.wait_ge(counted, q + 1 + CREDIT)
                    dve.tensor_reduce(rank[:, bass.ds(2 * q, 2)], ahead[b][:, :, :], AX.X, ALU.add).then_inc(ranked, 1)
            dve.wait_ge(ranked, BATCH + CREDIT)
            dve.tensor_scalar(chosen[:, :], rank[:, :], float(NQ), None, ALU.is_lt).then_inc(picked, 1)
            dve.wait_ge(picked, 1 + CREDIT)
            dve.wait_ge(turned_out, 1 + CREDIT)
            dve.tensor_tensor(SQ[:, :], SQ[:, :], chosen[:, :], ALU.mult).then_inc(scaled, 1)


class ScaledEpilogue(Epilogue):

    def __init__(self, wo, factors):
        self.wo, self.factors = wo, factors

    def alloc(self, sb, B):
        B["yb"] = sb("yb", [P, DM])

    def dve(self, dve, core, B, S, i, e, xt, y):
        t = 4 * i + e
        dve.tensor_scalar(B["yb"][:, :], y, self.factors[:, bass.ds(t, 1)], None, ALU.mult).then_inc(S["epilogue"], 1)
        dve.wait_ge(S["epilogue"], t + 1 + CREDIT)
        dve.tensor_tensor(xt, B["yb"][:, :], xt, ALU.add).then_inc(S["residual"], 1)


def l2_ffn(core, ctx, next_weights=()):
    with ExitStack() as mem:
        VS = mem.enter_context(core.nc.sbuf_tensor("VS", [P, BATCH + 1, 2], F32))
        SQ = mem.enter_context(core.nc.sbuf_tensor("SQ", [P, TILES], F32))
        D = Descent(core, mem)
        routing_start(core, ctx, D)
        normalize_stage(core, ctx, "u", unit=True)
        light = Heads(8, 64, 64, [(0, P), (P, P)])
        attention_stage(core, ctx, "5l", light, PlainSteps(5, ("l2_wql", "l2_wkl", "l2_wvl"), 512, 512, 64, -1.0 / 8.0),
                        Epilogue(weight(core, 5, "l2_wol")), moments=False, weights_of=5, beside=D)
        routing_finish(core, ctx, D, VS, SQ)
        heavy = Heads(8, 64, 64, [(0, SEQ), (0, SEQ)])
        attention_stage(core, ctx, "5h", heavy,
                        PlainSteps(5, ("l2_wqh", "l2_wkh", "l2_wvh"), 512, 512, 64, -1.0 / 8.0, value_scale=VS),
                        ScaledEpilogue(weight(core, 5, "l2_woh"), SQ), weights_of=5, next_weights=next_weights)



def build(nc, dram):
    with ExitStack() as ctx:
        core = Core(nc, ctx, dram)
        normalize_stage(core, ctx, 0, first=True, next_weights=(0, 1))
        l0_attention(core, ctx)
        normalize_stage(core, ctx, 1, next_weights=(2,))
        l0_ffn(core, ctx)
        normalize_stage(core, ctx, 2, next_weights=(3,))
        l1_attention(core, ctx)
        normalize_stage(core, ctx, 3, next_weights=(4,))
        l1_ffn(core, ctx)
        normalize_stage(core, ctx, 4, next_weights=(5,))
        l2_attention(core, ctx)
        normalize_stage(core, ctx, 5, next_weights=(6,))
        l2_ffn(core, ctx)
        normalize_stage(core, ctx, 6, next_weights=(7,))
        l3_attention(core, ctx)
        normalize_stage(core, ctx, 7)
        l3_ffn(core, ctx)
        normalize_stage(core, ctx, 8, last=True)


def spaced(a, H, dv, dvp):
    n = a.shape[1]
    out = np.zeros((H, dvp, n), np.float32)
    out[:, :dv] = a.reshape(H, dv, n)
    return out.reshape(-1, P, n).transpose(1, 0, 2).reshape(P, -1)


def half_swapped(a, H, d):
    return a.reshape(a.shape[0], H, 2, d // 2)[:, :, ::-1].reshape(a.shape)


def chunked(a):
    return a.reshape(-1, P, a.shape[1]).transpose(1, 0, 2).reshape(P, -1)


def lay_out(v):
    o = {}
    head_cat = lambda c, r: np.concatenate([c.reshape(-1, 16, 8), r.reshape(-1, 16, 32)], 2).reshape(-1, 640)
    zero = lambda rows, d: np.zeros((rows, 16 * d), np.float32)
    o["l0_wkv"], o["l0_wkvT"], o["l0_wqT"] = v["L0_attn_W_kv"], v["L0_attn_W_kv"].T, v["L0_attn_W_q"].T
    o["l0_gkv"] = v["L0_attn_g_kv"].reshape(32, 1)
    qr, kr = v["L0_attn_W_qrope"], v["L0_attn_W_krope"]
    o["l0_wqall"] = head_cat(v["L0_attn_W_qdec"], qr)
    o["l0_wqrot"] = head_cat(zero(64, 8), half_swapped(qr, 16, 32))
    o["l0_wkdec"] = head_cat(v["L0_attn_W_kdec"], zero(32, 32))
    o["l0_wkrope"] = head_cat(zero(128, 8), kr)
    o["l0_wkrot"] = head_cat(zero(128, 8), half_swapped(kr, 16, 32))
    o["l0_wvdec"] = v["L0_attn_W_vdec"]
    o["l0_wo"] = spaced(v["L0_attn_W_o"], 16, 8, 32)

    o["l0_rw"], o["l0_rb"] = v["L0_ffn_router_w"], v["L0_ffn_router_b"].reshape(1, 8)
    for k in "13":
        w = np.concatenate([v[f"L0_ffn_routed_w{k}"], v[f"L0_ffn_shared_w{k}"]], 0)
        o[f"l0_w{k}"] = w.transpose(1, 0, 2).reshape(P, 640)
    o["l0_w2"] = chunked(np.concatenate([v["L0_ffn_routed_w2"], v["L0_ffn_shared_w2"]], 0).reshape(640, P))

    for k in "qk":
        o[f"l1_w{k}"] = v[f"L1_attn_W{k}"]
        o[f"l1_w{k}rot"] = half_swapped(v[f"L1_attn_W{k}"], 16, 8)
    o["l1_wv"], o["l1_rel"] = v["L1_attn_Wv"], v["L1_attn_rel_emb"]
    o["l1_wo"] = spaced(v["L1_attn_Wo"], 16, 8, 32)

    o["l1_gw"], o["l1_gb"] = v["L1_ffn_gate_w"].T, v["L1_ffn_gate_b"].reshape(1, 8)
    o["l1_w1"] = v["L1_ffn_w1"].transpose(2, 0, 1).reshape(P, 4096)
    o["l1_b1"] = v["L1_ffn_b1"].reshape(8, 4, P).transpose(2, 1, 0).reshape(P, 32)
    o["l1_w2"] = v["L1_ffn_w2"].transpose(2, 0, 1).reshape(4, P, 8 * P).transpose(1, 0, 2).reshape(P, 4096)
    o["l1_b2"] = v["L1_ffn_b2"].reshape(1, 8 * P)
    o["l1_lower"], o["l1_ones"] = np.triu(np.ones((P, P), np.float32), 1), np.ones((P, P), np.float32)
    o["l1_earlier"] = np.tril(np.ones((8, 8), np.float32), -1).reshape(1, 64)
    o["l1_multiples"] = np.arange(0, TOK, P, dtype=np.float32).reshape(1, 32)
    o["l1_iota"] = np.arange(SORTED, dtype=np.float32).reshape(1, SORTED)

    for k in "qkv":
        o[f"l2_w{k}"] = v[f"L2_attn_W{k}"]
    o["l2_wo"] = spaced(v["L2_attn_Wo"], 16, 16, 32)

    for s, kind in (("l", "light"), ("h", "heavy")):
        o[f"l2_g{s}"] = v[f"L2_ffn_gamma_{kind}"].reshape(P, 1)
        o[f"l2_wq{s}"] = v[f"L2_ffn_wq_{kind}"]
        wkv = v[f"L2_ffn_wkv_{kind}"]
        if s == "l":
            k, w = wkv[:, 0:512], wkv[:, 512:1024]
        else:
            w = wkv.T.reshape(P, 8, 2, 64)
            k, w = w[:, :, 0].reshape(P, 512), w[:, :, 1].reshape(P, 512)
        o[f"l2_wk{s}"], o[f"l2_wv{s}"] = k, w
        o[f"l2_wo{s}"] = chunked(v[f"L2_ffn_wo_{kind}"])
    tok = np.zeros((P, 64), np.float32)
    tok[:, 15], tok[:, 31] = v["L2_ffn_q_routing_token"], v["L2_ffn_kv_routing_token"]
    o["l2_tok"] = tok

    w, bias = v["L3_attn_Wqkv_w"].T, v["L3_attn_Wqkv_b"]
    for j, k in enumerate("qkv"):
        o[f"l3_w{k}"] = w[:, j * 1024:(j + 1) * 1024]
        b = bias[j * 1024:(j + 1) * 1024]
        o[f"l3_b{k}"] = b.reshape(1, 1024) if k == "v" else b.reshape(8, P).T
    o["l3_wo"] = chunked(v["L3_attn_Wo_w"].T)
    o["l3_bo"], o["l3_ghost"] = v["L3_attn_Wo_b"].reshape(1, P), v["L3_attn_ghost"].reshape(1, 16)

    row = lambda *names: np.concatenate([v[s].reshape(-1) for s in names]).reshape(1, -1)
    o["l3_s1"] = np.concatenate([v["L3_ffn_sw1"].T, v["L3_ffn_sw2"].T], 1)
    o["l3_sb"] = row("L3_ffn_sb1", "L3_ffn_sb2")
    o["l3_s3"], o["l3_sb3"] = v["L3_ffn_sw3"].T, row("L3_ffn_sb3")
    o["l3_sln"] = row("L3_ffn_s_ln_g", "L3_ffn_s_ln_b")
    o["l3_gw"] = np.concatenate([v["L3_ffn_sg_w"], v["L3_ffn_eg_w"]], 0).T
    o["l3_gb"], o["l3_eb"] = row("L3_ffn_sg_b", "L3_ffn_eg_b"), row("L3_ffn_exp_bias")
    for k in "12":
        o[f"l3_e{k}"] = v[f"L3_ffn_ew{k}"].transpose(2, 0, 1).reshape(P, 512)
        o[f"l3_eb{k}"] = row(f"L3_ffn_eb{k}")
    o["l3_e3"] = chunked(v["L3_ffn_ew3"].transpose(0, 2, 1).reshape(512, P))
    o["l3_eb3"] = v["L3_ffn_eb3"]
    o["l3_eln"] = row("L3_ffn_sel_ln_g", "L3_ffn_sel_ln_b")
    for k in "bt":
        index = v[f"L3_ffn_index_{k}"]
        o[f"l3_i{k}col"], o[f"l3_i{k}row"] = index.reshape(2, P).T, index.reshape(1, 2 * P)
    o["l3_token"] = np.arange(TOK, dtype=np.float32).reshape(TILES, P).T
    o["l3_base"] = np.arange(0, TOK, BANK, dtype=np.float32).reshape(1, 8)
    o["l3_iota"] = np.arange(BANK, dtype=np.float32).reshape(1, BANK)
    return o


def kernel(**inputs):
    import concourse.bacc as bacc
    from concourse.bass_utils import run_bass_kernel_spmd

    nc = bacc.Bacc("TRN2", target_bir_lowering=False, num_devices=1)
    v = {k: np.asarray(a) for k, a in inputs.items()}
    arrays = lay_out(v)
    arrays["x"] = v["L0_attn_x"].reshape(TOK, DM)
    _, arrays["consts"], staged = shape_constants()
    arrays.update(staged)
    given, dram = {}, {}
    for name, a in arrays.items():
        a = np.ascontiguousarray(a)
        given["in_" + name] = a
        dram[name] = nc.dram_tensor("in_" + name, a.shape, mybir.dt.from_np(a.dtype), kind="ExternalInput").ap()
    dram["out"] = nc.dram_tensor("out_x", (TOK, DM), F32, kind="ExternalOutput").ap()
    build(nc, dram)
    r = run_bass_kernel_spmd(nc, [given], core_ids=[0])
    return r.results[0]["out_x"].reshape(BATCH, SEQ, DM)
```
